# Optimizing a Trainium2 kernel written in Bass

```python
import numpy as np
import jax
import jax.numpy as jnp

def _softmax(x, axis=-1):
    return jax.nn.softmax(x, axis=axis)

def _gelu(x):
    return jax.nn.gelu(x, approximate=True)

def _silu(x):
    return jax.nn.silu(x)

def _sigmoid(x):
    return jax.nn.sigmoid(x)

def _layernorm(x, axis=-1, eps=1e-05):
    m = jnp.mean(x, axis=axis, keepdims=True)
    v = jnp.var(x, axis=axis, keepdims=True)
    return (x - m) / jnp.sqrt(v + eps)

def _scatter_add(tgt, idx, src, axis=0):
    return tgt.at[idx].add(src)

def _segment_sum(src, seg, n):
    return jax.ops.segment_sum(src, seg, n)
kernel_name = 'mk_macaron_d1_jaxref_r8_bceeae'

def setup_inputs(seed: int=0):
    np.random.seed(seed)
    _w = jnp.asarray

    def _L0_attn_setup():
        import jax, jax.numpy as jnp
        import numpy as np
        B, S, E, H = (2, 256, 128, 16)
        D = E // H
        key = jax.random.key(seed)
        ks = jax.random.split(key, 5)
        return {'hidden_states': jax.random.normal(ks[0], (B, S, E), dtype=jnp.float32), 'c_attn_w': jax.random.normal(ks[1], (E, 3 * E), dtype=jnp.float32) * 0.02, 'c_attn_b': jax.random.normal(ks[2], (3 * E,), dtype=jnp.float32) * 0.02, 'c_proj_w': jax.random.normal(ks[3], (E, E), dtype=jnp.float32) * 0.02, 'c_proj_b': jax.random.normal(ks[4], (E,), dtype=jnp.float32) * 0.02}
    _L0_attn_in = _L0_attn_setup()

    def _L0_ffn_setup():
        import jax, jax.numpy as jnp
        import numpy as np
        H, I, E_ROUTED, TOP_K = (128, 352, 7, 2)
        B, S = (4, 256)

        def _expert(h, g, u, d):
            return jnp.einsum('...i,hi->...h', jax.nn.silu(h @ g.T) * (h @ u.T), d)
        key = jax.random.key(seed)
        ks = jax.random.split(key, 10)
        sc = 0.02
        return {'x': jax.random.normal(ks[0], (B, S, H), dtype=jnp.float32), 'sg': jax.random.normal(ks[1], (I, H), dtype=jnp.float32) * sc, 'su': jax.random.normal(ks[2], (I, H), dtype=jnp.float32) * sc, 'sd': jax.random.normal(ks[3], (H, I), dtype=jnp.float32) * sc, 'rg': jax.random.normal(ks[4], (E_ROUTED, I, H), dtype=jnp.float32) * sc, 'ru': jax.random.normal(ks[5], (E_ROUTED, I, H), dtype=jnp.float32) * sc, 'rd': jax.random.normal(ks[6], (E_ROUTED, H, I), dtype=jnp.float32) * sc, 'wr': jax.random.normal(ks[7], (E_ROUTED, H), dtype=jnp.float32) * sc, 'rb': jnp.zeros((E_ROUTED,), dtype=jnp.float32)}
    _L0_ffn_in = _L0_ffn_setup()
    _d = {'L0_attn_hidden_states': _L0_attn_in['hidden_states'], 'L0_attn_c_attn_w': _L0_attn_in['c_attn_w'], 'L0_attn_c_attn_b': _L0_attn_in['c_attn_b'], 'L0_attn_c_proj_w': _L0_attn_in['c_proj_w'], 'L0_attn_c_proj_b': _L0_attn_in['c_proj_b'], 'L0_ffn_sg': _L0_ffn_in['sg'], 'L0_ffn_su': _L0_ffn_in['su'], 'L0_ffn_sd': _L0_ffn_in['sd'], 'L0_ffn_rg': _L0_ffn_in['rg'], 'L0_ffn_ru': _L0_ffn_in['ru'], 'L0_ffn_rd': _L0_ffn_in['rd'], 'L0_ffn_wr': _L0_ffn_in['wr'], 'L0_ffn_rb': _L0_ffn_in['rb']}
    _x0 = _d['L0_attn_hidden_states']
    _d['L0_attn_hidden_states'] = jax.random.normal(jax.random.fold_in(jax.random.key(seed), 1), (2, 1024, 128), dtype=_x0.dtype)
    del _x0
    return _d

def reference(L0_attn_hidden_states, L0_attn_c_attn_w, L0_attn_c_attn_b, L0_attn_c_proj_w, L0_attn_c_proj_b, L0_ffn_sg, L0_ffn_su, L0_ffn_sd, L0_ffn_rg, L0_ffn_ru, L0_ffn_rd, L0_ffn_wr, L0_ffn_rb):

    def _L0_attn_ref(hidden_states, c_attn_w, c_attn_b, c_proj_w, c_proj_b):
        import jax, jax.numpy as jnp
        import numpy as np
        B, S, E, H = (2, 256, 128, 16)
        D = E // H
        x = hidden_states
        b, s, _ = x.shape
        w_q, w_k, w_v = jnp.split(c_attn_w, 3, axis=1)
        q_b, k_b, v_b = jnp.split(c_attn_b, 3, axis=0)
        v = x @ w_v + v_b
        v = v.reshape(b, s, H, D).transpose(0, 2, 1, 3)
        q = (x @ w_q + q_b) @ w_k.T + k_b
        qh = q.reshape(b, s, H, D).transpose(0, 2, 1, 3)
        kh = x.reshape(b, s, H, D).transpose(0, 2, 1, 3)
        scale = 1.0 / jnp.float32(D) ** 0.5
        scores = jnp.einsum('bhqd,bhkd->bhqk', qh.astype(jnp.float32), kh.astype(jnp.float32)) * scale
        causal = jnp.tril(jnp.ones((s, s), dtype=bool))
        mask_value = jnp.finfo(jnp.float32).min
        scores = jnp.where(causal[None, None], scores, mask_value)
        probs = jax.nn.softmax(scores, axis=-1).astype(v.dtype)
        out = jnp.einsum('bhqk,bhkd->bhqd', probs, v)
        out = out.transpose(0, 2, 1, 3).reshape(b, s, E)
        out = out @ c_proj_w + c_proj_b
        return out

    def _L0_ffn_ref(x, sg, su, sd, rg, ru, rd, wr, rb):
        import jax, jax.numpy as jnp
        import numpy as np
        H, I, E_ROUTED, TOP_K = (128, 352, 7, 2)
        B, S = (4, 256)

        def _expert(h, g, u, d):
            return jnp.einsum('...i,hi->...h', jax.nn.silu(h @ g.T) * (h @ u.T), d)
        shared_out = _expert(x, sg, su, sd)
        logits = x @ wr.T + rb
        probs = jax.nn.softmax(logits, axis=-1)
        scores, idx = jax.lax.top_k(probs, TOP_K)
        scores = scores / scores.sum(axis=-1, keepdims=True)
        w = jnp.sum(scores[..., None] * jax.nn.one_hot(idx, E_ROUTED, dtype=x.dtype), axis=-2)
        out = shared_out
        for e in range(E_ROUTED):
            out = out + w[..., e:e + 1] * _expert(x, rg[e], ru[e], rd[e])
        return out
    x = L0_attn_hidden_states
    x = x + 0.5 * _L0_ffn_ref(_layernorm(x, axis=-1), L0_ffn_sg, L0_ffn_su, L0_ffn_sd, L0_ffn_rg, L0_ffn_ru, L0_ffn_rd, L0_ffn_wr, L0_ffn_rb)
    x = x + _L0_attn_ref(_layernorm(x, axis=-1), L0_attn_c_attn_w, L0_attn_c_attn_b, L0_attn_c_proj_w, L0_attn_c_proj_b)
    x = x + 0.5 * _L0_ffn_ref(_layernorm(x, axis=-1), L0_ffn_sg, L0_ffn_su, L0_ffn_sd, L0_ffn_rg, L0_ffn_ru, L0_ffn_rd, L0_ffn_wr, L0_ffn_rb)
    return x

_drawn_inputs = setup_inputs


def setup_inputs(seed=0):
    import zlib

    import numpy as np

    out = dict(_drawn_inputs(seed))
    spreads = {'L0_ffn_rb': (0.0, 0.8)}
    factors = {'L0_attn_c_attn_w': 8.0,
     'L0_attn_c_attn_b': 8.0,
     'L0_attn_c_proj_w': 8.0,
     'L0_attn_c_proj_b': 2.77,
     'L0_ffn_sg': 5.527,
     'L0_ffn_su': 5.253,
     'L0_ffn_sd': 5.278,
     'L0_ffn_rg': 8.0,
     'L0_ffn_ru': 8.0,
     'L0_ffn_rd': 8.0,
     'L0_ffn_wr': 8.0}
    for name, (base, spread) in spreads.items():
        noise = np.random.default_rng([zlib.crc32(name.encode()), seed]).standard_normal(out[name].shape)
        drawn = base * np.exp(spread * noise) if base else spread * noise
        out[name] = jnp.asarray(drawn.astype(out[name].dtype))
    for name, factor in factors.items():
        out[name] = (out[name] * factor).astype(out[name].dtype)
    return out
```

```python
from contextlib import ExitStack

import numpy as np

import concourse.bass as bass
from concourse import mybir

F32 = mybir.dt.float32
F32R = mybir.dt.float32r
BF16 = mybir.dt.bfloat16
ALU = mybir.AluOpType
ACT = mybir.ActivationFunctionType
AX = mybir.AxisListType

P = 128
BATCH, SEQ, EMB = 2, 1024, 128
HEADS, HDIM = 16, 8
TOKENS = BATCH * SEQ
TT = TOKENS // P
CHUNK = 512
NCH = TOKENS // CHUNK
TPC = CHUNK // P
HID, ROUTED = 352, 7
EXPERTS = ROUTED + 1
HROWS = HID * EXPERTS
NT = HROWS // P
LN_EPS = 1e-5
SCALE = 1.0 / float(np.sqrt(HDIM))
MASKED = -1e30
GROUPS = BATCH * HEADS // 4
GPB = GROUPS // BATCH
KT = SEQ // P
NGATE = 8


def at(start, n):
    return slice(start, start + n) if isinstance(start, int) else bass.ds(start, n)


def hidden_pieces():
    tiles = []
    for n in range(NT):
        r, runs = n * P, []
        while r < (n + 1) * P:
            e = r // HID
            end = min((n + 1) * P, (e + 1) * HID)
            runs.append((r - n * P, end - n * P, e))
            r = end
        tiles.append(runs)
    return tiles


def weight_slots():
    slots, loads, slot_of, end = {}, [], {}, []
    for n, runs in enumerate(hidden_pieces()):
        if all(e == 0 for _, _, e in runs):
            continue
        key = ("expert", runs[0][2]) if len(runs) == 1 else ("tile", n)
        if key not in slots:
            slots[key] = len(loads)
            loads.append([(a, b, e) for a, b, e in runs if e])
            end.append(n)
        slot_of[n] = slots[key]
        end[slots[key]] = n
    return slot_of, loads, end


SLOT_OF, SLOT_LOADS, SLOT_END = weight_slots()
FIRST_ROUTED = min(SLOT_OF)
NROUTED = NT - FIRST_ROUTED


PLACE = [0, 1, 2, 3] * 4 + [0, 1, 2] * 2
BACK = [3, 3, 3, 10] + [4] * 15 + [3] * 3
assert len(PLACE) == len(BACK) == NT


MAX_BANKS = [
    [(0, 0, 1, 0, True), (2, 0, 3, 1, True)],
    [(1, 0, 2, 0, True), (5, 4, 2, 2, True)],
    [(5, 0, 4, 0, False)],
    [(4, 0, 4, 0, False)],
    [(4, 4, 1, 0, True), (6, 4, 3, 1, True)],
    [(6, 0, 4, 0, False)],
    [(3, 0, 4, 0, True)],
    [(7, 0, 4, 0, False)],
    [(7, 4, 4, 0, True)],
]
NBANK = len(MAX_BANKS)
NMAX = 4 * NBANK


def max_slots():
    runs = {}
    for b, pieces in enumerate(MAX_BANKS):
        for i, _, n, at0, _ in pieces:
            lo, hi = runs.get(i, (99, 0))
            runs[i] = (min(lo, 4 * b + at0), max(hi, 4 * b + at0 + n))
    assert all(hi - lo == i + 1 for i, (lo, hi) in runs.items())
    return runs


UNITS = [(kt, (j,)) for kt in range(4) for j in range(4)] + \
        [(kt, (j, j + 1)) for kt in range(4, KT) for j in (0, 2)]
NU = len(UNITS)
FIRST_UNIT = [min(n for n, (kt, _) in enumerate(UNITS) if kt == k) for k in range(KT)] + [NU]

LEAD = NMAX // 2
MT_LATER = 3
def ring_of_body(nxt, nxt2):
    a = [("max", 1, n) for n in range(LEAD, NMAX)] if nxt else []
    b = [("max", 2, n) for n in range(LEAD)] if nxt2 else []
    ring = a[:4] + [("out", -1, 1)] + a[4:] + b[:MT_LATER]
    if nxt:
        ring.append(("mrow", 1, 0))
    ring += b[MT_LATER:]
    ring.insert(min(len(ring), 33), ("out", 0, 0))
    return ring


RING_PROLOGUE = [("max", 0, n) for n in range(NMAX)] + [("max", 1, n) for n in range(MT_LATER)] + \
                [("mrow", 0, 0)] + [("max", 1, n) for n in range(MT_LATER, LEAD)]
LOOPED = GROUPS - 2
LOOP, LAST_BUT_ONE, LAST = 0, 1, 2
RINGS = [ring_of_body(True, True), ring_of_body(True, False), ring_of_body(False, False)]
SHARES = [[7, 7, 6, 4, 3, 2, 2, 8], [4, 4, 3, 3, 3, 3, 0, 1], [1, 0, 0, 0, 0, 0, 1, 0]]
RINGN = len(RINGS[LOOP])
RING0 = [len(RING_PROLOGUE), len(RING_PROLOGUE), len(RING_PROLOGUE) + len(RINGS[LAST_BUT_ONE]) - RINGN]
RING_END = RING0[LAST] + RINGN * (GROUPS - 1) + len(RINGS[LAST])


def count(p, u, each, more):
    return p * (2 * each) + (u * each + more)


def loads(p, u, d):
    return p + ((u + d) // 2 + 1)


G_BANK, U_BANK, Y_BANK, N_BANK, R_BANK = (0, 1), (2, 3), 4, 5, 6
RING, SLOTS, O_BANK = (0, 1), (2, 4), (6, 7)

TP_GROUPS = [(w, n, min(4, NT - n)) for n in range(0, NT, 4) for w in ("g", "u")] + \
            [("d", n, min(4, NT - n)) for n in range(0, NT, 4)]
TP_BANKS = (0, 1, 2, 3)
N_CONST = 9
N_SMALL = 8
N_CONST_DMA = 3


class Chip:
    pass


def place_memory(K, ctx):
    def sem(name):
        return ctx.enter_context(K.nc.semaphore(name))

    def sb(name, shape, dt=F32, scope=ctx):
        return scope.enter_context(K.nc.sbuf_tensor(name, shape, dt))

    K.wt_dram = [K.nc.dram_tensor(f"route_rows{f}", (TT, NGATE, P), F32, kind="Internal").ap() for f in range(2)]
    K.q_dram = K.nc.dram_tensor("q_stack", (GROUPS * 4, 32, SEQ), F32, kind="Internal").ap()
    K.k_dram = K.nc.dram_tensor("k_stack", (GROUPS * 4, 32, SEQ), F32, kind="Internal").ap()

    K.out_tiles = K.result.rearrange("b (t p) e -> p (b t) e", p=P)

    K.x = sb("x", [P, TT, EMB])
    K.wide = {}
    for w in ("g", "u", "d"):
        for part in ("h", "l"):
            K.wide[w + part] = sb(f"w{w}_{part}", [P, HROWS], F32R)
    K.small = {}
    for w in ("q", "k", "v", "p"):
        for part in ("h", "l"):
            K.small[w + part] = sb(f"w{w}_{part}", [P, EMB], F32R)
    K.rw_h = sb("rw_h", [P, NGATE], F32R)
    K.rw_l = sb("rw_l", [P, NGATE], F32R)
    K.ident = sb("ident", [P, P])
    K.ident_b = sb("ident_b", [P, P], BF16)
    K.mask_b = sb("mask_b", [P, P], BF16)
    K.b_q = sb("b_q", [P, 1])
    K.b_k = sb("b_k", [P, 1])
    K.b_v = sb("b_v", [P, EMB])
    K.b_p = sb("b_p", [P, EMB])
    K.rb_row = sb("rb_row", [P, NGATE])
    K.rank = sb("rank", [P, NGATE])
    K.rank_i = sb("rank_i", [P, NGATE], mybir.dt.int32)
    K.half_neg = sb("half_neg", [P, TPC])
    K.stats = sb("stats", [P, TPC, 6])
    K.mv = sb("mv", [P, TPC, 2])
    K.var_e = sb("var_e", [P, TPC])
    K.rstd = sb("rstd", [P, TPC])
    K.z = sb("z", [P, TPC, EMB])

    with ExitStack() as s:
        K.zt_h = sb("zt_h", [P, TOKENS], F32R, scope=s)
        K.zt_l = sb("zt_l", [P, TOKENS], F32R, scope=s)
        with ExitStack() as s2:
            K.w_slots = sb("w_slots", [P, len(SLOT_LOADS), CHUNK], scope=s2)
            K.silu = sb("silu", [P, 2, CHUNK], scope=s2)
            K.act = sb("act", [P, 4, CHUNK], scope=s2)
            K.act_h = sb("act_h", [P, 4, CHUNK], F32R, scope=s2)
            K.act_l = sb("act_l", [P, 4, CHUNK], F32R, scope=s2)
            K.yt = sb("yt", [P, CHUNK], scope=s2)
            K.r_log = sb("r_log", [P, TT, NGATE], scope=s2)
            K.r_exp = sb("r_exp", [P, TT, NGATE], scope=s2)
            K.r_p = sb("r_p", [P, TT, NGATE], scope=s2)
            K.r_c = sb("r_c", [P, TT, NGATE], scope=s2)
            K.r_s1 = sb("r_s1", [P, TT, NGATE], scope=s2)
            K.r_s2 = sb("r_s2", [P, TT, NGATE], scope=s2)
            K.r_w = sb("r_w", [P, TT, NGATE], scope=s2)
            K.r_wt = sb("r_wt", [P, P], scope=s2)
            K.r_m = sb("r_m", [P, TT], scope=s2)
            K.r_r = sb("r_r", [P, TT], scope=s2)
            K.nat = {w: sb(f"nat_{w}", [P, HROWS], scope=s2) for w in ("g", "u", "d")}
            K.nat_attn = sb("nat_attn", [P, 3 * EMB], scope=s2)
            K.nat_proj = sb("nat_proj", [P, EMB], scope=s2)
            K.nat_route = sb("nat_route", [P, P], scope=s2)
            K.rows0 = sb("rows0", [32, CHUNK], scope=s2)
            K.rows1 = sb("rows1", [32, CHUNK], scope=s2)
        with ExitStack() as s2:
            K.q1_f = sb("q1_f", [P, 2, CHUNK], scope=s2)
            K.q1_h = sb("q1_h", [P, 2, CHUNK], F32R, scope=s2)
            K.q1_l = sb("q1_l", [P, 2, CHUNK], F32R, scope=s2)
            K.q_f = sb("q_f", [P, 2, CHUNK], scope=s2)
            K.q_h = sb("q_h", [P, 2, CHUNK], F32R, scope=s2)
            K.q_l = sb("q_l", [P, 2, CHUNK], F32R, scope=s2)
        with ExitStack() as s2:
            K.ao_f = sb("ao_f", [P, 2, CHUNK], scope=s2)
            K.ao_h = sb("ao_h", [P, 2, CHUNK], F32R, scope=s2)
            K.ao_l = sb("ao_l", [P, 2, CHUNK], F32R, scope=s2)
    with ExitStack() as s:
        K.probs = sb("probs", [P, 2, 4, SEQ], scope=s)
        K.vg = [sb(f"vg{u}", [P, KT, 4, 32], scope=s) for u in range(2)]
        K.qm = [sb(f"qm{u}", [P, SEQ], F32R, scope=s) for u in range(2)]
        K.ks = [sb(f"ks{u}", [P, SEQ], F32R, scope=s) for u in range(2)]
        K.qs = [sb(f"qs{u}", [P, SEQ], F32R, scope=s) for u in range(2)]
        K.v_all = sb("v_all", [P, GROUPS, KT, 32], scope=s)
        K.o_all = sb("o_all", [P, GROUPS + 1, KT, 32], scope=s)
        K.ot = sb("ot", [P, 2, CHUNK], scope=s)
        K.rsum = sb("rsum", [P, 16, 1], scope=s)
        K.mxp = sb("mxp", [P, 4, 4 * NBANK], scope=s)
        K.nmax = sb("nmax", [P, 4, KT], scope=s)
        K.mm_hl = sb("mm_hl", [P, 8, 2, KT], F32R, scope=s)
        K.m_rows = sb("m_rows", [P, P], F32R, scope=s)
        K.km = [sb(f"km{u}", [P, 4, SEQ], F32R, scope=s) for u in range(2)]

    K.shared_rows = K.w_slots[0:SLOT_LOADS[SLOT_OF[FIRST_ROUTED]][0][0], SLOT_OF[FIRST_ROUTED], :]

    K.psum = ctx.enter_context(K.nc.psum_tensor("psum", [P, 8, CHUNK], F32))


    K.ld = {n: sem(f"ld_{n}") for n in ("x", "nat", "small", "const", "out")}
    K.passed = sem("passed")
    K.consts = sem("consts")
    K.tp_pe, K.tp_hi, K.tp_lo = sem("tp_pe"), sem("tp_hi"), sem("tp_lo")
    K.sw_hi, K.sw_lo = sem("sw_hi"), sem("sw_lo")
    K.blank, K.ones, K.cleared = sem("blank"), sem("ones"), sem("cleared")
    K.NS = [{n: sem(f"n{k}_{n}") for n in
                  ("bn", "mv", "ve", "rstd", "z", "tr", "hi", "lo")} for k in range(3)]
    K.RS = [{n: sem(f"r{k}_{n}") for n in
                   ("log", "neg", "exp", "step", "w", "tr", "wt", "st")} for k in range(2)]
    K.FF = [{n: sem(f"f{k}_{n}") for n in
                 ("up", "silu", "act", "route", "hi", "lo", "down", "yev", "ytr", "out")} for k in range(2)]
    K.slot_sems = [sem(f"slot{n}") for n in range(len(SLOT_LOADS))]
    K.A = {n: sem(f"a_{n}") for n in
            ("q1", "q1f", "q1h", "q1l", "q", "qf", "qh", "ql", "v", "vev", "init",
             "ring", "taken", "mm", "sp", "ex", "mk", "pv", "oev", "vg", "ready", "nm", "rs", "vi", "og", "otr", "oh", "ol", "op", "xup")}
    K.q_st = [sem(f"q_st{c}") for c in range(NCH)]
    K.k_st = [sem(f"k_st{c}") for c in range(NCH)]
    K.ld_m = [sem(f"ld_m{u}") for u in range(2)]
    K.ld_s = [sem(f"ld_s{u}") for u in range(2)]
    K.ld_r = [sem(f"ld_r{u}") for u in range(2)]


def bank(K, n):
    return K.psum[:, n, :]


def alone(K, e):
    e.sem_inc(K.passed, 1)


def norm_stats_dve(K, k, c):
    for t in range(TPC):
        K.nc.vector.bn_stats(K.stats[:, t, :], K.x[:, at(c * TPC + t, 1), :]).then_inc(K.NS[k]["bn"], 1)
    K.nc.vector.wait_ge(K.NS[k]["bn"], TPC * (c + 1))
    alone(K, K.nc.vector)
    for t in range(TPC):
        ins = K.nc.vector.bn_aggr(K.mv[:, t, :], K.stats[:, t, :])
    ins.then_inc(K.NS[k]["mv"], 1)


def norm_rstd_pool(K, k, c):
    K.nc.gpsimd.wait_ge(K.NS[k]["mv"], c + 1)
    alone(K, K.nc.gpsimd)
    K.nc.gpsimd.tensor_scalar(K.var_e[:, :], K.mv[:, :, 1], LN_EPS, None, ALU.add).then_inc(K.NS[k]["ve"], 1)
    K.nc.gpsimd.wait_ge(K.NS[k]["ve"], c + 1)
    K.nc.gpsimd.tensor_tensor(K.rstd[:, :], K.var_e[:, :], K.half_neg[:, :], ALU.pow).then_inc(K.NS[k]["rstd"], 1)


def norm_z_dve(K, k, c):
    K.nc.vector.wait_ge(K.NS[k]["rstd"], c + 1)
    K.nc.vector.wait_ge(K.NS[k]["mv"], c + 1)
    if k != 1 and c > 0:
        K.nc.vector.wait_ge(K.NS[k]["tr"], c)
    for t in range(TPC):
        ins = K.nc.vector.tensor_scalar(K.z[:, t, :], K.x[:, at(c * TPC + t, 1), :], K.mv[:, t, 0:1],
                                      K.rstd[:, t:t + 1], ALU.subtract, ALU.mult)
    ins.then_inc(K.NS[k]["z"], 1)


def norm_tr_pe(K, k, c):
    K.nc.tensor.wait_ge(K.NS[k]["z"], c + 1)
    if k != 1 and c > 0:
        K.nc.tensor.wait_ge(K.NS[k]["lo"], c)
    for t in range(TPC):
        ins = K.nc.tensor.transpose(bank(K, N_BANK)[:, t * P:(t + 1) * P], K.z[:, t, :], K.ident[:, :])
    ins.then_inc(K.NS[k]["tr"], 1)


def norm_hi_act(K, k, c):
    K.nc.scalar.wait_ge(K.NS[k]["tr"], c + 1)
    K.nc.scalar.copy(K.zt_h[:, at(c * CHUNK, CHUNK)], bank(K, N_BANK)).then_inc(K.NS[k]["hi"], 1)


def norm_lo_dve(K, k, c):
    K.nc.vector.wait_ge(K.NS[k]["hi"], c + 1)
    K.nc.vector.tensor_tensor(K.zt_l[:, at(c * CHUNK, CHUNK)], bank(K, N_BANK),
                            K.zt_h[:, at(c * CHUNK, CHUNK)].bitcast(F32), ALU.subtract).then_inc(K.NS[k]["lo"], 1)


def router_pe(K, f, k):
    e = K.nc.tensor
    e.wait_ge(K.sw_lo, 5)
    for t in range(TT):
        if t % TPC == 0:
            e.wait_ge(K.NS[k]["lo"], t // TPC + 1)
        dst = bank(K, R_BANK)[:, t * NGATE:(t + 1) * NGATE]
        zh, zl = K.zt_h[:, t * P:(t + 1) * P], K.zt_l[:, t * P:(t + 1) * P]
        e.matmul(dst, zh, K.rw_h[:, :], start=True, stop=False)
        e.matmul(dst, zh, K.rw_l[:, :], start=False, stop=False)
        ins = e.matmul(dst, zl, K.rw_h[:, :], start=False, stop=True)
    ins.then_inc(K.RS[f]["log"], 1)
    e.wait_ge(K.RS[f]["w"], 1)
    e.transpose(bank(K, R_BANK)[:, CHUNK - P:], K.r_w[:, :, :].rearrange("p t e -> p (t e)"),
                K.ident[:, :]).then_inc(K.RS[f]["tr"], 1)


def router_dve(K, f):
    e, s = K.nc.vector, K.RS[f]

    def wide_of(v):
        return v.unsqueeze(2).to_broadcast([P, TT, NGATE])

    e.wait_ge(s["log"], 1)
    logits = bank(K, R_BANK)[:, 0:TT * NGATE].rearrange("p (t e) -> p t e", e=NGATE)
    e.tensor_tensor(K.r_log[:, :, :], logits, K.rb_row[:, :].unsqueeze(1).to_broadcast([P, TT, NGATE]), ALU.add).then_inc(s["step"], 1)
    e.wait_ge(s["step"], 1)
    e.tensor_reduce(K.r_m[:, :], K.r_log[:, :, :], AX.X, ALU.max).then_inc(s["step"], 1)
    e.wait_ge(s["step"], 2)
    e.tensor_tensor(K.r_c[:, :, :], K.r_log[:, :, :], wide_of(K.r_m[:, :]), ALU.subtract).then_inc(s["neg"], 1)
    e.wait_ge(s["exp"], 1)
    e.tensor_reduce(K.r_m[:, :], K.r_exp[:, :, :], AX.X, ALU.add).then_inc(s["step"], 1)
    e.wait_ge(s["step"], 3)
    e.reciprocal(K.r_r[:, :], K.r_m[:, :]).then_inc(s["step"], 1)
    e.wait_ge(s["step"], 4)
    e.tensor_tensor(K.r_p[:, :, :], K.r_exp[:, :, :], wide_of(K.r_r[:, :]), ALU.mult).then_inc(s["step"], 1)
    e.wait_ge(s["step"], 5)
    e.tensor_scalar(K.r_w[:, :, :], K.r_p[:, :, :], 1.0, None, ALU.mult).then_inc(s["step"], 1)
    e.wait_ge(s["step"], 6)
    for sel, steps in ((K.r_s1, 6), (K.r_s2, 12)):
        e.tensor_reduce(K.r_m[:, :], K.r_w[:, :, :], AX.X, ALU.max).then_inc(s["step"], 1)
        e.wait_ge(s["step"], steps + 1)
        e.tensor_tensor(K.r_c[:, :, :], K.r_w[:, :, :], wide_of(K.r_m[:, :]), ALU.is_equal).then_inc(s["step"], 1)
        e.wait_ge(s["step"], steps + 2)
        e.tensor_tensor(K.r_c[:, :, :], K.r_c[:, :, :], K.rank[:, :].unsqueeze(1).to_broadcast([P, TT, NGATE]),
                        ALU.mult).then_inc(s["step"], 1)
        e.wait_ge(s["step"], steps + 3)
        e.tensor_reduce(K.r_m[:, :], K.r_c[:, :, :], AX.X, ALU.max).then_inc(s["step"], 1)
        e.wait_ge(s["step"], steps + 4)
        e.tensor_tensor(sel[:, :, :], K.r_c[:, :, :], wide_of(K.r_m[:, :]), ALU.is_equal).then_inc(s["step"], 1)
        e.wait_ge(s["step"], steps + 5)
        if sel is K.r_s1:
            e.scalar_tensor_tensor(K.r_w[:, :, :], K.r_s1[:, :, :], -2.0, K.r_p[:, :, :], ALU.mult, ALU.add).then_inc(s["step"], 1)
            e.wait_ge(s["step"], steps + 6)
    e.tensor_tensor(K.r_c[:, :, :], K.r_s1[:, :, :], K.r_s2[:, :, :], ALU.add).then_inc(s["step"], 1)
    e.wait_ge(s["step"], 18)
    e.tensor_tensor(K.r_c[:, :, :], K.r_c[:, :, :], K.r_p[:, :, :], ALU.mult).then_inc(s["step"], 1)
    e.wait_ge(s["step"], 19)
    e.tensor_reduce(K.r_m[:, :], K.r_c[:, :, :], AX.X, ALU.add).then_inc(s["step"], 1)
    e.wait_ge(s["step"], 20)
    e.reciprocal(K.r_r[:, :], K.r_m[:, :]).then_inc(s["step"], 1)
    e.wait_ge(s["step"], 21)
    e.tensor_tensor(K.r_w[:, :, :], K.r_c[:, :, :], wide_of(K.r_r[:, :]), ALU.mult).then_inc(s["w"], 1)
    e.wait_ge(s["tr"], 1)
    e.tensor_copy(K.r_wt[:, :], bank(K, R_BANK)[:, CHUNK - P:]).then_inc(s["wt"], 1)


def router_act(K, f):
    K.nc.scalar.wait_ge(K.RS[f]["neg"], 1)
    K.nc.scalar.activation(K.r_exp[:, :, :], K.r_c[:, :, :], ACT.Exp).then_inc(K.RS[f]["exp"], 1)


def router_sp(K, f):
    K.nc.sync.wait_ge(K.RS[f]["wt"], 1)
    K.nc.sync.dma_start(K.wt_dram[f].rearrange("t e p -> (t e) p"), K.r_wt[:, :]).then_inc(K.RS[f]["st"], 16)
    K.nc.sync.wait_ge(K.RS[f]["st"], 16)


def slot_load(K, f, c, n):
    for a, b, e in SLOT_LOADS[n]:
        src = K.wt_dram[f][at(c * TPC, TPC), e - 1, :].partition_broadcast(b - a)
        K.nc.sync.dma_start(K.w_slots[a:b, n, :].rearrange("p (t q) -> p t q", q=P), src).then_inc(K.slot_sems[n], 16)


def slot_base(K, f, n):
    return 16 * len(SLOT_LOADS[n]) * NCH * f


def T(K, c, n):
    return c * NT + n


def up_pe(K, f, c, n, first=False):
    e, s = K.nc.tensor, K.FF[f]
    if n == 0:
        e.wait_ge(K.NS[2 * f]["lo"], c + 1)
    if not (first and n < 2):
        e.wait_ge(s["act"], T(K, c, n) - 1)
    w = slice(n * P, (n + 1) * P)
    zc = at(c * CHUNK, CHUNK)
    for which, b in (("g", G_BANK[n % 2]), ("u", U_BANK[n % 2])):
        e.matmul(bank(K, b), K.wide[which + "h"][:, w], K.zt_h[:, zc], start=True, stop=False)
        e.matmul(bank(K, b), K.wide[which + "h"][:, w], K.zt_l[:, zc], start=False, stop=False)
        ins = e.matmul(bank(K, b), K.wide[which + "l"][:, w], K.zt_h[:, zc], start=False, stop=True)
    ins.then_inc(s["up"], 1)


def down_pe(K, f, c, n, first=False):
    e, s = K.nc.tensor, K.FF[f]
    if n == 0 and not first:
        e.wait_ge(s["yev"], c)
    e.wait_ge(s["lo"], T(K, c, n) + 1)
    w = slice(n * P, (n + 1) * P)
    e.matmul(bank(K, Y_BANK), K.wide["dh"][:, w], K.act_h[:, PLACE[n], :], start=(n == 0), stop=False)
    e.matmul(bank(K, Y_BANK), K.wide["dl"][:, w], K.act_h[:, PLACE[n], :], start=False, stop=False)
    e.matmul(bank(K, Y_BANK), K.wide["dh"][:, w], K.act_l[:, PLACE[n], :], start=False,
             stop=(n == NT - 1)).then_inc(s["down"], 1)


def ytr_pe(K, f, c, first=False):
    e, s = K.nc.tensor, K.FF[f]
    e.wait_ge(s["yev"], c + 1)
    if not first:
        if f == 0:
            e.wait_ge(K.NS[1]["lo"], c)
        else:
            e.wait_ge(s["out"], c)
    for t in range(TPC):
        ins = e.transpose(bank(K, N_BANK)[:, t * P:(t + 1) * P], K.yt[:, t * P:(t + 1) * P], K.ident[:, :])
    ins.then_inc(s["ytr"], 1)


def ffn_pe(K, f):
    def body(c, before):
        for n in range(NT):
            up_pe(K, f, c, n, before is None)
            if n >= 3:
                down_pe(K, f, c, n - 3, before is None)
            elif before is not None:
                down_pe(K, f, before, n + NT - 3)
            if before is not None and n == 4:
                ytr_pe(K, f, before)
            if before is not None and n == 10 and f == 0:
                norm_tr_pe(K, 1, before)
    body(0, None)
    with K.nc.tensor.Fori(1, NCH) as c:
        body(c, c - 1)
    for n in range(NT - 3, NT):
        down_pe(K, f, NCH - 1, n)
    ytr_pe(K, f, NCH - 1)
    if f == 0:
        norm_tr_pe(K, 1, NCH - 1)


def silu_act(K, f, c, n):
    e, s = K.nc.scalar, K.FF[f]
    e.wait_ge(s["up"], T(K, c, n) + 1)
    e.activation(K.silu[:, n % 2, :], bank(K, G_BANK[n % 2]), ACT.Silu).then_inc(s["silu"], 1)


def hi_act(K, f, c, n, first=False):
    e, s = K.nc.scalar, K.FF[f]
    if n >= FIRST_ROUTED:
        e.wait_ge(s["route"], c * NROUTED + (n - FIRST_ROUTED + 1))
    else:
        e.wait_ge(s["act"], T(K, c, n) + 1)
    if not (first and n < 4):
        e.wait_ge(s["down"], T(K, c, n - BACK[n]) + 1)
    e.copy(K.act_h[:, PLACE[n], :], K.act[:, PLACE[n], :]).then_inc(s["hi"], 1)


def ffn_act(K, f):
    def body(c, before):
        for n in range(NT):
            silu_act(K, f, c, n)
            if n >= 2:
                hi_act(K, f, c, n - 2, before is None)
            elif before is not None:
                hi_act(K, f, before, n + NT - 2)
            if before is not None and n == 11 and f == 0:
                norm_hi_act(K, 1, before)
    body(0, None)
    with K.nc.scalar.Fori(1, NCH) as c:
        body(c, c - 1)
    for n in range(NT - 2, NT):
        hi_act(K, f, NCH - 1, n)
    if f == 0:
        norm_hi_act(K, 1, NCH - 1)


def act_dve(K, f, c, n, first=False):
    e, s = K.nc.vector, K.FF[f]
    e.wait_ge(s["silu"], T(K, c, n) + 1)
    if not (first and n < 4):
        e.wait_ge(s["lo"], T(K, c, n - BACK[n]) + 1)
    e.tensor_tensor(K.act[:, PLACE[n], :], K.silu[:, n % 2, :], bank(K, U_BANK[n % 2]), ALU.mult).then_inc(s["act"], 1)


def lo_dve(K, f, c, n):
    e, s = K.nc.vector, K.FF[f]
    e.wait_ge(s["hi"], T(K, c, n) + 1)
    e.tensor_tensor(K.act_l[:, PLACE[n], :], K.act[:, PLACE[n], :], K.act_h[:, PLACE[n], :].bitcast(F32),
                    ALU.subtract).then_inc(s["lo"], 1)


def yev_dve(K, f, c, first=False):
    e, s = K.nc.vector, K.FF[f]
    e.wait_ge(s["down"], T(K, c, NT - 1) + 1)
    if not first:
        e.wait_ge(s["ytr"], c)
    e.tensor_scalar(K.yt[:, :], bank(K, Y_BANK), 0.5, None, ALU.mult).then_inc(s["yev"], 1)


def xup_dve(K, f, c):
    e, s = K.nc.vector, K.FF[f]
    e.wait_ge(s["ytr"], c + 1)
    xc = K.x[:, at(c * TPC, TPC), :]
    e.tensor_tensor(xc, xc, bank(K, N_BANK).rearrange("p (t e) -> p t e", e=EMB), ALU.add)\
     .then_inc(s["out"], 1)


def ffn_dve(K, f):
    def after(c, n):
        if n == 3:
            yev_dve(K, f, c)
        if n == 5:
            xup_dve(K, f, c)
        if f == 0:
            if n == 6:
                K.nc.vector.wait_ge(K.FF[0]["out"], c + 1)
                alone(K, K.nc.vector)
                norm_stats_dve(K, 1, c)
            if n == 9:
                norm_z_dve(K, 1, c)
            if n == 12:
                norm_lo_dve(K, 1, c)

    def body(c, before):
        for n in range(NT):
            if before is not None:
                after(before, n)
            act_dve(K, f, c, n, before is None)
            if n >= 2:
                lo_dve(K, f, c, n - 2)
            elif before is not None:
                lo_dve(K, f, before, n + NT - 2)
    body(0, None)
    with K.nc.vector.Fori(1, NCH) as c:
        body(c, c - 1)
    for n in range(NT - 2, NT):
        lo_dve(K, f, NCH - 1, n)
    for n in range(NT):
        after(NCH - 1, n)


def ffn_pool(K, f):
    e, s = K.nc.gpsimd, K.FF[f]

    def body(c, before):
        for n in range(NT):
            if before is not None and n == 8 and f == 0:
                norm_rstd_pool(K, 1, before)
            if n < FIRST_ROUTED:
                continue
            slot = SLOT_OF[n]
            e.wait_ge(s["act"], T(K, c, n) + 1)
            if n == FIRST_ROUTED or SLOT_OF[n - 1] != slot:
                e.wait_ge(K.slot_sems[slot], slot_base(K, f, slot) + 16 * len(SLOT_LOADS[slot]) * (c + 1))
            e.tensor_tensor(K.act[:, PLACE[n], :], K.act[:, PLACE[n], :], K.w_slots[:, slot, :], ALU.mult)\
             .then_inc(s["route"], 1)
    body(0, None)
    with e.Fori(1, NCH) as c:
        body(c, c - 1)
    if f == 0:
        norm_rstd_pool(K, 1, NCH - 1)


def ffn_sp(K, f):
    e, s = K.nc.sync, K.FF[f]
    order = sorted(range(len(SLOT_LOADS)), key=lambda n: SLOT_END[n])
    for n in order:
        slot_load(K, f, 0, n)
    with e.Fori(1, NCH) as c:
        for n in order:
            e.wait_ge(s["route"], (c - 1) * NROUTED + (SLOT_END[n] - FIRST_ROUTED + 1))
            slot_load(K, f, c, n)
        if f == 1:
            store_out(K, c - 1)
    if f == 1:
        store_out(K, NCH - 1)
        e.wait_ge(K.ld["out"], 16 * NCH)


def store_out(K, c):
    K.nc.sync.wait_ge(K.FF[1]["out"], c + 1)
    K.nc.sync.dma_start(K.out_tiles[:, at(c * TPC, TPC), :], K.x[:, at(c * TPC, TPC), :])\
      .then_inc(K.ld["out"], 16)



def start_sp(K):
    e = K.nc.sync
    e.dma_start(K.x[:, :, :], K.tokens.rearrange("b (t p) e -> p (b t) e", p=P)).then_inc(K.ld["x"], 16)
    r0 = HID // P * P
    rg_rows, ru_rows = (w.rearrange("e i h -> (e i) h") for w in (K.gate_r, K.up_r))
    for w, shared, routed in (("g", K.gate_s, rg_rows), ("u", K.up_s, ru_rows)):
        dst = K.nat[w][:, :].rearrange("p (n h) -> p n h", h=EMB)
        head = (HID // P + 1) * P - HID
        e.dma_start(dst[:, 0:HID // P, :], shared[0:r0, :].rearrange("(n p) h -> p n h", p=P))\
         .then_inc(K.ld["nat"], 16)
        e.dma_start(dst[0:HID - r0, HID // P, :], shared[r0:HID, :]).then_inc(K.ld["nat"], 16)
        e.dma_start(dst[HID - r0:P, HID // P, :], routed[0:head, :]).then_inc(K.ld["nat"], 16)
        e.dma_start(dst[:, HID // P + 1:, :], routed[head:, :].rearrange("(n p) h -> p n h", p=P))\
         .then_inc(K.ld["nat"], 16)
    e.dma_start(K.nat["d"][:, 0:HID], K.down_s).then_inc(K.ld["nat"], 16)
    e.dma_start(K.nat["d"][:, HID:].rearrange("p (e i) -> p e i", i=HID), K.down_r.rearrange("e h i -> h e i"))\
     .then_inc(K.ld["nat"], 16)
    e.wait_ge(K.consts, N_CONST)
    def many(src, n):
        return src[:, :].unsqueeze(1).to_broadcast([32, n * SEQ // CHUNK, CHUNK])
    def rows(dram, a, b):
        return dram[:, a:b, :].rearrange("g r (s t) -> g (r s) t", t=CHUNK)
    e.dma_start(rows(K.q_dram, 0, 8), many(K.rows0, 8)).then_inc(K.ld["const"], 16)
    e.dma_start(rows(K.k_dram, 0, 2), many(K.rows1, 2)).then_inc(K.ld["const"], 16)
    e.dma_start(rows(K.k_dram, 2, 8), many(K.rows0, 6)).then_inc(K.ld["const"], 16)


def start_act(K):
    e = K.nc.scalar
    e.dma_start(K.nat_attn[:, :], K.attn_w).then_inc(K.ld["small"], 16)
    e.dma_start(K.nat_proj[:, :], K.proj_w).then_inc(K.ld["small"], 16)
    e.wait_ge(K.consts, N_CONST)
    e.dma_start(K.nat_route[0:ROUTED, :], K.route_w).then_inc(K.ld["small"], 16)
    e.dma_start(K.b_q[:, :], K.attn_b[0:EMB].rearrange("(p a) -> p a", a=1)).then_inc(K.ld["small"], 16)
    e.dma_start(K.b_k[:, :], K.attn_b[EMB:2 * EMB].rearrange("(p a) -> p a", a=1)).then_inc(K.ld["small"], 16)
    e.dma_start(K.b_v[:, :], K.attn_b[2 * EMB:3 * EMB].partition_broadcast(P)).then_inc(K.ld["small"], 16)
    e.dma_start(K.b_p[:, :], K.proj_b.partition_broadcast(P)).then_inc(K.ld["small"], 16)
    e.dma_start(K.rb_row[:, 0:ROUTED], K.route_b.partition_broadcast(P)).then_inc(K.ld["small"], 16)


def start_pool(K):
    e = K.nc.gpsimd
    e.memset(K.ident[:, :], 0.0).then_inc(K.blank, 1)
    e.memset(K.mask_b[:, :], 0.0).then_inc(K.blank, 1)
    e.iota(K.rank_i[:, :], pattern=[[-1, NGATE]], base=NGATE, channel_multiplier=0).then_inc(K.blank, 1)
    e.wait_ge(K.blank, 3)
    e.affine_select(out=K.ident[:, :], in_=K.ident[:, :], compare_op=ALU.not_equal, fill=1.0, base=0,
                    pattern=[[-1, P]], channel_multiplier=1).then_inc(K.blank, 1)
    e.wait_ge(K.blank, 4)
    e.tensor_copy(K.ident_b[:, :], K.ident[:, :]).then_inc(K.consts, 1)
    e.affine_select(out=K.mask_b[:, :], in_=K.mask_b[:, :], compare_op=ALU.is_ge, fill=MASKED, base=0,
                    pattern=[[1, P]], channel_multiplier=-1).then_inc(K.consts, 1)
    e.memset(K.rows0[:, :], 0.0).then_inc(K.consts, 1)
    e.memset(K.rows1[:, :], 1.0).then_inc(K.consts, 1)
    e.memset(K.nat_route[:, :], 0.0).then_inc(K.consts, 1)
    e.memset(K.rb_row[:, :], MASKED).then_inc(K.consts, 1)
    e.tensor_copy(K.rank[:, :], K.rank_i[:, :]).then_inc(K.consts, 1)
    e.memset(K.half_neg[:, :], -0.5).then_inc(K.consts, 1)
    e.memset(K.shared_rows, 1.0).then_inc(K.consts, 1)
    for c in range(NCH):
        norm_rstd_pool(K, 0, c)


def clear_pool(K):
    e = K.nc.gpsimd
    e.wait_ge(K.tp_pe, len(TP_GROUPS))
    e.wait_ge(K.sw_lo, 5)
    e.wait_ge(K.ld["const"], 16 * N_CONST_DMA)
    for u in range(2):
        e.memset(K.km[u][:, :, :].bitcast(F32), 0.0).then_inc(K.cleared, 1)


def weights_pe(K, part):
    e = K.nc.tensor
    if part == 0:
        e.wait_ge(K.ld["small"], 16 * N_SMALL)
        e.wait_ge(K.consts, N_CONST)
        e.transpose(bank(K, 6)[:, 0:P], K.nat_attn[:, EMB:2 * EMB], K.ident[:, :])
        e.transpose(bank(K, 6)[:, P:2 * P], K.nat_route[:, :], K.ident[:, :]).then_inc(K.A["init"], 1)
        e.wait_ge(K.ld["nat"], 16 * 10)
    for m, (w, n0, k) in enumerate(TP_GROUPS):
        if m >= 4:
            e.wait_ge(K.tp_lo, m - 3)
        for t in range(k):
            ins = e.transpose(bank(K, TP_BANKS[m % 4])[:, t * P:(t + 1) * P],
                              K.nat[w][:, (n0 + t) * P:(n0 + t + 1) * P], K.ident[:, :])
        ins.then_inc(K.tp_pe, 1)


def weights_act(K):
    e = K.nc.scalar
    e.wait_ge(K.ld["small"], 16 * N_SMALL)
    e.copy(K.small["qh"][:, :], K.nat_attn[:, 0:EMB]).then_inc(K.sw_hi, 1)
    e.copy(K.small["vh"][:, :], K.nat_attn[:, 2 * EMB:]).then_inc(K.sw_hi, 1)
    e.copy(K.small["ph"][:, :], K.nat_proj[:, :]).then_inc(K.sw_hi, 1)
    e.wait_ge(K.A["init"], 1)
    e.copy(K.small["kh"][:, :], bank(K, 6)[:, 0:P]).then_inc(K.sw_hi, 1)
    e.copy(K.rw_h[:, :], bank(K, 6)[:, P:P + NGATE]).then_inc(K.sw_hi, 1)


def weights_hi_act(K, m):
    w, n0, k = TP_GROUPS[m]
    K.nc.scalar.wait_ge(K.tp_pe, m + 1)
    K.nc.scalar.copy(K.wide[w + "h"][:, n0 * P:(n0 + k) * P], bank(K, TP_BANKS[m % 4])[:, 0:k * P]).then_inc(K.tp_hi, 1)


def weights_small_dve(K):
    e = K.nc.vector
    for n, (w, src) in enumerate((("q", K.nat_attn[:, 0:EMB]), ("v", K.nat_attn[:, 2 * EMB:]),
                                  ("p", K.nat_proj[:, :]), ("k", bank(K, 6)[:, 0:P]))):
        e.wait_ge(K.sw_hi, 5)
        e.tensor_tensor(K.small[w + "l"][:, :], src, K.small[w + "h"][:, :].bitcast(F32), ALU.subtract)\
         .then_inc(K.sw_lo, 1)
    e.tensor_tensor(K.rw_l[:, :], bank(K, 6)[:, P:P + NGATE], K.rw_h[:, :].bitcast(F32), ALU.subtract)\
     .then_inc(K.sw_lo, 1)


def weights_lo_dve(K, m):
    w, n0, k = TP_GROUPS[m]
    K.nc.vector.wait_ge(K.tp_hi, m + 1)
    cols = slice(n0 * P, (n0 + k) * P)
    K.nc.vector.tensor_tensor(K.wide[w + "l"][:, cols], bank(K, TP_BANKS[m % 4])[:, 0:k * P],
                            K.wide[w + "h"][:, cols].bitcast(F32), ALU.subtract).then_inc(K.tp_lo, 1)


def three(K, e, dst, left, right):
    e.matmul(dst, left[0], right[0], start=True, stop=False)
    e.matmul(dst, left[0], right[1], start=False, stop=False)
    return e.matmul(dst, left[1], right[0], start=False, stop=True)


def qkv_pe(K):
    e = K.nc.tensor
    for c in range(NCH):
        u, cols = c % 2, slice(c * CHUNK, (c + 1) * CHUNK)
        e.wait_ge(K.NS[1]["lo"], c + 1)
        if c >= 2:
            e.wait_ge(K.A["q1f"], c - 1)
        three(K, e, bank(K, 0 + u), (K.small["qh"][:, :], K.small["ql"][:, :]), (K.zt_h[:, cols], K.zt_l[:, cols]))\
            .then_inc(K.A["q1"], 1)
        if c >= 2:
            e.wait_ge(K.A["vev"], c - 1)
        for t in range(TPC):
            tc = slice(c * CHUNK + t * P, c * CHUNK + (t + 1) * P)
            ins = three(K, e, bank(K, 4 + u)[:, t * P:(t + 1) * P], (K.zt_h[:, tc], K.zt_l[:, tc]),
                        (K.small["vh"][:, :], K.small["vl"][:, :]))
        ins.then_inc(K.A["v"], 1)
        e.wait_ge(K.A["q1l"], c + 1)
        if c >= 2:
            e.wait_ge(K.A["qf"], c - 1)
        three(K, e, bank(K, 2 + u), (K.small["kh"][:, :], K.small["kl"][:, :]), (K.q1_h[:, u, :], K.q1_l[:, u, :]))\
            .then_inc(K.A["q"], 1)


def qkv_act(K):
    e = K.nc.scalar
    for c in range(NCH):
        u = c % 2
        e.wait_ge(K.A["q1"], c + 1)
        if c >= 2:
            e.wait_ge(K.A["q"], c - 1)
        e.activation(K.q1_f[:, u, :], bank(K, 0 + u), ACT.Identity, bias=K.b_q[:, 0:1]).then_inc(K.A["q1f"], 1)
        e.wait_ge(K.A["q1f"], c + 1)
        e.copy(K.q1_h[:, u, :], K.q1_f[:, u, :]).then_inc(K.A["q1h"], 1)
        e.wait_ge(K.A["q"], c + 1)
        if c >= 2:
            e.wait_ge(K.A["ql"], c - 1)
            e.wait_ge(K.q_st[c - 2], 16 * 3)
        e.activation(K.q_f[:, u, :], bank(K, 2 + u), ACT.Identity, bias=K.b_k[:, 0:1]).then_inc(K.A["qf"], 1)
        e.wait_ge(K.A["qf"], c + 1)
        e.copy(K.q_h[:, u, :], K.q_f[:, u, :]).then_inc(K.A["qh"], 1)


def qkv_dve(K):
    e = K.nc.vector
    for c in range(NCH):
        u, b, half = c % 2, c // 2, c % 2
        e.wait_ge(K.A["q1h"], c + 1)
        e.tensor_tensor(K.q1_l[:, u, :], K.q1_f[:, u, :], K.q1_h[:, u, :].bitcast(F32), ALU.subtract)\
         .then_inc(K.A["q1l"], 1)
        e.wait_ge(K.A["v"], c + 1)
        dst = K.v_all[:, b * GPB:(b + 1) * GPB, half * TPC:(half + 1) * TPC, :].rearrange("p g t m -> p t g m")
        src = bank(K, 4 + u).rearrange("p (t g m) -> p t g m", g=GPB, m=32)
        bias = K.b_v[:, :].rearrange("p (g m) -> p g m", m=32)
        for t in range(TPC):
            ins = e.tensor_tensor(dst[:, t], src[:, t], bias, ALU.add)
        ins.then_inc(K.A["vev"], 1)
        e.wait_ge(K.A["qh"], c + 1)
        e.tensor_tensor(K.q_l[:, u, :], K.q_f[:, u, :], K.q_h[:, u, :].bitcast(F32), ALU.subtract)\
         .then_inc(K.A["ql"], 1)


def stack_store(K, dram, part, c, src, s):
    b, half = c // 2, c % 2
    dst = dram[b * HEADS:(b + 1) * HEADS, 8 + 8 * part:16 + 8 * part, half * CHUNK:(half + 1) * CHUNK]
    K.nc.sync.dma_start(dst, src.bitcast(F32)).then_inc(s, 16)


def qkv_sp(K):
    e = K.nc.sync
    for c in range(NCH):
        u, cols = c % 2, slice(c * CHUNK, (c + 1) * CHUNK)
        e.wait_ge(K.NS[1]["lo"], c + 1)
        stack_store(K, K.k_dram, 0, c, K.zt_h[:, cols], K.k_st[c])
        stack_store(K, K.k_dram, 1, c, K.zt_l[:, cols], K.k_st[c])
        stack_store(K, K.k_dram, 2, c, K.zt_h[:, cols], K.k_st[c])
        e.wait_ge(K.A["ql"], c + 1)
        stack_store(K, K.q_dram, 0, c, K.q_h[:, u, :], K.q_st[c])
        stack_store(K, K.q_dram, 1, c, K.q_h[:, u, :], K.q_st[c])
        stack_store(K, K.q_dram, 2, c, K.q_l[:, u, :], K.q_st[c])


def m_unit_pe(K, n, r_bank, u):
    e = K.nc.tensor
    pieces, j = MAX_BANKS[n // 4], n % 4
    dst = bank(K, r_bank)
    for m, (i, k0, nb, at0, diag) in enumerate(pieces):
        ins = e.matmul(dst[:, at0 * P:(at0 + nb) * P], K.qm[u][:, i * P:(i + 1) * P],
                       K.km[u][:, j, k0 * P:(k0 + nb) * P], start=(m == 0), stop=True, skip_group_check=True)
    for i, k0, nb, at0, diag in pieces:
        if diag:
            last = (at0 + nb - 1) * P
            ins = e.matmul(dst[:, last:last + P], K.mask_b[:, :], K.ident_b[:, :], start=False, stop=True,
                           skip_group_check=True)
    return ins


def ring_pe(K, what, d, n, p, u, r, r_bank, start=False):
    e, v = K.nc.tensor, (u + d) % 2
    if not start:
        e.wait_ge(K.A["taken"], r - 1)
    if what == "max":
        if n == 0:
            e.wait_ge(K.ld_m[v], 80 * loads(p, u, d))
        ins = m_unit_pe(K, n, r_bank, v)
    elif what == "mrow":
        e.wait_ge(K.A["mm"], count(p, u, 1, d + 2))
        ins = e.transpose(bank(K, r_bank)[:, 0:P],
                          K.mm_hl[:, :, :, :].bitcast(F32).rearrange("p j a i -> p (j a i)"), K.ident[:, :])
    else:
        e.wait_ge(K.A["oev"], count(p, u, 2, 2 * d + n + 2))
        for t in range(4):
            ins = e.transpose(bank(K, r_bank)[:, t * P:(t + 1) * P], K.ot[:, n, t * P:(t + 1) * P], K.ident[:, :])
    ins.then_inc(K.A["ring"], 1)


def unit_pe(K, p, u, d, n, start=False):
    e = K.nc.tensor
    kt, heads = UNITS[n]
    v = (u + d) % 2
    if not start:
        e.wait_ge(K.A["ex"], count(p, u, NU, d * NU + n - 1))
    if n == 0:
        e.wait_ge(K.ld_s[v], 32 * loads(p, u, d))
        e.wait_ge(K.ld_r[v], 64 * loads(p, u, d))
    slot = SLOTS[n % 2]
    for m, j in enumerate(heads):
        rows = slice(32 * j, 32 * j + 32)
        for half in range(2):
            q0, q1 = max(kt * P, half * CHUNK), (half + 1) * CHUNK
            if q0 < q1:
                b = slot + (m if len(heads) > 1 else half)
                ins = e.matmul(bank(K, b)[:, q0 - half * CHUNK:CHUNK], K.ks[v][rows, kt * P:(kt + 1) * P],
                               K.qs[v][rows, q0:q1], start=True, stop=True)
    ins.then_inc(K.A["sp"], 1)


def pv_pe(K, p, u, kt):
    e = K.nc.tensor
    e.wait_ge(K.A["mk"], count(p, u, KT, kt + 1))
    if kt == 0:
        e.wait_ge(K.A["vg"], count(p, u, 1, 1))
        e.wait_ge(K.A["oev"], count(p, u, 2, 1))
    for half in range(2):
        q0, q1 = max(kt * P, half * CHUNK), (half + 1) * CHUNK
        if q0 >= q1:
            continue
        for j in range(4):
            ins = e.matmul(bank(K, O_BANK[half])[32 * j:32 * j + 32, q0 - half * CHUNK:CHUNK],
                           K.vg[u][:, kt, j, :], K.probs[:, kt % 2, j, q0:q1],
                           start=(kt == 0), stop=(kt == 4 * half + 3), skip_group_check=True)
    ins.then_inc(K.A["pv"], 1)


def pe_body(K, p, u, kind):
    ring, took = RINGS[kind], 0
    for step in range(KT):
        d, kt = (0, step + 1) if step + 1 < KT else (1, 0)
        units = list(range(FIRST_UNIT[kt], FIRST_UNIT[kt + 1])) if d == 0 or kind != LAST else []
        share = SHARES[kind][step]
        for k in range(max(share, len(units))):
            if k < len(units):
                unit_pe(K, p, u, d, units[k])
            if k < share:
                what, dd, n = ring[took]
                number = count(p, u, RINGN, RING0[kind] + took)
                ring_pe(K, what, dd, n, p, u, number, RING[(u * RINGN + RING0[kind] + took) % 2])
                took += 1
        pv_pe(K, p, u, step)
    assert took == len(ring)


def attn_pe(K):
    e = K.nc.tensor
    for r, (what, d, n) in enumerate(RING_PROLOGUE):
        ring_pe(K, what, d, n, 0, 0, r, RING[r % 2], start=r < 2)
    e.sem_inc(K.A["pv"], 1)
    for n in range(FIRST_UNIT[1]):
        unit_pe(K, 0, 0, 0, n, start=n < 2)
    with e.Fori(0, LOOPED // 2) as p:
        for u in range(2):
            pe_body(K, p, u, LOOP)
    pe_body(K, LOOPED // 2, 0, LAST_BUT_ONE)
    pe_body(K, LOOPED // 2, 1, LAST)
    ring_pe(K, "out", -1, 1, GROUPS // 2, 0, RING_END, RING[RING_END % 2])


def ring_dve(K, what, d, n, p, u, r, r_bank, start=False):
    e = K.nc.vector
    e.wait_ge(K.A["ring"], r + 1)
    if what == "max":
        if n == 0:
            e.wait_ge(K.A["nm"], count(p, u, KT + 1, (KT + 1) * d))
        b, j = n // 4, n % 4
        e.tensor_reduce(K.mxp[:, j, 4 * b:4 * b + 4], bank(K, r_bank).rearrange("p (m k) -> p m k", k=P),
                        AX.X, ALU.max).then_inc(K.A["taken"], 1)
        if n == NMAX - 1:
            e.wait_ge(K.A["taken"], r + 1)
            e.wait_ge(K.A["mm"], count(p, u, 1, d + 1))
            for i, (lo, hi) in sorted(max_slots().items()):
                e.tensor_reduce(K.nmax[:, :, i:i + 1], K.mxp[:, :, lo:hi], AX.X, ALU.max, negate=True)\
                 .then_inc(K.A["nm"], 1)
            e.wait_ge(K.A["nm"], count(p, u, KT + 1, (KT + 1) * d + KT))
            e.tensor_copy(K.mm_hl[:, 0:4, 0, :], K.nmax[:, :, :]).then_inc(K.A["nm"], 1)
            e.wait_ge(K.A["nm"], count(p, u, KT + 1, (KT + 1) * (d + 1)))
            e.tensor_tensor(K.mm_hl[:, 0:4, 1, :], K.nmax[:, :, :], K.mm_hl[:, 0:4, 0, :].bitcast(F32),
                            ALU.subtract).then_inc(K.A["mm"], 1)
    elif what == "mrow":
        if not start:
            e.wait_ge(K.ld_r[(u + d - 1) % 2], 64 * loads(p, u, d - 1))
        e.tensor_copy(K.m_rows[:, :], bank(K, r_bank)[:, 0:P]).then_inc(K.A["taken"], 1)
    else:
        b = bank(K, r_bank).rearrange("p (m c) -> p m c", c=32)
        e.wait_ge(K.A["taken"], r)
        e.reciprocal(K.rsum[:, :, :], b[:, :, HDIM:HDIM + 1]).then_inc(K.A["rs"], 1)
        e.wait_ge(K.A["rs"], count(p, u, 2, 2 * d + n + 2))
        dst = K.o_all[:, at(count(p, u, 1, d + 1), 1), 4 * n:4 * n + 4, :].rearrange("p g t (j c) -> p (g t j) c", c=HDIM)
        e.tensor_tensor(dst, b[:, :, 0:HDIM], K.rsum[:, :, :].to_broadcast([P, 16, HDIM]), ALU.mult)\
         .then_inc(K.A["taken"], 1)


def dve_body(K, p, u, kind):
    for k, (what, d, n) in enumerate(RINGS[kind]):
        number = count(p, u, RINGN, RING0[kind] + k)
        ring_dve(K, what, d, n, p, u, number, RING[(u * RINGN + RING0[kind] + k) % 2])


def attn_dve(K):
    e = K.nc.vector
    e.memset(K.mm_hl[:, :, :, :].bitcast(F32), 0.0).then_inc(K.A["mm"], 1)
    for r, (what, d, n) in enumerate(RING_PROLOGUE):
        ring_dve(K, what, d, n, 0, 0, r, RING[r % 2], start=True)
    with e.Fori(0, LOOPED // 2) as p:
        for u in range(2):
            dve_body(K, p, u, LOOP)
    dve_body(K, LOOPED // 2, 0, LAST_BUT_ONE)
    dve_body(K, LOOPED // 2, 1, LAST)
    ring_dve(K, "out", -1, 1, GROUPS // 2, 0, RING_END, RING[RING_END % 2])


def unit_act(K, p, u, d, n, start=False):
    e = K.nc.scalar
    kt, heads = UNITS[n]
    e.wait_ge(K.A["sp"], count(p, u, NU, d * NU + n + 1))
    if n == FIRST_UNIT[kt] and not start:
        e.wait_ge(K.A["pv"], count(p, u, KT, d * KT + kt))
    q0 = kt * P
    if len(heads) == 1:
        src = K.psum[:, SLOTS[n % 2]:SLOTS[n % 2] + 2, :].rearrange("p b c -> p (b c)")[:, q0:SEQ]
        dst = K.probs[:, kt % 2, heads[0], q0:SEQ]
    else:
        src = K.psum[:, SLOTS[n % 2]:SLOTS[n % 2] + 2, q0 - CHUNK:CHUNK]
        dst = K.probs[:, kt % 2, heads[0]:heads[1] + 1, q0:SEQ]
    e.activation(dst, src, ACT.Exp, scale=SCALE).then_inc(K.A["ex"], 1)


def oev_act(K, p, u, kind, half):
    e = K.nc.scalar
    e.wait_ge(K.A["pv"], count(p, u, KT, 4 * half + 5))
    if half == 0:
        at0 = RINGS[LAST_BUT_ONE if kind == LAST else LOOP].index(("out", 0, 0)) + RING0[LOOP] - RINGN
    else:
        at0 = RINGS[kind].index(("out", -1, 1)) + RING0[kind]
    e.wait_ge(K.A["ring"], count(p, u, RINGN, at0 + 1))
    e.copy(K.ot[:, half, :], bank(K, O_BANK[half])).then_inc(K.A["oev"], 1)


def act_body(K, p, u, kind):
    for step in range(KT):
        d, kt = (0, step + 1) if step + 1 < KT else (1, 0)
        if d == 0 or kind != LAST:
            for n in range(FIRST_UNIT[kt], FIRST_UNIT[kt + 1]):
                unit_act(K, p, u, d, n)
        if step == 4:
            oev_act(K, p, u, kind, 0)
    oev_act(K, p, u, kind, 1)


def attn_act(K):
    e = K.nc.scalar
    e.wait_ge(K.A["ready"], 1)
    e.sem_inc(K.A["oev"], 1)
    for n in range(FIRST_UNIT[1]):
        unit_act(K, 0, 0, 0, n, start=True)
    with e.Fori(0, LOOPED // 2) as p:
        for u in range(2):
            act_body(K, p, u, LOOP)
    act_body(K, LOOPED // 2, 0, LAST_BUT_ONE)
    act_body(K, LOOPED // 2, 1, LAST)


def mask_pool(K, p, u, kt):
    e = K.nc.gpsimd
    e.wait_ge(K.A["ex"], count(p, u, NU, FIRST_UNIT[kt + 1]))
    alone(K, e)
    blk = K.probs[:, kt % 2, :, kt * P:(kt + 1) * P]
    e.affine_select(out=blk, in_=blk, compare_op=ALU.is_ge, fill=0.0, base=0,
                    pattern=[[0, 4], [1, P]], channel_multiplier=-1).then_inc(K.A["mk"], 1)


def vg_pool(K, p, u, d, start=False):
    e, v = K.nc.gpsimd, (u + d) % 2
    if not start:
        e.wait_ge(K.A["pv"], count(p, u, KT, d * KT - KT + 1))
    src = K.v_all[:, at(count(p, u, 1, d), 1), :, :].rearrange("p g t (j c) -> p (g t j) c", c=HDIM)
    dst = K.vg[v][:, :, :, :].rearrange("p t j c -> p (t j) c")[:, :, 0:HDIM]
    e.tensor_copy(dst, src).then_inc(K.A["vg"], 1)


def pool_body(K, p, u, kind):
    for kt in range(KT):
        mask_pool(K, p, u, kt)
        if kt == 1 and kind != LAST:
            vg_pool(K, p, u, 1)


def attn_pool(K):
    e = K.nc.gpsimd
    for c in range(NCH):
        e.wait_ge(K.q_st[c], 16 * 3)
    for u in range(2):
        e.memset(K.vg[u][:, :, :, :], 0.0).then_inc(K.A["vi"], 1)
    e.memset(K.ot[:, :, :], 1.0).then_inc(K.A["ready"], 1)
    e.wait_ge(K.A["vi"], 2)
    for u in range(2):
        e.memset(K.vg[u][:, :, :, HDIM:HDIM + 1], 1.0).then_inc(K.A["vi"], 1)
    e.wait_ge(K.A["vi"], 4)
    e.wait_ge(K.A["vev"], NCH)
    vg_pool(K, 0, 0, 0, start=True)
    with e.Fori(0, LOOPED // 2) as p:
        for u in range(2):
            pool_body(K, p, u, LOOP)
    pool_body(K, LOOPED // 2, 0, LAST_BUT_ONE)
    pool_body(K, LOOPED // 2, 1, LAST)


def max_load(K, p, u, d):
    v, row = (u + d) % 2, count(p, u, 4, 4 * d)
    K.nc.sync.dma_start(K.qm[v][:, :].bitcast(F32), K.q_dram[at(row, 4)].rearrange("g r t -> (g r) t"))\
     .then_inc(K.ld_m[v], 16)
    for j in range(4):
        K.nc.sync.dma_start(K.km[v][32 * j:32 * j + 32, j, :].bitcast(F32),
                            K.k_dram[at(row + j, 1)].rearrange("g r t -> (g r) t")).then_inc(K.ld_m[v], 16)


def score_load(K, p, u, d):
    v, row = (u + d) % 2, count(p, u, 4, 4 * d)
    for dst, dram in ((K.qs[v], K.q_dram), (K.ks[v], K.k_dram)):
        K.nc.sync.dma_start(dst[:, :].bitcast(F32), dram[at(row, 4)].rearrange("g r t -> (g r) t"))\
         .then_inc(K.ld_s[v], 16)


def rows_load(K, p, u, d, r):
    e, v = K.nc.sync, (u + d) % 2
    e.wait_ge(K.A["taken"], r + 1)
    e.wait_ge(K.ld_s[v], 32 * loads(p, u, d))
    for j in range(4):
        dst = K.qs[v][32 * j:32 * j + 2, :].bitcast(F32).rearrange("p (i q) -> p i q", q=P)
        e.dma_start(dst, K.m_rows[2 * KT * j:2 * KT * (j + 1), :].bitcast(F32)).then_inc(K.ld_r[v], 16)


def sp_body(K, p, u, kind):
    e = K.nc.sync
    e.wait_ge(K.A["sp"], count(p, u, NU, 1))
    score_load(K, p, u, 1)
    if kind == LOOP:
        e.wait_ge(K.A["ring"], count(p, u, RINGN, NMAX))
        max_load(K, p, u, 2)
    rows_load(K, p, u, 1, count(p, u, RINGN, RING0[kind] + RINGS[kind].index(("mrow", 1, 0))))


def attn_sp(K):
    e = K.nc.sync
    for c in range(NCH // 2):
        e.wait_ge(K.k_st[c], 16 * 3)
        e.wait_ge(K.q_st[c], 16 * 3)
    e.wait_ge(K.ld["const"], 16 * N_CONST_DMA)
    e.wait_ge(K.cleared, 2)
    max_load(K, 0, 0, 0)
    max_load(K, 0, 0, 1)
    score_load(K, 0, 0, 0)
    for c in range(NCH // 2, NCH):
        e.wait_ge(K.k_st[c], 16 * 3)
        e.wait_ge(K.q_st[c], 16 * 3)
    rows_load(K, 0, 0, 0, RING_PROLOGUE.index(("mrow", 0, 0)))
    with e.Fori(0, LOOPED // 2) as p:
        for u in range(2):
            sp_body(K, p, u, LOOP)
    sp_body(K, LOOPED // 2, 0, LAST_BUT_ONE)


def proj_pe(K):
    e = K.nc.tensor
    for c in range(NCH):
        b, u = c // 2, c % 2
        if c >= 2:
            e.wait_ge(K.A["ol"], c - 1)
        e.wait_ge(K.A["og"], c + 1)
        for t in range(TPC):
            ins = e.transpose(bank(K, 0 + u)[:, t * P:(t + 1) * P], K.ao_f[:, u, t * P:(t + 1) * P], K.ident[:, :])
        ins.then_inc(K.A["otr"], 1)
        if c >= 1:
            proj_mm(K, c - 1)
    proj_mm(K, NCH - 1)


def proj_mm(K, c):
    e, u = K.nc.tensor, c % 2
    e.wait_ge(K.A["ol"], c + 1)
    if c >= 2:
        e.wait_ge(K.A["xup"], 2 * (c - 1))
    for t in range(TPC):
        tc = slice(t * P, (t + 1) * P)
        ins = three(K, e, bank(K, 2 + u)[:, tc], (K.ao_h[:, u, tc], K.ao_l[:, u, tc]), (K.small["ph"][:, :], K.small["pl"][:, :]))
    ins.then_inc(K.A["op"], 1)


def gather_act(K, c):
    e, b, u = K.nc.scalar, c // 2, c % 2
    if c == 0:
        e.wait_ge(K.A["taken"], RING_END + 1)
    if c >= 2:
        e.wait_ge(K.A["otr"], c - 1)
    src = K.o_all[:, 1 + b * GPB:1 + (b + 1) * GPB, TPC * (c % 2):TPC * (c % 2) + TPC, :]
    e.copy(K.ao_f[:, u, :].rearrange("p (t g m) -> p g t m", g=GPB, m=32), src).then_inc(K.A["og"], 1)


def proj_act(K, c):
    e, u = K.nc.scalar, c % 2
    e.wait_ge(K.A["otr"], c + 1)
    if c >= 2:
        e.wait_ge(K.A["op"], c - 1)
    e.copy(K.ao_h[:, u, :], bank(K, 0 + u)).then_inc(K.A["oh"], 1)


def proj_lo_dve(K, c):
    e, u = K.nc.vector, c % 2
    e.wait_ge(K.A["oh"], c + 1)
    e.tensor_tensor(K.ao_l[:, u, :], bank(K, 0 + u), K.ao_h[:, u, :].bitcast(F32), ALU.subtract).then_inc(K.A["ol"], 1)


def proj_x_dve(K, c):
    e, u = K.nc.vector, c % 2
    e.wait_ge(K.A["op"], c + 1)
    xc = K.x[:, c * TPC:(c + 1) * TPC, :]
    e.tensor_tensor(xc, xc, bank(K, 2 + u).rearrange("p (t e) -> p t e", e=EMB), ALU.add).then_inc(K.A["xup"], 1)
    e.wait_ge(K.A["xup"], 2 * c + 1)
    e.tensor_tensor(xc, xc, K.b_p[:, :].unsqueeze(1).to_broadcast([P, TPC, EMB]), ALU.add).then_inc(K.A["xup"], 1)


def build(nc, tokens, attn_w, attn_b, proj_w, proj_b, gate_s, up_s, down_s, gate_r, up_r, down_r,
          route_w, route_b, result):
    K = Chip()
    K.nc, K.tokens, K.result = nc, tokens, result
    K.attn_w, K.attn_b, K.proj_w, K.proj_b = attn_w, attn_b, proj_w, proj_b
    K.gate_s, K.up_s, K.down_s = gate_s, up_s, down_s
    K.gate_r, K.up_r, K.down_r = gate_r, up_r, down_r
    K.route_w, K.route_b = route_w, route_b
    with ExitStack() as ctx:
        place_memory(K, ctx)

        block = ctx.enter_context(K.nc.Block())

        @block.sync
        def _(e):
            start_sp(K)
            router_sp(K, 0)
            ffn_sp(K, 0)
            qkv_sp(K)
            attn_sp(K)
            router_sp(K, 1)
            ffn_sp(K, 1)

        @block.tensor
        def _(e):
            weights_pe(K, 0)
            for c in range(NCH):
                norm_tr_pe(K, 0, c)
            router_pe(K, 0, 0)
            e.wait_ge(K.tp_lo, len(TP_GROUPS))
            ffn_pe(K, 0)
            qkv_pe(K)
            attn_pe(K)
            proj_pe(K)
            for c in range(NCH):
                norm_tr_pe(K, 2, c)
            router_pe(K, 1, 2)
            ffn_pe(K, 1)

        @block.scalar
        def _(e):
            start_act(K)
            weights_act(K)
            for m in range(len(TP_GROUPS)):
                weights_hi_act(K, m)
            for c in range(NCH):
                norm_hi_act(K, 0, c)
            router_act(K, 0)
            ffn_act(K, 0)
            qkv_act(K)
            attn_act(K)
            gather_act(K, 0)
            for c in range(NCH):
                if c + 1 < NCH:
                    gather_act(K, c + 1)
                proj_act(K, c)
            for c in range(NCH):
                norm_hi_act(K, 2, c)
            router_act(K, 1)
            ffn_act(K, 1)

        @block.gpsimd
        def _(e):
            start_pool(K)
            clear_pool(K)
            ffn_pool(K, 0)
            attn_pool(K)
            for c in range(NCH):
                norm_rstd_pool(K, 2, c)
            e.memset(K.shared_rows, 1.0).then_inc(K.ones, 1)
            e.wait_ge(K.ones, 1)
            ffn_pool(K, 1)

        @block.vector
        def _(e):
            weights_small_dve(K)
            for m in range(len(TP_GROUPS)):
                weights_lo_dve(K, m)
            e.wait_ge(K.ld["x"], 16)
            for c in range(NCH):
                norm_stats_dve(K, 0, c)
                norm_z_dve(K, 0, c)
                norm_lo_dve(K, 0, c)
            router_dve(K, 0)
            ffn_dve(K, 0)
            qkv_dve(K)
            attn_dve(K)
            for c in range(NCH):
                proj_lo_dve(K, c)
                if c:
                    proj_x_dve(K, c - 1)
            proj_x_dve(K, NCH - 1)
            for c in range(NCH):
                e.wait_ge(K.A["xup"], 2 * c + 2)
                norm_stats_dve(K, 2, c)
                norm_z_dve(K, 2, c)
                norm_lo_dve(K, 2, c)
            router_dve(K, 1)
            ffn_dve(K, 1)


_INS = ["attn_hidden_states", "attn_c_attn_w", "attn_c_attn_b", "attn_c_proj_w", "attn_c_proj_b",
        "ffn_sg", "ffn_su", "ffn_sd", "ffn_rg", "ffn_ru", "ffn_rd", "ffn_wr", "ffn_rb"]


def kernel(**inputs):
    import concourse.bacc as bacc
    from concourse.bass_utils import run_bass_kernel_spmd

    nc = bacc.Bacc("TRN2", target_bir_lowering=False, num_devices=1)
    arrays, args = {}, []
    for name in _INS:
        a = np.ascontiguousarray(inputs["L0_" + name])
        arrays["in_" + name] = a
        args.append(nc.dram_tensor("in_" + name, a.shape, mybir.dt.from_np(a.dtype), kind="ExternalInput").ap())
    out = nc.dram_tensor("out", (BATCH, SEQ, EMB), F32, kind="ExternalOutput").ap()
    build(nc, *args, out)
    r = run_bass_kernel_spmd(nc, [arrays], core_ids=[0])
    return r.results[0]["out"]
```

```python
from contextlib import ExitStack

import numpy as np

import concourse.bass as bass
from concourse import mybir

F32 = mybir.dt.float32
F32R = mybir.dt.float32r
BF16 = mybir.dt.bfloat16
ALU = mybir.AluOpType
ACT = mybir.ActivationFunctionType
AX = mybir.AxisListType

P = 128
BATCH, SEQ, EMB = 2, 1024, 128
HEADS, HDIM = 16, 8
TOKENS = BATCH * SEQ
TT = TOKENS // P
CHUNK = 512
NCH = TOKENS // CHUNK
TPC = CHUNK // P
HID, ROUTED = 352, 7
EXPERTS = ROUTED + 1
HROWS = HID * EXPERTS
NT = HROWS // P
LN_EPS = 1e-5
SCALE = 1.0 / float(np.sqrt(HDIM))
MASKED = -1e30
GROUPS = BATCH * HEADS // 4
GPB = GROUPS // BATCH
KT = SEQ // P
NGATE = 8


def at(start, n):
    return slice(start, start + n) if isinstance(start, int) else bass.ds(start, n)


def hidden_pieces():
    tiles = []
    for n in range(NT):
        r, runs = n * P, []
        while r < (n + 1) * P:
            e = r // HID
            end = min((n + 1) * P, (e + 1) * HID)
            runs.append((r - n * P, end - n * P, e))
            r = end
        tiles.append(runs)
    return tiles


def weight_slots():
    slots, loads, slot_of, end = {}, [], {}, []
    for n, runs in enumerate(hidden_pieces()):
        if all(e == 0 for _, _, e in runs):
            continue
        key = ("expert", runs[0][2]) if len(runs) == 1 else ("tile", n)
        if key not in slots:
            slots[key] = len(loads)
            loads.append([(a, b, e) for a, b, e in runs if e])
            end.append(n)
        slot_of[n] = slots[key]
        end[slots[key]] = n
    return slot_of, loads, end


SLOT_OF, SLOT_LOADS, SLOT_END = weight_slots()
FIRST_ROUTED = min(SLOT_OF)
NROUTED = NT - FIRST_ROUTED


PLACE = [0, 1, 2, 3] * 4 + [0, 1, 2] * 2
BACK = [3, 3, 3, 10] + [4] * 15 + [3] * 3
assert len(PLACE) == len(BACK) == NT


MAX_BANKS = [
    [(0, 0, 1, 0, True), (2, 0, 3, 1, True)],
    [(1, 0, 2, 0, True), (5, 4, 2, 2, True)],
    [(5, 0, 4, 0, False)],
    [(4, 0, 4, 0, False)],
    [(4, 4, 1, 0, True), (6, 4, 3, 1, True)],
    [(6, 0, 4, 0, False)],
    [(3, 0, 4, 0, True)],
    [(7, 0, 4, 0, False)],
    [(7, 4, 4, 0, True)],
]
NBANK = len(MAX_BANKS)
NMAX = 4 * NBANK


def max_slots():
    runs = {}
    for b, pieces in enumerate(MAX_BANKS):
        for i, _, n, at0, _ in pieces:
            lo, hi = runs.get(i, (99, 0))
            runs[i] = (min(lo, 4 * b + at0), max(hi, 4 * b + at0 + n))
    assert all(hi - lo == i + 1 for i, (lo, hi) in runs.items())
    return runs


UNITS = [(kt, (j,)) for kt in range(4) for j in range(4)] + \
        [(kt, (j, j + 1)) for kt in range(4, KT) for j in (0, 2)]
NU = len(UNITS)
FIRST_UNIT = [min(n for n, (kt, _) in enumerate(UNITS) if kt == k) for k in range(KT)] + [NU]

LEAD = NMAX // 2
MT_LATER = 3
def ring_of_body(nxt, nxt2):
    a = [("max", 1, n) for n in range(LEAD, NMAX)] if nxt else []
    b = [("max", 2, n) for n in range(LEAD)] if nxt2 else []
    ring = a[:4] + [("out", -1, 1)] + a[4:] + b[:MT_LATER]
    if nxt:
        ring += [("mrow", 1, 0), ("mrow", 1, 1)]
    ring += b[MT_LATER:]
    ring.insert(min(len(ring), 34), ("out", 0, 0))
    assert len(ring) % 2 == 0
    return ring


RING_PROLOGUE = [("max", 0, n) for n in range(NMAX)] + [("max", 1, n) for n in range(MT_LATER)] + \
                [("mrow", 0, 0), ("mrow", 0, 1)] + [("max", 1, n) for n in range(MT_LATER, LEAD)]
LOOPED = GROUPS - 2
LOOP3 = LOOPED // 3
LOOP, LAST_BUT_ONE, LAST = 0, 1, 2
RINGS = [ring_of_body(True, True), ring_of_body(True, False), ring_of_body(False, False)]
ORDERS = [["URURRaRRURbRUR", "URURaRRURbRUR", "URURaRURbRUR", "URURaRbRR", "URURaRR", "URURaR", "URUaR",
           "URURaURURR"],
          ["URUaRURbRU", "URUaRURbRU", "URUaURbRU", "URURaRb", "URURaR", "URURaR", "UURa", "UURaUU"],
          ["UURaUbU", "UUaUbU", "UUaUbU", "UUab", "UUa", "UUa", "UURa", "a"]]
RINGN = len(RINGS[LOOP])
RING0 = [len(RING_PROLOGUE), len(RING_PROLOGUE), len(RING_PROLOGUE) + len(RINGS[LAST_BUT_ONE]) - RINGN]
RING_END = RING0[LAST] + RINGN * (GROUPS - 1) + len(RINGS[LAST])


def count(p, u, each, more):
    return p * (3 * each) + (u * each + more)


def loads(p, u, d):
    return p + ((u + d) // 3 + 1)


G_BANK, U_BANK, Y_BANK, N_BANK, R_BANK = (0, 1), (2, 3), 4, 5, 6
RING, SLOTS, O_BANK = (0, 1), (2, 4), (6, 7)

TP_GROUPS = [(w, n, min(4, NT - n)) for n in range(0, NT, 4) for w in ("g", "u")] + \
            [("d", n, min(4, NT - n)) for n in range(0, NT, 4)]
TP_BANKS = (0, 1, 2, 3)
N_CONST = 7
N_SMALL = 8
N_CONST_DMA = 3


class Chip:
    pass


def place_memory(K, ctx):
    def sem(name):
        return ctx.enter_context(K.nc.semaphore(name))

    def sb(name, shape, dt=F32, scope=ctx):
        return scope.enter_context(K.nc.sbuf_tensor(name, shape, dt))

    K.wt_dram = [K.nc.dram_tensor(f"route_rows{f}", (TT, NGATE, P), F32, kind="Internal").ap() for f in range(2)]
    K.q_dram = K.nc.dram_tensor("q_stack", (GROUPS * 4, 32, SEQ), F32, kind="Internal").ap()
    K.k_dram = K.nc.dram_tensor("k_stack", (GROUPS * 4, 32, SEQ), F32, kind="Internal").ap()

    K.out_tiles = K.result.rearrange("b (t p) e -> p (b t) e", p=P)

    K.x = sb("x", [P, TT, EMB])
    K.wide = {}
    for w in ("g", "u", "d"):
        for part in ("h", "l"):
            K.wide[w + part] = sb(f"w{w}_{part}", [P, HROWS], F32R)
    K.small = {}
    for w in ("q", "k", "v", "p"):
        for part in ("h", "l"):
            K.small[w + part] = sb(f"w{w}_{part}", [P, EMB], F32R)
    K.rw_h = sb("rw_h", [P, NGATE], F32R)
    K.rw_l = sb("rw_l", [P, NGATE], F32R)
    K.ident = sb("ident", [P, P])
    K.ident_b = sb("ident_b", [P, P], BF16)
    K.mask_b = sb("mask_b", [P, P], BF16)
    K.b_q = sb("b_q", [P, 1])
    K.b_k = sb("b_k", [P, 1])
    K.b_v = sb("b_v", [P, EMB])
    K.b_p = sb("b_p", [P, EMB])
    K.rb_row = sb("rb_row", [P, NGATE])
    K.rank = sb("rank", [P, NGATE])
    K.rank_i = sb("rank_i", [P, NGATE], mybir.dt.int32)
    K.stats = sb("stats", [P, 2, TPC, 6])
    K.mv = sb("mv", [P, 2, TPC, 2])
    K.var_e = sb("var_e", [P, 2, TPC])
    K.half_neg = sb("half_neg", [P, TPC])
    K.rstd = sb("rstd", [P, 2, TPC])
    z0 = sb("z", [P, TPC, EMB])

    with ExitStack() as s:
        K.zt_h = sb("zt_h", [P, TOKENS], F32R, scope=s)
        K.zt_l = sb("zt_l", [P, TOKENS], F32R, scope=s)
        with ExitStack() as s2:
            K.w_slots = sb("w_slots", [P, len(SLOT_LOADS), CHUNK], scope=s2)
            K.silu = sb("silu", [P, 2, CHUNK], scope=s2)
            K.act = sb("act", [P, 4, CHUNK], scope=s2)
            K.act_h = sb("act_h", [P, 4, CHUNK], F32R, scope=s2)
            K.act_l = sb("act_l", [P, 4, CHUNK], F32R, scope=s2)
            K.yt = sb("yt", [P, CHUNK], scope=s2)
            K.z = [z0, K.yt[:, :].rearrange("p (t e) -> p t e", e=EMB)]
            K.r_log = sb("r_log", [P, TT, NGATE], scope=s2)
            K.r_exp = sb("r_exp", [P, TT, NGATE], scope=s2)
            K.r_p = sb("r_p", [P, TT, NGATE], scope=s2)
            K.r_c = sb("r_c", [P, TT, NGATE], scope=s2)
            K.r_s1 = sb("r_s1", [P, TT, NGATE], scope=s2)
            K.r_s2 = sb("r_s2", [P, TT, NGATE], scope=s2)
            K.r_w = sb("r_w", [P, TT, NGATE], scope=s2)
            K.r_wt = sb("r_wt", [P, P], scope=s2)
            K.r_m = sb("r_m", [P, TT], scope=s2)
            K.r_r = sb("r_r", [P, TT], scope=s2)
            with ExitStack() as s3:
                K.nat = {w: sb(f"nat_{w}", [P, HROWS], scope=s3) for w in ("g", "u", "d")}
                K.nat_attn = sb("nat_attn", [P, 3 * EMB], scope=s3)
                K.nat_proj = sb("nat_proj", [P, EMB], scope=s3)
                K.nat_route = sb("nat_route", [P, P], scope=s3)
                K.rows0 = sb("rows0", [32, CHUNK], scope=s3)
                K.rows1 = sb("rows1", [32, CHUNK], scope=s3)
            with ExitStack() as s3:
                K.keys = [sb(f"keys{u}", [P, 4, SEQ], F32R, scope=s3) for u in range(3)]
        with ExitStack() as s2:
            K.q1_f = sb("q1_f", [P, 2, CHUNK], scope=s2)
            K.q1_h = sb("q1_h", [P, 2, CHUNK], F32R, scope=s2)
            K.q1_l = sb("q1_l", [P, 2, CHUNK], F32R, scope=s2)
            K.q_f = sb("q_f", [P, 2, CHUNK], scope=s2)
            K.q_h = sb("q_h", [P, 2, CHUNK], F32R, scope=s2)
            K.q_l = sb("q_l", [P, 2, CHUNK], F32R, scope=s2)
        with ExitStack() as s2:
            K.ao_f = sb("ao_f", [P, 2, CHUNK], scope=s2)
            K.ao_h = sb("ao_h", [P, 2, CHUNK], F32R, scope=s2)
            K.ao_l = sb("ao_l", [P, 2, CHUNK], F32R, scope=s2)
    with ExitStack() as s:
        K.probs = sb("probs", [P, 2, 4, SEQ], scope=s)
        K.vg = sb("vg", [P, KT, 4, 32], scope=s)
        K.o_all = sb("o_all", [P, GROUPS + 1, KT, 32], scope=s)
        K.queries = [sb(f"queries{u}", [P, SEQ], F32R, scope=s) for u in range(3)]
        K.v_all = sb("v_all", [P, GROUPS, KT, 32], scope=s)
        K.ot = sb("ot", [P, 2, CHUNK], scope=s)
        K.rsum = sb("rsum", [P, 16, 1], scope=s)
        K.mxp = sb("mxp", [P, 4, 4 * NBANK], scope=s)
        K.nmax = sb("nmax", [P, 4, KT], scope=s)
        K.mm_hl = sb("mm_hl", [P, 4, 2, KT], F32R, scope=s)
        K.m_rows = sb("m_rows", [64, P], F32R, scope=s)

    K.shared_rows = K.w_slots[0:SLOT_LOADS[SLOT_OF[FIRST_ROUTED]][0][0], SLOT_OF[FIRST_ROUTED], :]

    K.psum = ctx.enter_context(K.nc.psum_tensor("psum", [P, 8, CHUNK], F32))


    K.ld = {n: sem(f"ld_{n}") for n in ("nat", "small", "const", "out")}
    K.ld_x = [sem(f"ld_x{b}") for b in range(BATCH)]
    K.passed = sem("passed")
    K.consts = sem("consts")
    K.tp_pe, K.tp_hi, K.tp_lo = sem("tp_pe"), sem("tp_hi"), sem("tp_lo")
    K.sw_hi, K.sw_lo = sem("sw_hi"), sem("sw_lo")
    K.padded, K.blank, K.ones, K.cleared = sem("padded"), sem("blank"), sem("ones"), sem("cleared")
    K.NS = [{n: sem(f"n{k}_{n}") for n in
                  ("bn", "mv", "ve", "rstd", "z", "tr", "hi", "lo")} for k in range(3)]
    K.RS = [{n: sem(f"r{k}_{n}") for n in
                   ("log", "neg", "exp", "step", "w", "tr", "wt", "st")} for k in range(2)]
    K.FF = [{n: sem(f"f{k}_{n}") for n in
                 ("up", "silu", "act", "route", "hi", "lo", "down", "yev", "ytr", "out")} for k in range(2)]
    K.slot_sems = [sem(f"slot{n}") for n in range(len(SLOT_LOADS))]
    K.A = {n: sem(f"a_{n}") for n in
            ("q1", "q1f", "q1h", "q1l", "q", "qf", "qh", "ql", "v", "vev", "init",
             "ring", "taken", "mm", "sp", "ex", "mk", "pv", "oev", "vg", "ready", "nm", "rs", "vi", "og", "otr", "oh", "ol", "op", "xup")}
    K.q_st = [sem(f"q_st{c}") for c in range(NCH)]
    K.k_st = [sem(f"k_st{c}") for c in range(NCH)]
    K.ld_k = [sem(f"ld_k{u}") for u in range(3)]
    K.ld_r = [sem(f"ld_r{u}") for u in range(3)]


def bank(K, n):
    return K.psum[:, n, :]


def alone(K, e):
    e.sem_inc(K.passed, 1)


def norm_stats_dve(K, k, c):
    e, v = K.nc.vector, 0 if k == 1 else c % 2
    if k != 1 and c > 1:
        e.wait_ge(K.NS[k]["z"], c - 1)
    for t in range(TPC):
        e.bn_stats(K.stats[:, v, t, :], K.x[:, at(c * TPC + t, 1), :]).then_inc(K.NS[k]["bn"], 1)
    e.wait_ge(K.NS[k]["bn"], TPC * (c + 1))
    alone(K, e)
    for t in range(TPC):
        ins = e.bn_aggr(K.mv[:, v, t, :], K.stats[:, v, t, :])
    ins.then_inc(K.NS[k]["mv"], 1)


def norm_rstd_pool(K, k, c):
    e, v = K.nc.gpsimd, 0 if k == 1 else c % 2
    e.wait_ge(K.NS[k]["mv"], c + 1)
    alone(K, e)
    e.tensor_scalar(K.var_e[:, v, :], K.mv[:, v, :, 1], LN_EPS, None, ALU.add).then_inc(K.NS[k]["ve"], 1)
    e.wait_ge(K.NS[k]["ve"], c + 1)
    e.tensor_tensor(K.rstd[:, v, :], K.var_e[:, v, :], K.half_neg[:, :], ALU.pow).then_inc(K.NS[k]["rstd"], 1)


def norm_z_dve(K, k, c):
    e, v = K.nc.vector, 0 if k == 1 else c % 2
    e.wait_ge(K.NS[k]["rstd"], c + 1)
    e.wait_ge(K.NS[k]["mv"], c + 1)
    if k != 1 and c > 1:
        e.wait_ge(K.NS[k]["tr"], c - 1)
    for t in range(TPC):
        ins = e.tensor_scalar(K.z[v][:, t, :], K.x[:, at(c * TPC + t, 1), :], K.mv[:, v, t, 0:1],
                              K.rstd[:, v, t:t + 1], ALU.subtract, ALU.mult)
    ins.then_inc(K.NS[k]["z"], 1)


def norm_bank(k, c):
    return N_BANK if k == 1 else (N_BANK, Y_BANK)[c % 2]


def norm_tr_pe(K, k, c):
    e, v = K.nc.tensor, 0 if k == 1 else c % 2
    e.wait_ge(K.NS[k]["z"], c + 1)
    if k != 1 and c > 1:
        e.wait_ge(K.NS[k]["lo"], c - 1)
    for t in range(TPC):
        ins = e.transpose(bank(K, norm_bank(k, c))[:, t * P:(t + 1) * P], K.z[v][:, t, :], K.ident[:, :])
    ins.then_inc(K.NS[k]["tr"], 1)


def norm_hi_act(K, k, c):
    K.nc.scalar.wait_ge(K.NS[k]["tr"], c + 1)
    K.nc.scalar.copy(K.zt_h[:, at(c * CHUNK, CHUNK)], bank(K, norm_bank(k, c))).then_inc(K.NS[k]["hi"], 1)


def norm_lo_dve(K, k, c):
    K.nc.vector.wait_ge(K.NS[k]["hi"], c + 1)
    K.nc.vector.tensor_tensor(K.zt_l[:, at(c * CHUNK, CHUNK)], bank(K, norm_bank(k, c)),
                            K.zt_h[:, at(c * CHUNK, CHUNK)].bitcast(F32), ALU.subtract).then_inc(K.NS[k]["lo"], 1)


def logits_pe(K, f, k, c):
    e = K.nc.tensor
    if f == 0 and c == 0:
        e.wait_ge(K.sw_lo, 5)
    e.wait_ge(K.NS[k]["lo"], c + 1)
    for t in range(c * TPC, (c + 1) * TPC):
        dst = bank(K, R_BANK)[:, t * NGATE:(t + 1) * NGATE]
        zh, zl = K.zt_h[:, t * P:(t + 1) * P], K.zt_l[:, t * P:(t + 1) * P]
        e.matmul(dst, zh, K.rw_h[:, :], start=True, stop=False)
        e.matmul(dst, zh, K.rw_l[:, :], start=False, stop=False)
        ins = e.matmul(dst, zl, K.rw_h[:, :], start=False, stop=True)
    ins.then_inc(K.RS[f]["log"], 1)


def route_tr_pe(K, f):
    e = K.nc.tensor
    e.wait_ge(K.RS[f]["w"], 1)
    e.transpose(bank(K, R_BANK)[:, CHUNK - P:], K.r_w[:, :, :].rearrange("p t e -> p (t e)"),
                K.ident[:, :]).then_inc(K.RS[f]["tr"], 1)


def router_dve(K, f):
    e, s = K.nc.vector, K.RS[f]

    def wide_of(v):
        return v.unsqueeze(2).to_broadcast([P, TT, NGATE])

    e.wait_ge(s["log"], NCH)
    logits = bank(K, R_BANK)[:, 0:TT * NGATE].rearrange("p (t e) -> p t e", e=NGATE)
    e.tensor_tensor(K.r_log[:, :, :], logits, K.rb_row[:, :].unsqueeze(1).to_broadcast([P, TT, NGATE]), ALU.add).then_inc(s["step"], 1)
    e.wait_ge(s["step"], 1)
    e.tensor_reduce(K.r_m[:, :], K.r_log[:, :, :], AX.X, ALU.max).then_inc(s["step"], 1)
    e.wait_ge(s["step"], 2)
    e.tensor_tensor(K.r_c[:, :, :], K.r_log[:, :, :], wide_of(K.r_m[:, :]), ALU.subtract).then_inc(s["neg"], 1)
    e.wait_ge(s["exp"], 1)
    e.tensor_reduce(K.r_m[:, :], K.r_exp[:, :, :], AX.X, ALU.add).then_inc(s["step"], 1)
    e.wait_ge(s["step"], 3)
    e.reciprocal(K.r_r[:, :], K.r_m[:, :]).then_inc(s["step"], 1)
    e.wait_ge(s["step"], 4)
    e.tensor_tensor(K.r_p[:, :, :], K.r_exp[:, :, :], wide_of(K.r_r[:, :]), ALU.mult).then_inc(s["step"], 1)
    e.wait_ge(s["step"], 5)
    e.tensor_scalar(K.r_w[:, :, :], K.r_p[:, :, :], 1.0, None, ALU.mult).then_inc(s["step"], 1)
    e.wait_ge(s["step"], 6)
    for sel, steps in ((K.r_s1, 6), (K.r_s2, 12)):
        e.tensor_reduce(K.r_m[:, :], K.r_w[:, :, :], AX.X, ALU.max).then_inc(s["step"], 1)
        e.wait_ge(s["step"], steps + 1)
        e.tensor_tensor(K.r_c[:, :, :], K.r_w[:, :, :], wide_of(K.r_m[:, :]), ALU.is_equal).then_inc(s["step"], 1)
        e.wait_ge(s["step"], steps + 2)
        e.tensor_tensor(K.r_c[:, :, :], K.r_c[:, :, :], K.rank[:, :].unsqueeze(1).to_broadcast([P, TT, NGATE]),
                        ALU.mult).then_inc(s["step"], 1)
        e.wait_ge(s["step"], steps + 3)
        e.tensor_reduce(K.r_m[:, :], K.r_c[:, :, :], AX.X, ALU.max).then_inc(s["step"], 1)
        e.wait_ge(s["step"], steps + 4)
        e.tensor_tensor(sel[:, :, :], K.r_c[:, :, :], wide_of(K.r_m[:, :]), ALU.is_equal).then_inc(s["step"], 1)
        e.wait_ge(s["step"], steps + 5)
        if sel is K.r_s1:
            e.scalar_tensor_tensor(K.r_w[:, :, :], K.r_s1[:, :, :], -2.0, K.r_p[:, :, :], ALU.mult, ALU.add).then_inc(s["step"], 1)
            e.wait_ge(s["step"], steps + 6)
    e.tensor_tensor(K.r_c[:, :, :], K.r_s1[:, :, :], K.r_s2[:, :, :], ALU.add).then_inc(s["step"], 1)
    e.wait_ge(s["step"], 18)
    e.tensor_tensor(K.r_c[:, :, :], K.r_c[:, :, :], K.r_p[:, :, :], ALU.mult).then_inc(s["step"], 1)
    e.wait_ge(s["step"], 19)
    e.tensor_reduce(K.r_m[:, :], K.r_c[:, :, :], AX.X, ALU.add).then_inc(s["step"], 1)
    e.wait_ge(s["step"], 20)
    e.reciprocal(K.r_r[:, :], K.r_m[:, :]).then_inc(s["step"], 1)
    e.wait_ge(s["step"], 21)
    e.tensor_tensor(K.r_w[:, :, :], K.r_c[:, :, :], wide_of(K.r_r[:, :]), ALU.mult).then_inc(s["w"], 1)
    e.wait_ge(s["tr"], 1)
    e.tensor_copy(K.r_wt[:, :], bank(K, R_BANK)[:, CHUNK - P:]).then_inc(s["wt"], 1)


def router_act(K, f):
    K.nc.scalar.wait_ge(K.RS[f]["neg"], 1)
    K.nc.scalar.activation(K.r_exp[:, :, :], K.r_c[:, :, :], ACT.Exp).then_inc(K.RS[f]["exp"], 1)


def router_sp(K, f):
    K.nc.sync.wait_ge(K.RS[f]["wt"], 1)
    K.nc.sync.dma_start(K.wt_dram[f].rearrange("t e p -> (t e) p"), K.r_wt[:, :]).then_inc(K.RS[f]["st"], 16)
    K.nc.sync.wait_ge(K.RS[f]["st"], 16)


def slot_load(K, f, c, n):
    for a, b, e in SLOT_LOADS[n]:
        src = K.wt_dram[f][at(c * TPC, TPC), e - 1, :].partition_broadcast(b - a)
        K.nc.sync.dma_start(K.w_slots[a:b, n, :].rearrange("p (t q) -> p t q", q=P), src).then_inc(K.slot_sems[n], 16)


def slot_base(K, f, n):
    return 16 * len(SLOT_LOADS[n]) * NCH * f


def T(K, c, n):
    return c * NT + n


def up_pe(K, f, c, n, first=False):
    e, s = K.nc.tensor, K.FF[f]
    if n == 0:
        e.wait_ge(K.NS[2 * f]["lo"], c + 1)
    if not (first and n < 2):
        e.wait_ge(s["act"], T(K, c, n) - 1)
    w = slice(n * P, (n + 1) * P)
    zc = at(c * CHUNK, CHUNK)
    for which, b in (("g", G_BANK[n % 2]), ("u", U_BANK[n % 2])):
        e.matmul(bank(K, b), K.wide[which + "h"][:, w], K.zt_h[:, zc], start=True, stop=False)
        e.matmul(bank(K, b), K.wide[which + "h"][:, w], K.zt_l[:, zc], start=False, stop=False)
        ins = e.matmul(bank(K, b), K.wide[which + "l"][:, w], K.zt_h[:, zc], start=False, stop=True)
    ins.then_inc(s["up"], 1)


def down_pe(K, f, c, n, first=False):
    e, s = K.nc.tensor, K.FF[f]
    if n == 0 and not first:
        e.wait_ge(s["yev"], c)
    e.wait_ge(s["lo"], T(K, c, n) + 1)
    w = slice(n * P, (n + 1) * P)
    e.matmul(bank(K, Y_BANK), K.wide["dh"][:, w], K.act_h[:, PLACE[n], :], start=(n == 0), stop=False)
    e.matmul(bank(K, Y_BANK), K.wide["dl"][:, w], K.act_h[:, PLACE[n], :], start=False, stop=False)
    e.matmul(bank(K, Y_BANK), K.wide["dh"][:, w], K.act_l[:, PLACE[n], :], start=False,
             stop=(n == NT - 1)).then_inc(s["down"], 1)


def ytr_pe(K, f, c, first=False):
    e, s = K.nc.tensor, K.FF[f]
    e.wait_ge(s["yev"], c + 1)
    if not first:
        if f == 0:
            e.wait_ge(K.NS[1]["lo"], c)
        else:
            e.wait_ge(s["out"], c)
    for t in range(TPC):
        ins = e.transpose(bank(K, N_BANK)[:, t * P:(t + 1) * P], K.yt[:, t * P:(t + 1) * P], K.ident[:, :])
    ins.then_inc(s["ytr"], 1)


def ffn_pe(K, f):
    def body(c, before):
        for n in range(NT):
            up_pe(K, f, c, n, before is None)
            if n >= 3:
                down_pe(K, f, c, n - 3, before is None)
            elif before is not None:
                down_pe(K, f, before, n + NT - 3)
            if before is None and n == 1 and f == 1:
                route_tr_pe(K, 1)
            if before is not None and n == 4:
                ytr_pe(K, f, before)
            if before is not None and n == 10 and f == 0:
                norm_tr_pe(K, 1, before)
    body(0, None)
    with K.nc.tensor.Fori(1, NCH) as c:
        body(c, c - 1)
    for n in range(NT - 3, NT):
        down_pe(K, f, NCH - 1, n)
    ytr_pe(K, f, NCH - 1)
    if f == 0:
        norm_tr_pe(K, 1, NCH - 1)


def silu_act(K, f, c, n):
    e, s = K.nc.scalar, K.FF[f]
    e.wait_ge(s["up"], T(K, c, n) + 1)
    e.activation(K.silu[:, n % 2, :], bank(K, G_BANK[n % 2]), ACT.Silu).then_inc(s["silu"], 1)


def hi_act(K, f, c, n, first=False):
    e, s = K.nc.scalar, K.FF[f]
    if n >= FIRST_ROUTED:
        e.wait_ge(s["route"], c * NROUTED + (n - FIRST_ROUTED + 1))
    else:
        e.wait_ge(s["act"], T(K, c, n) + 1)
    if not (first and n < 4):
        e.wait_ge(s["down"], T(K, c, n - BACK[n]) + 1)
    e.copy(K.act_h[:, PLACE[n], :], K.act[:, PLACE[n], :]).then_inc(s["hi"], 1)


def ffn_act(K, f):
    def body(c, before):
        for n in range(NT):
            if n >= 2:
                hi_act(K, f, c, n - 2, before is None)
            elif before is not None:
                hi_act(K, f, before, n + NT - 2)
            silu_act(K, f, c, n)
            if before is not None and n == 11 and f == 0:
                norm_hi_act(K, 1, before)
    body(0, None)
    with K.nc.scalar.Fori(1, NCH) as c:
        body(c, c - 1)
    for n in range(NT - 2, NT):
        hi_act(K, f, NCH - 1, n)
    if f == 0:
        norm_hi_act(K, 1, NCH - 1)


def act_dve(K, f, c, n, first=False):
    e, s = K.nc.vector, K.FF[f]
    e.wait_ge(s["silu"], T(K, c, n) + 1)
    if not (first and n < 4):
        e.wait_ge(s["lo"], T(K, c, n - BACK[n]) + 1)
    e.tensor_tensor(K.act[:, PLACE[n], :], K.silu[:, n % 2, :], bank(K, U_BANK[n % 2]), ALU.mult).then_inc(s["act"], 1)


def lo_dve(K, f, c, n):
    e, s = K.nc.vector, K.FF[f]
    e.wait_ge(s["hi"], T(K, c, n) + 1)
    e.tensor_tensor(K.act_l[:, PLACE[n], :], K.act[:, PLACE[n], :], K.act_h[:, PLACE[n], :].bitcast(F32),
                    ALU.subtract).then_inc(s["lo"], 1)


def yev_dve(K, f, c, first=False):
    e, s = K.nc.vector, K.FF[f]
    e.wait_ge(s["down"], T(K, c, NT - 1) + 1)
    if not first:
        e.wait_ge(s["ytr"], c)
    e.tensor_scalar(K.yt[:, :], bank(K, Y_BANK), 0.5, None, ALU.mult).then_inc(s["yev"], 1)


def xup_dve(K, f, c):
    e, s = K.nc.vector, K.FF[f]
    e.wait_ge(s["ytr"], c + 1)
    xc = K.x[:, at(c * TPC, TPC), :]
    e.tensor_tensor(xc, xc, bank(K, N_BANK).rearrange("p (t e) -> p t e", e=EMB), ALU.add)\
     .then_inc(s["out"], 1)


def ffn_dve(K, f):
    def after(c, n):
        if n == 3:
            yev_dve(K, f, c)
        if n == 5:
            xup_dve(K, f, c)
        if f == 0:
            if n == 6:
                K.nc.vector.wait_ge(K.FF[0]["out"], c + 1)
                alone(K, K.nc.vector)
                norm_stats_dve(K, 1, c)
            if n == 9:
                norm_z_dve(K, 1, c)
            if n == 12:
                norm_lo_dve(K, 1, c)

    def body(c, before):
        for n in range(NT):
            if before is not None:
                after(before, n)
            if n >= 2:
                lo_dve(K, f, c, n - 2)
            elif before is not None:
                lo_dve(K, f, before, n + NT - 2)
            act_dve(K, f, c, n, before is None)
    body(0, None)
    with K.nc.vector.Fori(1, NCH) as c:
        body(c, c - 1)
    for n in range(NT - 2, NT):
        lo_dve(K, f, NCH - 1, n)
    for n in range(NT):
        after(NCH - 1, n)


def ffn_pool(K, f):
    e, s = K.nc.gpsimd, K.FF[f]

    def body(c, before):
        for n in range(NT):
            if before is not None and n == 8 and f == 0:
                norm_rstd_pool(K, 1, before)
            if n < FIRST_ROUTED:
                continue
            slot = SLOT_OF[n]
            e.wait_ge(s["act"], T(K, c, n) + 1)
            if n == FIRST_ROUTED or SLOT_OF[n - 1] != slot:
                e.wait_ge(K.slot_sems[slot], slot_base(K, f, slot) + 16 * len(SLOT_LOADS[slot]) * (c + 1))
            e.tensor_tensor(K.act[:, PLACE[n], :], K.act[:, PLACE[n], :], K.w_slots[:, slot, :], ALU.mult)\
             .then_inc(s["route"], 1)
    body(0, None)
    with e.Fori(1, NCH) as c:
        body(c, c - 1)
    if f == 0:
        norm_rstd_pool(K, 1, NCH - 1)


def ffn_sp(K, f):
    e, s = K.nc.sync, K.FF[f]
    order = sorted(range(len(SLOT_LOADS)), key=lambda n: SLOT_END[n])
    for n in order:
        slot_load(K, f, 0, n)
    with e.Fori(1, NCH) as c:
        for n in order:
            e.wait_ge(s["route"], (c - 1) * NROUTED + (SLOT_END[n] - FIRST_ROUTED + 1))
            slot_load(K, f, c, n)
        if f == 1:
            store_out(K, c - 1)
    if f == 1:
        store_out(K, NCH - 1)
        e.wait_ge(K.ld["out"], 16 * NCH)


def store_out(K, c):
    K.nc.sync.wait_ge(K.FF[1]["out"], c + 1)
    K.nc.sync.dma_start(K.out_tiles[:, at(c * TPC, TPC), :], K.x[:, at(c * TPC, TPC), :])\
      .then_inc(K.ld["out"], 16)



def start_sp(K):
    e = K.nc.sync
    for b in range(BATCH):
        e.dma_start(K.x[:, b * KT:(b + 1) * KT, :], K.tokens[b].rearrange("(t p) e -> p t e", p=P)).then_inc(K.ld_x[b], 16)
    r0 = HID // P * P
    rg_rows, ru_rows = (w.rearrange("e i h -> (e i) h") for w in (K.gate_r, K.up_r))
    for w, shared, routed in (("g", K.gate_s, rg_rows), ("u", K.up_s, ru_rows)):
        dst = K.nat[w][:, :].rearrange("p (n h) -> p n h", h=EMB)
        head = (HID // P + 1) * P - HID
        e.dma_start(dst[:, 0:HID // P, :], shared[0:r0, :].rearrange("(n p) h -> p n h", p=P))\
         .then_inc(K.ld["nat"], 16)
        e.dma_start(dst[0:HID - r0, HID // P, :], shared[r0:HID, :]).then_inc(K.ld["nat"], 16)
        e.dma_start(dst[HID - r0:P, HID // P, :], routed[0:head, :]).then_inc(K.ld["nat"], 16)
        e.dma_start(dst[:, HID // P + 1:, :], routed[head:, :].rearrange("(n p) h -> p n h", p=P))\
         .then_inc(K.ld["nat"], 16)
    e.dma_start(K.nat["d"][:, 0:HID], K.down_s).then_inc(K.ld["nat"], 16)
    e.dma_start(K.nat["d"][:, HID:].rearrange("p (e i) -> p e i", i=HID), K.down_r.rearrange("e h i -> h e i"))\
     .then_inc(K.ld["nat"], 16)
    e.wait_ge(K.consts, N_CONST)
    def many(src, n):
        return src[:, :].unsqueeze(1).to_broadcast([32, n * SEQ // CHUNK, CHUNK])
    def rows(dram, a, b):
        return dram[:, a:b, :].rearrange("g r (s t) -> g (r s) t", t=CHUNK)
    e.dma_start(rows(K.q_dram, 0, 8), many(K.rows0, 8)).then_inc(K.ld["const"], 16)
    e.dma_start(rows(K.k_dram, 0, 2), many(K.rows1, 2)).then_inc(K.ld["const"], 16)
    e.dma_start(rows(K.k_dram, 2, 8), many(K.rows0, 6)).then_inc(K.ld["const"], 16)


def start_act(K):
    e = K.nc.scalar
    e.dma_start(K.nat_attn[:, :], K.attn_w).then_inc(K.ld["small"], 16)
    e.dma_start(K.nat_proj[:, :], K.proj_w).then_inc(K.ld["small"], 16)
    e.wait_ge(K.padded, 2)
    e.dma_start(K.nat_route[0:ROUTED, :], K.route_w).then_inc(K.ld["small"], 16)
    e.dma_start(K.b_q[:, :], K.attn_b[0:EMB].rearrange("(p a) -> p a", a=1)).then_inc(K.ld["small"], 16)
    e.dma_start(K.b_k[:, :], K.attn_b[EMB:2 * EMB].rearrange("(p a) -> p a", a=1)).then_inc(K.ld["small"], 16)
    e.dma_start(K.b_v[:, :], K.attn_b[2 * EMB:3 * EMB].partition_broadcast(P)).then_inc(K.ld["small"], 16)
    e.dma_start(K.b_p[:, :], K.proj_b.partition_broadcast(P)).then_inc(K.ld["small"], 16)
    e.dma_start(K.rb_row[:, 0:ROUTED], K.route_b.partition_broadcast(P)).then_inc(K.ld["small"], 16)


def start_pool(K):
    e = K.nc.gpsimd
    e.memset(K.nat_route[:, :], 0.0).then_inc(K.padded, 1)
    e.memset(K.rb_row[:, :], MASKED).then_inc(K.padded, 1)
    e.memset(K.ident[:, :], 0.0).then_inc(K.blank, 1)
    e.memset(K.mask_b[:, :], 0.0).then_inc(K.blank, 1)
    e.iota(K.rank_i[:, :], pattern=[[-1, NGATE]], base=NGATE, channel_multiplier=0).then_inc(K.blank, 1)
    e.wait_ge(K.blank, 3)
    e.affine_select(out=K.ident[:, :], in_=K.ident[:, :], compare_op=ALU.not_equal, fill=1.0, base=0,
                    pattern=[[-1, P]], channel_multiplier=1).then_inc(K.blank, 1)
    e.wait_ge(K.blank, 4)
    e.tensor_copy(K.ident_b[:, :], K.ident[:, :]).then_inc(K.consts, 1)
    e.affine_select(out=K.mask_b[:, :], in_=K.mask_b[:, :], compare_op=ALU.is_ge, fill=MASKED, base=0,
                    pattern=[[1, P]], channel_multiplier=-1).then_inc(K.consts, 1)
    e.memset(K.rows0[:, :], 0.0).then_inc(K.consts, 1)
    e.memset(K.rows1[:, :], 1.0).then_inc(K.consts, 1)
    e.memset(K.half_neg[:, :], -0.5).then_inc(K.consts, 1)
    e.tensor_copy(K.rank[:, :], K.rank_i[:, :]).then_inc(K.consts, 1)
    e.memset(K.shared_rows, 1.0).then_inc(K.consts, 1)


def clear_pool(K):
    e = K.nc.gpsimd
    e.wait_ge(K.tp_pe, len(TP_GROUPS))
    e.wait_ge(K.sw_lo, 5)
    e.wait_ge(K.ld["const"], 16 * N_CONST_DMA)
    for u in range(3):
        e.memset(K.keys[u][:, :, :].bitcast(F32), 0.0).then_inc(K.cleared, 1)


def weights_small_pe(K):
    e = K.nc.tensor
    e.wait_ge(K.ld["small"], 16 * N_SMALL)
    e.wait_ge(K.consts, N_CONST)
    e.transpose(bank(K, 7)[:, 0:P], K.nat_attn[:, EMB:2 * EMB], K.ident[:, :])
    e.transpose(bank(K, 7)[:, P:2 * P], K.nat_route[:, :], K.ident[:, :]).then_inc(K.A["init"], 1)


def weights_pe(K, m):
    e, (w, n0, k) = K.nc.tensor, TP_GROUPS[m]
    if w == "g" and n0 == 0:
        e.wait_ge(K.ld["nat"], 16 * 10)
    if m >= 4:
        e.wait_ge(K.tp_lo, m - 3)
    for t in range(k):
        ins = e.transpose(bank(K, TP_BANKS[m % 4])[:, t * P:(t + 1) * P],
                          K.nat[w][:, (n0 + t) * P:(n0 + t + 1) * P], K.ident[:, :])
    ins.then_inc(K.tp_pe, 1)


def weights_act(K):
    e = K.nc.scalar
    e.wait_ge(K.ld["small"], 16 * N_SMALL)
    e.copy(K.small["qh"][:, :], K.nat_attn[:, 0:EMB]).then_inc(K.sw_hi, 1)
    e.copy(K.small["vh"][:, :], K.nat_attn[:, 2 * EMB:]).then_inc(K.sw_hi, 1)
    e.copy(K.small["ph"][:, :], K.nat_proj[:, :]).then_inc(K.sw_hi, 1)
    e.wait_ge(K.A["init"], 1)
    e.copy(K.small["kh"][:, :], bank(K, 7)[:, 0:P]).then_inc(K.sw_hi, 1)
    e.copy(K.rw_h[:, :], bank(K, 7)[:, P:P + NGATE]).then_inc(K.sw_hi, 1)


def weights_hi_act(K, m):
    w, n0, k = TP_GROUPS[m]
    K.nc.scalar.wait_ge(K.tp_pe, m + 1)
    K.nc.scalar.copy(K.wide[w + "h"][:, n0 * P:(n0 + k) * P], bank(K, TP_BANKS[m % 4])[:, 0:k * P]).then_inc(K.tp_hi, 1)


def weights_small_dve(K):
    e = K.nc.vector
    for n, (w, src) in enumerate((("q", K.nat_attn[:, 0:EMB]), ("v", K.nat_attn[:, 2 * EMB:]),
                                  ("p", K.nat_proj[:, :]), ("k", bank(K, 7)[:, 0:P]))):
        e.wait_ge(K.sw_hi, 5)
        e.tensor_tensor(K.small[w + "l"][:, :], src, K.small[w + "h"][:, :].bitcast(F32), ALU.subtract)\
         .then_inc(K.sw_lo, 1)
    e.tensor_tensor(K.rw_l[:, :], bank(K, 7)[:, P:P + NGATE], K.rw_h[:, :].bitcast(F32), ALU.subtract)\
     .then_inc(K.sw_lo, 1)


def weights_lo_dve(K, m):
    w, n0, k = TP_GROUPS[m]
    K.nc.vector.wait_ge(K.tp_hi, m + 1)
    cols = slice(n0 * P, (n0 + k) * P)
    K.nc.vector.tensor_tensor(K.wide[w + "l"][:, cols], bank(K, TP_BANKS[m % 4])[:, 0:k * P],
                            K.wide[w + "h"][:, cols].bitcast(F32), ALU.subtract).then_inc(K.tp_lo, 1)


def three(K, e, dst, left, right):
    e.matmul(dst, left[0], right[0], start=True, stop=False)
    e.matmul(dst, left[0], right[1], start=False, stop=False)
    return e.matmul(dst, left[1], right[0], start=False, stop=True)


def qkv_pe(K):
    e = K.nc.tensor
    for c in range(NCH):
        u, cols = c % 2, slice(c * CHUNK, (c + 1) * CHUNK)
        e.wait_ge(K.NS[1]["lo"], c + 1)
        if c >= 2:
            e.wait_ge(K.A["q1f"], c - 1)
        three(K, e, bank(K, 0 + u), (K.small["qh"][:, :], K.small["ql"][:, :]), (K.zt_h[:, cols], K.zt_l[:, cols]))\
            .then_inc(K.A["q1"], 1)
        if c >= 2:
            e.wait_ge(K.A["vev"], c - 1)
        for t in range(TPC):
            tc = slice(c * CHUNK + t * P, c * CHUNK + (t + 1) * P)
            ins = three(K, e, bank(K, 4 + u)[:, t * P:(t + 1) * P], (K.zt_h[:, tc], K.zt_l[:, tc]),
                        (K.small["vh"][:, :], K.small["vl"][:, :]))
        ins.then_inc(K.A["v"], 1)
        e.wait_ge(K.A["q1l"], c + 1)
        if c >= 2:
            e.wait_ge(K.A["qf"], c - 1)
        three(K, e, bank(K, 2 + u), (K.small["kh"][:, :], K.small["kl"][:, :]), (K.q1_h[:, u, :], K.q1_l[:, u, :]))\
            .then_inc(K.A["q"], 1)


def qkv_act(K):
    e = K.nc.scalar
    for c in range(NCH):
        u = c % 2
        e.wait_ge(K.A["q1"], c + 1)
        if c >= 2:
            e.wait_ge(K.A["q"], c - 1)
        e.activation(K.q1_f[:, u, :], bank(K, 0 + u), ACT.Identity, bias=K.b_q[:, 0:1]).then_inc(K.A["q1f"], 1)
        e.wait_ge(K.A["q1f"], c + 1)
        e.copy(K.q1_h[:, u, :], K.q1_f[:, u, :]).then_inc(K.A["q1h"], 1)
        e.wait_ge(K.A["q"], c + 1)
        if c >= 2:
            e.wait_ge(K.A["ql"], c - 1)
            e.wait_ge(K.q_st[c - 2], 16 * 3)
        e.activation(K.q_f[:, u, :], bank(K, 2 + u), ACT.Identity, bias=K.b_k[:, 0:1]).then_inc(K.A["qf"], 1)
        e.wait_ge(K.A["qf"], c + 1)
        e.copy(K.q_h[:, u, :], K.q_f[:, u, :]).then_inc(K.A["qh"], 1)


def qkv_dve(K):
    e = K.nc.vector
    for c in range(NCH):
        u, b, half = c % 2, c // 2, c % 2
        e.wait_ge(K.A["q1h"], c + 1)
        e.tensor_tensor(K.q1_l[:, u, :], K.q1_f[:, u, :], K.q1_h[:, u, :].bitcast(F32), ALU.subtract)\
         .then_inc(K.A["q1l"], 1)
        e.wait_ge(K.A["v"], c + 1)
        dst = K.v_all[:, b * GPB:(b + 1) * GPB, half * TPC:(half + 1) * TPC, :].rearrange("p g t m -> p t g m")
        src = bank(K, 4 + u).rearrange("p (t g m) -> p t g m", g=GPB, m=32)
        bias = K.b_v[:, :].rearrange("p (g m) -> p g m", m=32)
        for t in range(TPC):
            ins = e.tensor_tensor(dst[:, t], src[:, t], bias, ALU.add)
        ins.then_inc(K.A["vev"], 1)
        e.wait_ge(K.A["qh"], c + 1)
        e.tensor_tensor(K.q_l[:, u, :], K.q_f[:, u, :], K.q_h[:, u, :].bitcast(F32), ALU.subtract)\
         .then_inc(K.A["ql"], 1)


def stack_store(K, dram, part, c, src, s):
    b, half = c // 2, c % 2
    dst = dram[b * HEADS:(b + 1) * HEADS, 8 + 8 * part:16 + 8 * part, half * CHUNK:(half + 1) * CHUNK]
    K.nc.sync.dma_start(dst, src.bitcast(F32)).then_inc(s, 16)


def qkv_sp(K):
    e = K.nc.sync
    for c in range(NCH):
        u, cols = c % 2, slice(c * CHUNK, (c + 1) * CHUNK)
        e.wait_ge(K.NS[1]["lo"], c + 1)
        stack_store(K, K.k_dram, 0, c, K.zt_h[:, cols], K.k_st[c])
        stack_store(K, K.k_dram, 1, c, K.zt_l[:, cols], K.k_st[c])
        stack_store(K, K.k_dram, 2, c, K.zt_h[:, cols], K.k_st[c])
        e.wait_ge(K.A["ql"], c + 1)
        stack_store(K, K.q_dram, 0, c, K.q_h[:, u, :], K.q_st[c])
        stack_store(K, K.q_dram, 1, c, K.q_h[:, u, :], K.q_st[c])
        stack_store(K, K.q_dram, 2, c, K.q_l[:, u, :], K.q_st[c])


def m_unit_pe(K, n, r_bank, u):
    e = K.nc.tensor
    pieces, j = MAX_BANKS[n // 4], n % 4
    dst = bank(K, r_bank)
    for m, (i, k0, nb, at0, diag) in enumerate(pieces):
        ins = e.matmul(dst[:, at0 * P:(at0 + nb) * P], K.queries[u][:, i * P:(i + 1) * P],
                       K.keys[u][:, j, k0 * P:(k0 + nb) * P], start=(m == 0), stop=True, skip_group_check=True)
    for i, k0, nb, at0, diag in pieces:
        if diag:
            last = (at0 + nb - 1) * P
            ins = e.matmul(dst[:, last:last + P], K.mask_b[:, :], K.ident_b[:, :], start=False, stop=True,
                           skip_group_check=True)
    return ins


def ring_pe(K, what, d, n, p, u, r, r_bank, start=False):
    e, v = K.nc.tensor, (u + d) % 3
    if not start:
        e.wait_ge(K.A["taken"], r - 1)
    if what == "max":
        if n == 0:
            e.wait_ge(K.ld_k[v], 80 * loads(p, u, d))
        ins = m_unit_pe(K, n, r_bank, v)
    elif what == "mrow":
        e.wait_ge(K.A["mm"], count(p, u, 1, d + 2))
        ins = e.transpose(bank(K, r_bank)[0:32, 0:P],
                          K.mm_hl[:, 2 * n:2 * n + 2, :, :].bitcast(F32).rearrange("p j a i -> p (j a i)"), K.ident[:, :])
    else:
        e.wait_ge(K.A["oev"], count(p, u, 2, 2 * d + n + 2))
        for t in range(4):
            ins = e.transpose(bank(K, r_bank)[:, t * P:(t + 1) * P], K.ot[:, n, t * P:(t + 1) * P], K.ident[:, :])
    ins.then_inc(K.A["ring"], 1)


def unit_pe(K, p, u, d, n, start=False):
    e = K.nc.tensor
    kt, heads = UNITS[n]
    v = (u + d) % 3
    if not start:
        e.wait_ge(K.A["ex"], count(p, u, NU, d * NU + n - 1))
    if n == 0:
        e.wait_ge(K.ld_r[v], 64 * loads(p, u, d))
    slot = SLOTS[n % 2]
    for m, j in enumerate(heads):
        for half in range(2):
            q0, q1 = max(kt * P, half * CHUNK), (half + 1) * CHUNK
            if q0 < q1:
                b = slot + (m if len(heads) > 1 else half)
                ins = e.matmul(bank(K, b)[:, q0 - half * CHUNK:CHUNK], K.keys[v][:, j, kt * P:(kt + 1) * P],
                               K.queries[v][:, q0:q1], start=True, stop=True)
    ins.then_inc(K.A["sp"], 1)


def pv_pe(K, p, u, kt, half):
    e = K.nc.tensor
    if half == kt // 4:
        e.wait_ge(K.A["mk"], count(p, u, KT, kt + 1))
    else:
        e.wait_ge(K.A["ex"], count(p, u, NU, FIRST_UNIT[kt + 1]))
    if kt == 0:
        e.wait_ge(K.A["vg"], count(p, u, 1, 1))
        e.wait_ge(K.A["oev"], count(p, u, 2, 1))
    q0, q1 = max(kt * P, half * CHUNK), (half + 1) * CHUNK
    for j in range(4):
        ins = e.matmul(bank(K, O_BANK[half])[32 * j:32 * j + 32, q0 - half * CHUNK:CHUNK],
                       K.vg[:, kt, j, :], K.probs[:, kt % 2, j, q0:q1],
                       start=(kt == 0), stop=(kt == 4 * half + 3), skip_group_check=True)
    if half == kt // 4:
        ins.then_inc(K.A["pv"], 1)


def pe_body(K, p, u, kind):
    ring, took = RINGS[kind], 0
    for step, order in enumerate(ORDERS[kind]):
        d, kt = (0, step + 1) if step + 1 < KT else (1, 0)
        units = list(range(FIRST_UNIT[kt], FIRST_UNIT[kt + 1])) if d == 0 or kind != LAST else []
        for what in order:
            if what == "U":
                unit_pe(K, p, u, d, units.pop(0))
            elif what == "R":
                kind_of, dd, n = ring[took]
                number = count(p, u, RINGN, RING0[kind] + took)
                ring_pe(K, kind_of, dd, n, p, u, number, RING[(u * RINGN + RING0[kind] + took) % 2])
                took += 1
            else:
                pv_pe(K, p, u, step, 1 if what == "a" else 0)
        assert not units
    assert took == len(ring)


def attn_pe(K):
    e = K.nc.tensor
    for r, (what, d, n) in enumerate(RING_PROLOGUE):
        ring_pe(K, what, d, n, 0, 0, r, RING[r % 2], start=r < 2)
    e.sem_inc(K.A["pv"], 1)
    for n in range(FIRST_UNIT[1]):
        unit_pe(K, 0, 0, 0, n, start=n < 2)
    with e.Fori(0, LOOP3) as p:
        for u in range(3):
            pe_body(K, p, u, LOOP)
    pe_body(K, LOOP3, 0, LAST_BUT_ONE)
    pe_body(K, LOOP3, 1, LAST)
    ring_pe(K, "out", -1, 1, GROUPS // 3, GROUPS % 3, RING_END, RING[RING_END % 2])


def ring_dve(K, what, d, n, p, u, r, r_bank, start=False):
    e = K.nc.vector
    e.wait_ge(K.A["ring"], r + 1)
    if what == "max":
        if n == 0:
            e.wait_ge(K.A["nm"], count(p, u, KT + 1, (KT + 1) * d))
        b, j = n // 4, n % 4
        e.tensor_reduce(K.mxp[:, j, 4 * b:4 * b + 4], bank(K, r_bank).rearrange("p (m k) -> p m k", k=P),
                        AX.X, ALU.max).then_inc(K.A["taken"], 1)
        if n == NMAX - 1:
            e.wait_ge(K.A["taken"], r + 1)
            e.wait_ge(K.A["mm"], count(p, u, 1, d + 1))
            for i, (lo, hi) in sorted(max_slots().items()):
                e.tensor_reduce(K.nmax[:, :, i:i + 1], K.mxp[:, :, lo:hi], AX.X, ALU.max, negate=True)\
                 .then_inc(K.A["nm"], 1)
            e.wait_ge(K.A["nm"], count(p, u, KT + 1, (KT + 1) * d + KT))
            e.tensor_copy(K.mm_hl[:, 0:4, 0, :], K.nmax[:, :, :]).then_inc(K.A["nm"], 1)
            e.wait_ge(K.A["nm"], count(p, u, KT + 1, (KT + 1) * (d + 1)))
            e.tensor_tensor(K.mm_hl[:, 0:4, 1, :], K.nmax[:, :, :], K.mm_hl[:, 0:4, 0, :].bitcast(F32),
                            ALU.subtract).then_inc(K.A["mm"], 1)
    elif what == "mrow":
        if not start:
            e.wait_ge(K.ld_r[(u + d - 1) % 3], 64 * loads(p, u, d - 1))
        e.tensor_copy(K.m_rows[32 * n:32 * n + 32, :], bank(K, r_bank)[0:32, 0:P]).then_inc(K.A["taken"], 1)
    else:
        b = bank(K, r_bank).rearrange("p (m c) -> p m c", c=32)
        e.wait_ge(K.A["taken"], r)
        e.reciprocal(K.rsum[:, :, :], b[:, :, HDIM:HDIM + 1]).then_inc(K.A["rs"], 1)
        e.wait_ge(K.A["rs"], count(p, u, 2, 2 * d + n + 2))
        dst = K.o_all[:, at(count(p, u, 1, d + 1), 1), 4 * n:4 * n + 4, :].rearrange("p g t (j c) -> p (g t j) c", c=HDIM)
        e.tensor_tensor(dst, b[:, :, 0:HDIM], K.rsum[:, :, :].to_broadcast([P, 16, HDIM]), ALU.mult)\
         .then_inc(K.A["taken"], 1)


def dve_body(K, p, u, kind):
    for k, (what, d, n) in enumerate(RINGS[kind]):
        number = count(p, u, RINGN, RING0[kind] + k)
        ring_dve(K, what, d, n, p, u, number, RING[(u * RINGN + RING0[kind] + k) % 2])


def attn_dve(K):
    e = K.nc.vector
    e.memset(K.mm_hl[:, :, :, :].bitcast(F32), 0.0).then_inc(K.A["mm"], 1)
    for r, (what, d, n) in enumerate(RING_PROLOGUE):
        ring_dve(K, what, d, n, 0, 0, r, RING[r % 2], start=True)
    with e.Fori(0, LOOP3) as p:
        for u in range(3):
            dve_body(K, p, u, LOOP)
    dve_body(K, LOOP3, 0, LAST_BUT_ONE)
    dve_body(K, LOOP3, 1, LAST)
    ring_dve(K, "out", -1, 1, GROUPS // 3, GROUPS % 3, RING_END, RING[RING_END % 2])


def unit_act(K, p, u, d, n, start=False):
    e = K.nc.scalar
    kt, heads = UNITS[n]
    e.wait_ge(K.A["sp"], count(p, u, NU, d * NU + n + 1))
    if n == FIRST_UNIT[kt] and not start:
        e.wait_ge(K.A["pv"], count(p, u, KT, d * KT + kt))
    q0 = kt * P
    if len(heads) == 1:
        src = K.psum[:, SLOTS[n % 2]:SLOTS[n % 2] + 2, :].rearrange("p b c -> p (b c)")[:, q0:SEQ]
        dst = K.probs[:, kt % 2, heads[0], q0:SEQ]
    else:
        src = K.psum[:, SLOTS[n % 2]:SLOTS[n % 2] + 2, q0 - CHUNK:CHUNK]
        dst = K.probs[:, kt % 2, heads[0]:heads[1] + 1, q0:SEQ]
    e.activation(dst, src, ACT.Exp, scale=SCALE).then_inc(K.A["ex"], 1)


def oev_act(K, p, u, kind, half):
    e = K.nc.scalar
    e.wait_ge(K.A["pv"], count(p, u, KT, 4 * half + 5))
    if half == 0:
        at0 = RINGS[LAST_BUT_ONE if kind == LAST else LOOP].index(("out", 0, 0)) + RING0[LOOP] - RINGN
    else:
        at0 = RINGS[kind].index(("out", -1, 1)) + RING0[kind]
    e.wait_ge(K.A["ring"], count(p, u, RINGN, at0 + 1))
    e.copy(K.ot[:, half, :], bank(K, O_BANK[half])).then_inc(K.A["oev"], 1)


def act_body(K, p, u, kind):
    for step in range(KT):
        d, kt = (0, step + 1) if step + 1 < KT else (1, 0)
        if d == 0 or kind != LAST:
            for n in range(FIRST_UNIT[kt], FIRST_UNIT[kt + 1]):
                unit_act(K, p, u, d, n)
        if step == 4:
            oev_act(K, p, u, kind, 0)
    oev_act(K, p, u, kind, 1)


def attn_act(K):
    e = K.nc.scalar
    e.wait_ge(K.A["ready"], 1)
    e.sem_inc(K.A["oev"], 1)
    for n in range(FIRST_UNIT[1]):
        unit_act(K, 0, 0, 0, n, start=True)
    with e.Fori(0, LOOP3) as p:
        for u in range(3):
            act_body(K, p, u, LOOP)
    act_body(K, LOOP3, 0, LAST_BUT_ONE)
    act_body(K, LOOP3, 1, LAST)


def mask_pool(K, p, u, kt):
    e = K.nc.gpsimd
    e.wait_ge(K.A["ex"], count(p, u, NU, FIRST_UNIT[kt + 1]))
    alone(K, e)
    blk = K.probs[:, kt % 2, :, kt * P:(kt + 1) * P]
    e.affine_select(out=blk, in_=blk, compare_op=ALU.is_ge, fill=0.0, base=0,
                    pattern=[[0, 4], [1, P]], channel_multiplier=-1).then_inc(K.A["mk"], 1)


def vg_pool(K, p, u, start=False):
    e = K.nc.gpsimd
    if not start:
        e.wait_ge(K.A["pv"], count(p, u, KT, 1))
    src = K.v_all[:, at(count(p, u, 1, 0), 1), :, :].rearrange("p g t (j c) -> p (g t j) c", c=HDIM)
    dst = K.vg[:, :, :, :].rearrange("p t j c -> p (t j) c")[:, :, 0:HDIM]
    e.tensor_copy(dst, src).then_inc(K.A["vg"], 1)


def pool_body(K, p, u):
    vg_pool(K, p, u)
    for kt in range(KT):
        mask_pool(K, p, u, kt)


def attn_pool(K):
    e = K.nc.gpsimd
    for c in range(NCH):
        e.wait_ge(K.q_st[c], 16 * 3)
    e.memset(K.vg[:, :, :, :], 0.0).then_inc(K.A["vi"], 1)
    e.memset(K.ot[:, :, :], 1.0).then_inc(K.A["ready"], 1)
    e.wait_ge(K.A["vi"], 1)
    e.memset(K.vg[:, :, :, HDIM:HDIM + 1], 1.0).then_inc(K.A["vi"], 1)
    e.wait_ge(K.A["vi"], 2)
    e.wait_ge(K.A["vev"], NCH)
    with e.Fori(0, LOOP3) as p:
        for u in range(3):
            pool_body(K, p, u)
    pool_body(K, LOOP3, 0)
    pool_body(K, LOOP3, 1)


def stack_load(K, p, u, d):
    v, row = (u + d) % 3, count(p, u, 4, 4 * d)
    K.nc.sync.dma_start(K.queries[v][:, :].bitcast(F32), K.q_dram[at(row, 4)].rearrange("g r t -> (g r) t"))\
     .then_inc(K.ld_k[v], 16)
    for j in range(4):
        K.nc.sync.dma_start(K.keys[v][32 * j:32 * j + 32, j, :].bitcast(F32),
                            K.k_dram[at(row + j, 1)].rearrange("g r t -> (g r) t")).then_inc(K.ld_k[v], 16)


def rows_load(K, p, u, d, r):
    e, v = K.nc.sync, (u + d) % 3
    e.wait_ge(K.ld_k[v], 80 * loads(p, u, d))
    alone(K, e)
    for j in range(4):
        if j % 2 == 0:
            e.wait_ge(K.A["taken"], r + (j // 2 + 1))
        dst = K.queries[v][32 * j:32 * j + 2, :].bitcast(F32).rearrange("p (i q) -> p i q", q=P)
        e.dma_start(dst, K.m_rows[2 * KT * j:2 * KT * (j + 1), :].bitcast(F32)).then_inc(K.ld_r[v], 16)


def sp_body(K, p, u, kind):
    if kind == LOOP:
        K.nc.sync.wait_ge(K.A["sp"], count(p, u, NU, 1))
        stack_load(K, p, u, 2)
    rows_load(K, p, u, 1, count(p, u, RINGN, RING0[kind] + RINGS[kind].index(("mrow", 1, 0))))


def attn_sp(K):
    e = K.nc.sync
    for c in range(NCH // 2):
        e.wait_ge(K.k_st[c], 16 * 3)
        e.wait_ge(K.q_st[c], 16 * 3)
    e.wait_ge(K.ld["const"], 16 * N_CONST_DMA)
    e.wait_ge(K.cleared, 3)
    stack_load(K, 0, 0, 0)
    stack_load(K, 0, 0, 1)
    for c in range(NCH // 2, NCH):
        e.wait_ge(K.k_st[c], 16 * 3)
        e.wait_ge(K.q_st[c], 16 * 3)
    rows_load(K, 0, 0, 0, RING_PROLOGUE.index(("mrow", 0, 0)))
    with e.Fori(0, LOOP3) as p:
        for u in range(3):
            sp_body(K, p, u, LOOP)
    sp_body(K, LOOP3, 0, LAST_BUT_ONE)


def proj_tr_pe(K, c):
    e, u = K.nc.tensor, c % 2
    if c >= 2:
        e.wait_ge(K.A["ol"], c - 1)
    e.wait_ge(K.A["og"], c + 1)
    for t in range(TPC):
        ins = e.transpose(bank(K, 0 + u)[:, t * P:(t + 1) * P], K.ao_f[:, u, t * P:(t + 1) * P], K.ident[:, :])
    ins.then_inc(K.A["otr"], 1)


def proj_mm(K, c):
    e, u = K.nc.tensor, c % 2
    e.wait_ge(K.A["ol"], c + 1)
    if c >= 2:
        e.wait_ge(K.A["xup"], 2 * (c - 1))
    for t in range(TPC):
        tc = slice(t * P, (t + 1) * P)
        ins = three(K, e, bank(K, 2 + u)[:, tc], (K.ao_h[:, u, tc], K.ao_l[:, u, tc]), (K.small["ph"][:, :], K.small["pl"][:, :]))
    ins.then_inc(K.A["op"], 1)


def gather_act(K, c):
    e, b, u = K.nc.scalar, c // 2, c % 2
    if c == 0:
        e.wait_ge(K.A["taken"], RING_END + 1)
    if c >= 2:
        e.wait_ge(K.A["otr"], c - 1)
    src = K.o_all[:, 1 + b * GPB:1 + (b + 1) * GPB, TPC * (c % 2):TPC * (c % 2) + TPC, :]
    e.copy(K.ao_f[:, u, :].rearrange("p (t g m) -> p g t m", g=GPB, m=32), src).then_inc(K.A["og"], 1)


def proj_act(K, c):
    e, u = K.nc.scalar, c % 2
    e.wait_ge(K.A["otr"], c + 1)
    if c >= 2:
        e.wait_ge(K.A["op"], c - 1)
    e.copy(K.ao_h[:, u, :], bank(K, 0 + u)).then_inc(K.A["oh"], 1)


def proj_lo_dve(K, c):
    e, u = K.nc.vector, c % 2
    e.wait_ge(K.A["oh"], c + 1)
    e.tensor_tensor(K.ao_l[:, u, :], bank(K, 0 + u), K.ao_h[:, u, :].bitcast(F32), ALU.subtract).then_inc(K.A["ol"], 1)


def proj_x_dve(K, c):
    e, u = K.nc.vector, c % 2
    e.wait_ge(K.A["op"], c + 1)
    xc = K.x[:, c * TPC:(c + 1) * TPC, :]
    e.tensor_tensor(xc, xc, bank(K, 2 + u).rearrange("p (t e) -> p t e", e=EMB), ALU.add).then_inc(K.A["xup"], 1)
    e.wait_ge(K.A["xup"], 2 * c + 1)
    e.tensor_tensor(xc, xc, K.b_p[:, :].unsqueeze(1).to_broadcast([P, TPC, EMB]), ALU.add).then_inc(K.A["xup"], 1)


def build(nc, tokens, attn_w, attn_b, proj_w, proj_b, gate_s, up_s, down_s, gate_r, up_r, down_r,
          route_w, route_b, result):
    K = Chip()
    K.nc, K.tokens, K.result = nc, tokens, result
    K.attn_w, K.attn_b, K.proj_w, K.proj_b = attn_w, attn_b, proj_w, proj_b
    K.gate_s, K.up_s, K.down_s = gate_s, up_s, down_s
    K.gate_r, K.up_r, K.down_r = gate_r, up_r, down_r
    K.route_w, K.route_b = route_w, route_b
    with ExitStack() as ctx:
        place_memory(K, ctx)

        block = ctx.enter_context(K.nc.Block())

        @block.sync
        def _(e):
            start_sp(K)
            router_sp(K, 0)
            ffn_sp(K, 0)
            qkv_sp(K)
            attn_sp(K)
            router_sp(K, 1)
            ffn_sp(K, 1)

        @block.tensor
        def _(e):
            weights_small_pe(K)
            for c in range(NCH + 1):
                if c < NCH:
                    norm_tr_pe(K, 0, c)
                if c:
                    logits_pe(K, 0, 0, c - 1)
            for m in range(len(TP_BANKS)):
                weights_pe(K, m)
            route_tr_pe(K, 0)
            for m in range(len(TP_BANKS), len(TP_GROUPS)):
                weights_pe(K, m)
            e.wait_ge(K.tp_lo, len(TP_GROUPS))
            ffn_pe(K, 0)
            qkv_pe(K)
            attn_pe(K)
            for c in range(NCH + 3):
                if c < NCH:
                    proj_tr_pe(K, c)
                if 0 <= c - 1 < NCH:
                    proj_mm(K, c - 1)
                if 0 <= c - 2 < NCH:
                    norm_tr_pe(K, 2, c - 2)
                if 0 <= c - 3 < NCH:
                    logits_pe(K, 1, 2, c - 3)
            ffn_pe(K, 1)

        @block.scalar
        def _(e):
            start_act(K)
            weights_act(K)
            for c in range(NCH):
                norm_hi_act(K, 0, c)
            router_act(K, 0)
            for m in range(len(TP_GROUPS)):
                weights_hi_act(K, m)
            ffn_act(K, 0)
            qkv_act(K)
            attn_act(K)
            gather_act(K, 0)
            for c in range(NCH + 2):
                if c + 1 < NCH:
                    gather_act(K, c + 1)
                if c < NCH:
                    proj_act(K, c)
                if c >= 2:
                    norm_hi_act(K, 2, c - 2)
            router_act(K, 1)
            ffn_act(K, 1)

        @block.gpsimd
        def _(e):
            start_pool(K)
            for c in range(NCH):
                norm_rstd_pool(K, 0, c)
            clear_pool(K)
            ffn_pool(K, 0)
            attn_pool(K)
            for c in range(NCH):
                norm_rstd_pool(K, 2, c)
            e.wait_ge(K.NS[2]["lo"], 1)
            e.memset(K.shared_rows, 1.0).then_inc(K.ones, 1)
            e.wait_ge(K.ones, 1)
            ffn_pool(K, 1)

        @block.vector
        def _(e):
            weights_small_dve(K)
            for c in range(NCH + 2):
                if c < NCH:
                    e.wait_ge(K.ld_x[c // 2], 16)
                    norm_stats_dve(K, 0, c)
                if 0 <= c - 1 < NCH:
                    norm_z_dve(K, 0, c - 1)
                if c >= 2:
                    norm_lo_dve(K, 0, c - 2)
            router_dve(K, 0)
            for m in range(len(TP_GROUPS)):
                weights_lo_dve(K, m)
            ffn_dve(K, 0)
            qkv_dve(K)
            attn_dve(K)
            for c in range(NCH + 3):
                if c < NCH:
                    proj_lo_dve(K, c)
                if 0 <= c - 1 < NCH:
                    proj_x_dve(K, c - 1)
                    e.wait_ge(K.A["xup"], 2 * c)
                    norm_stats_dve(K, 2, c - 1)
                if 0 <= c - 2 < NCH:
                    norm_z_dve(K, 2, c - 2)
                if c >= 3:
                    norm_lo_dve(K, 2, c - 3)
            router_dve(K, 1)
            ffn_dve(K, 1)


_INS = ["attn_hidden_states", "attn_c_attn_w", "attn_c_attn_b", "attn_c_proj_w", "attn_c_proj_b",
        "ffn_sg", "ffn_su", "ffn_sd", "ffn_rg", "ffn_ru", "ffn_rd", "ffn_wr", "ffn_rb"]


def kernel(**inputs):
    import concourse.bacc as bacc
    from concourse.bass_utils import run_bass_kernel_spmd

    nc = bacc.Bacc("TRN2", target_bir_lowering=False, num_devices=1)
    arrays, args = {}, []
    for name in _INS:
        a = np.ascontiguousarray(inputs["L0_" + name])
        arrays["in_" + name] = a
        args.append(nc.dram_tensor("in_" + name, a.shape, mybir.dt.from_np(a.dtype), kind="ExternalInput").ap())
    out = nc.dram_tensor("out", (BATCH, SEQ, EMB), F32, kind="ExternalOutput").ap()
    build(nc, *args, out)
    r = run_bass_kernel_spmd(nc, [arrays], core_ids=[0])
    return r.results[0]["out"]
```

```python
from contextlib import ExitStack

import numpy as np

import concourse.bass as bass
from concourse import mybir

F32 = mybir.dt.float32
F32R = mybir.dt.float32r
BF16 = mybir.dt.bfloat16
ALU = mybir.AluOpType
ACT = mybir.ActivationFunctionType
AX = mybir.AxisListType

P = 128
BATCH, SEQ, EMB = 2, 1024, 128
HEADS, HDIM = 16, 8
TOKENS = BATCH * SEQ
TT = TOKENS // P
CHUNK = 512
NCH = TOKENS // CHUNK
TPC = CHUNK // P
HID, ROUTED = 352, 7
EXPERTS = ROUTED + 1
HROWS = HID * EXPERTS
NT = HROWS // P
LN_EPS = 1e-5
SCALE = 1.0 / float(np.sqrt(HDIM))
MASKED = -1e30
GROUPS = BATCH * HEADS // 4
GPB = GROUPS // BATCH
KT = SEQ // P
NGATE = 8


def at(start, n):
    return slice(start, start + n) if isinstance(start, int) else bass.ds(start, n)


def hidden_pieces():
    tiles = []
    for n in range(NT):
        r, runs = n * P, []
        while r < (n + 1) * P:
            e = r // HID
            end = min((n + 1) * P, (e + 1) * HID)
            runs.append((r - n * P, end - n * P, e))
            r = end
        tiles.append(runs)
    return tiles


def weight_slots():
    slots, loads, slot_of, end = {}, [], {}, []
    for n, runs in enumerate(hidden_pieces()):
        if all(e == 0 for _, _, e in runs):
            continue
        key = ("expert", runs[0][2]) if len(runs) == 1 else ("tile", n)
        if key not in slots:
            slots[key] = len(loads)
            loads.append([(a, b, e) for a, b, e in runs if e])
            end.append(n)
        slot_of[n] = slots[key]
        end[slots[key]] = n
    return slot_of, loads, end


SLOT_OF, SLOT_LOADS, SLOT_END = weight_slots()
FIRST_ROUTED = min(SLOT_OF)
NROUTED = NT - FIRST_ROUTED


PLACE = [0, 1, 2, 3] * 4 + [0, 1, 2] * 2
BACK = [3, 3, 3, 10] + [4] * 15 + [3] * 3
assert len(PLACE) == len(BACK) == NT


MAX_BANKS = [
    [(0, 0, 1, 0, True), (2, 0, 3, 1, True)],
    [(1, 0, 2, 0, True), (5, 4, 2, 2, True)],
    [(5, 0, 4, 0, False)],
    [(4, 0, 4, 0, False)],
    [(4, 4, 1, 0, True), (6, 4, 3, 1, True)],
    [(6, 0, 4, 0, False)],
    [(3, 0, 4, 0, True)],
    [(7, 0, 4, 0, False)],
    [(7, 4, 4, 0, True)],
]
NBANK = len(MAX_BANKS)
NMAX = 4 * NBANK


def max_slots():
    runs = {}
    for b, pieces in enumerate(MAX_BANKS):
        for i, _, n, at0, _ in pieces:
            lo, hi = runs.get(i, (99, 0))
            runs[i] = (min(lo, 4 * b + at0), max(hi, 4 * b + at0 + n))
    assert all(hi - lo == i + 1 for i, (lo, hi) in runs.items())
    return runs


UNITS = [(kt, half, tuple(range(j, j + per)))
         for kt in range(KT) for half in range(2) if kt < 4 * (half + 1)
         for per in [min(4, CHUNK // (CHUNK * (half + 1) - max(kt * P, CHUNK * half)))]
         for per in [(1, 1, 2, 2, 4)[per]]
         for j in range(0, 4, per)]
NU = len(UNITS)
FIRST_UNIT = [min(n for n, (kt, _, _) in enumerate(UNITS) if kt == k) for k in range(KT)] + [NU]
DIAGONAL_UNITS = [sum(1 for kt, half, _ in UNITS if kt == k and half == k // 4) for k in range(KT)]

LEAD = NMAX // 3
MT_LATER = 3
def ring_of_body(nxt, nxt2):
    a = [("max", 1, n) for n in range(LEAD, NMAX)] if nxt else []
    b = [("max", 2, n) for n in range(LEAD)] if nxt2 else []
    ring = a[:4] + [("out", -1, 1)] + a[4:] + b[:MT_LATER]
    if nxt:
        ring += [("mrow", 1, 0), ("mrow", 1, 1)]
    ring += b[MT_LATER:]
    ring.insert(min(len(ring), 34), ("out", 0, 0))
    return ring


RING_PROLOGUE = [("max", 0, n) for n in range(NMAX)] + [("max", 1, n) for n in range(MT_LATER)] + \
                [("mrow", 0, 0), ("mrow", 0, 1)] + [("max", 1, n) for n in range(MT_LATER, LEAD)]
LOOPED = GROUPS - 2
LOOP3 = LOOPED // 3
LOOP, LAST_BUT_ONE, LAST = 0, 1, 2
RINGS = [ring_of_body(True, True), ring_of_body(True, False), ring_of_body(False, False)]
ORDERS = [["URURURbURURURaURUR", "URURbURURaRURUR", "URURbURUaRURR", "URURbURaRUR", "URURaRURU", "URUaRR", "URaR",
           "URURaURURUURUU"],
          ["UURURbURURaURURUR", "URURbURURaRURUR", "URURbURUaRURR", "URURbURaRUR", "UUaRUUR", "UUa", "UaR",
           "UUaUUUUUU"],
          ["UURUbUUaUUU", "UUbUUaUU", "UUbUUaU", "UUbUaU", "UUaUU", "UaU", "URa", "a"]]
RINGN = len(RINGS[LOOP])
RING0 = [len(RING_PROLOGUE), len(RING_PROLOGUE), len(RING_PROLOGUE) + len(RINGS[LAST_BUT_ONE]) - RINGN]
RING_END = RING0[LAST] + RINGN * (GROUPS - 1) + len(RINGS[LAST])


def count(p, u, each, more):
    return p * (3 * each) + (u * each + more)


def loads(p, u, d):
    return p + ((u + d) // 3 + 1)


G_BANK, U_BANK, Y_BANK, N_BANK, R_BANK = (0, 1), (2, 3), 4, 5, 6
RING, SLOTS, O_BANK = (0, 1, 2), (3, 4, 5), (6, 7)

TP_GROUPS = [(w, n, min(4, NT - n)) for n in range(0, NT, 4) for w in ("g", "u")] + \
            [("d", n, min(4, NT - n)) for n in range(0, NT, 4)]
TP_BANKS = (0, 1, 2, 3)
N_CONST = 7
N_SMALL, N_BIAS = 3, 5
N_CONST_DMA = 3


class Chip:
    pass


def place_memory(K, ctx):
    def sem(name):
        return ctx.enter_context(K.nc.semaphore(name))

    def sb(name, shape, dt=F32, scope=ctx):
        return scope.enter_context(K.nc.sbuf_tensor(name, shape, dt))

    K.wt_dram = [K.nc.dram_tensor(f"route_rows{f}", (TT, NGATE, P), F32, kind="Internal").ap() for f in range(2)]
    K.q_dram = K.nc.dram_tensor("q_stack", (GROUPS * 4, 32, SEQ), F32, kind="Internal").ap()
    K.k_dram = K.nc.dram_tensor("k_stack", (GROUPS * 4, 32, SEQ), F32, kind="Internal").ap()

    K.out_tiles = K.result.rearrange("b (t p) e -> p (b t) e", p=P)

    K.x = sb("x", [P, TT, EMB])
    K.wide = {}
    for w in ("g", "u", "d"):
        for part in ("h", "l"):
            K.wide[w + part] = sb(f"w{w}_{part}", [P, HROWS], F32R)
    K.small = {}
    for w in ("q", "k", "v", "p"):
        for part in ("h", "l"):
            K.small[w + part] = sb(f"w{w}_{part}", [P, EMB], F32R)
    K.rw = sb("rw", [P, 2 * NGATE], F32R)
    K.ident = sb("ident", [P, P])
    K.ident_b = sb("ident_b", [P, P], BF16)
    K.mask_b = sb("mask_b", [P, P], BF16)
    K.b_q = sb("b_q", [P, 1])
    K.b_k = sb("b_k", [P, 1])
    K.b_v = sb("b_v", [P, EMB])
    K.b_p = sb("b_p", [P, EMB])
    K.rb_row = sb("rb_row", [P, NGATE])
    K.rank = sb("rank", [P, NGATE])
    K.rank_i = sb("rank_i", [P, NGATE], mybir.dt.int32)
    K.stats = sb("stats", [P, 2, TPC, 6])
    K.mv = sb("mv", [P, 2, TPC, 2])
    K.var_e = sb("var_e", [P, 2, TPC])
    K.half_neg = sb("half_neg", [P, TPC])
    K.rstd = sb("rstd", [P, 2, TPC])
    z0 = sb("z", [P, TPC, EMB])

    with ExitStack() as s:
        K.zt_h = sb("zt_h", [P, TOKENS], F32R, scope=s)
        K.zt_l = sb("zt_l", [P, TOKENS], F32R, scope=s)
        with ExitStack() as s2:
            K.w_slots = sb("w_slots", [P, len(SLOT_LOADS), CHUNK], scope=s2)
            K.silu = sb("silu", [P, 2, CHUNK], scope=s2)
            K.act = sb("act", [P, 4, CHUNK], scope=s2)
            K.act_h = sb("act_h", [P, 4, CHUNK], F32R, scope=s2)
            K.act_l = sb("act_l", [P, 4, CHUNK], F32R, scope=s2)
            K.yt = sb("yt", [P, CHUNK], scope=s2)
            K.z = [z0, K.yt[:, :].rearrange("p (t e) -> p t e", e=EMB)]
            K.r_log = sb("r_log", [P, TT, NGATE], scope=s2)
            K.r_exp = sb("r_exp", [P, TT, NGATE], scope=s2)
            K.r_c = sb("r_c", [P, TT, NGATE], scope=s2)
            K.r_s1 = sb("r_s1", [P, TT, NGATE], scope=s2)
            K.r_s2 = sb("r_s2", [P, TT, NGATE], scope=s2)
            K.r_w = sb("r_w", [P, TT, NGATE], scope=s2)
            K.r_wt = sb("r_wt", [P, P], scope=s2)
            K.r_m = sb("r_m", [P, TT], scope=s2)
            K.r_r = sb("r_r", [P, TT], scope=s2)
            with ExitStack() as s3:
                K.nat = {w: sb(f"nat_{w}", [P, HROWS], scope=s3) for w in ("g", "u", "d")}
                K.nat_attn = sb("nat_attn", [P, 3 * EMB], scope=s3)
                K.nat_proj = sb("nat_proj", [P, EMB], scope=s3)
                K.nat_route = sb("nat_route", [P, P], scope=s3)
                K.rows0 = sb("rows0", [32, CHUNK], scope=s3)
                K.rows1 = sb("rows1", [32, CHUNK], scope=s3)
            with ExitStack() as s3:
                K.keys = [sb(f"keys{u}", [P, 4, SEQ], F32R, scope=s3) for u in range(2)]
                with ExitStack() as s4:
                    K.keys.append(sb("keys2", [P, 4, SEQ], F32R, scope=s4))
                with ExitStack() as s4:
                    K.ao_f = sb("ao_f", [P, 2, CHUNK], scope=s4)
                    K.ao_h = sb("ao_h", [P, 2, CHUNK], F32R, scope=s4)
                    K.ao_l = sb("ao_l", [P, 2, CHUNK], F32R, scope=s4)
        with ExitStack() as s2:
            K.q1_f = sb("q1_f", [P, 2, CHUNK], scope=s2)
            K.q1_h = sb("q1_h", [P, 2, CHUNK], F32R, scope=s2)
            K.q1_l = sb("q1_l", [P, 2, CHUNK], F32R, scope=s2)
            K.q_f = sb("q_f", [P, 2, CHUNK], scope=s2)
            K.q_h = sb("q_h", [P, 2, CHUNK], F32R, scope=s2)
            K.q_l = sb("q_l", [P, 2, CHUNK], F32R, scope=s2)
    with ExitStack() as s:
        K.probs = sb("probs", [P, 2, 4, SEQ], scope=s)
        K.vg = sb("vg", [P, KT, 4, 32], scope=s)
        K.o_all = sb("o_all", [P, GROUPS + 1, KT, 32], scope=s)
        K.queries = [sb(f"queries{u}", [P, SEQ], F32R, scope=s) for u in range(3)]
        K.v_all = sb("v_all", [P, GROUPS, KT, 32], scope=s)
        K.ot = sb("ot", [P, 2, CHUNK], scope=s)
        K.rsum = sb("rsum", [P, 16, 1], scope=s)
        K.mxp = sb("mxp", [P, 4, 4 * NBANK], scope=s)
        K.nmax = sb("nmax", [P, 4, KT], scope=s)
        K.mm_hl = sb("mm_hl", [P, 4, 2, KT], F32R, scope=s)
        K.m_rows = sb("m_rows", [64, P], F32R, scope=s)

    K.shared_rows = K.w_slots[0:SLOT_LOADS[SLOT_OF[FIRST_ROUTED]][0][0], SLOT_OF[FIRST_ROUTED], :]

    K.psum = ctx.enter_context(K.nc.psum_tensor("psum", [P, 8, CHUNK], F32))


    K.ld = {n: sem(f"ld_{n}") for n in ("nat", "small", "bias", "const", "out")}
    K.ld_x = [sem(f"ld_x{b}") for b in range(BATCH)]
    K.passed = sem("passed")
    K.consts = sem("consts")
    K.tp_pe, K.tp_hi, K.tp_lo = sem("tp_pe"), sem("tp_hi"), sem("tp_lo")
    K.sw_hi, K.sw_lo = sem("sw_hi"), sem("sw_lo")
    K.padded, K.blank, K.ones, K.cleared = sem("padded"), sem("blank"), sem("ones"), sem("cleared")
    K.NS = [{n: sem(f"n{k}_{n}") for n in
                  ("bn", "mv", "ve", "rstd", "z", "tr", "hi", "lo")} for k in range(3)]
    K.RS = [{n: sem(f"r{k}_{n}") for n in
                   ("log", "sum", "neg", "exp", "step", "w", "tr", "wt", "st")} for k in range(2)]
    K.FF = [{n: sem(f"f{k}_{n}") for n in
                 ("up", "silu", "act", "route", "hi", "lo", "down", "yev", "ytr", "out")} for k in range(2)]
    K.slot_sems = [sem(f"slot{n}") for n in range(len(SLOT_LOADS))]
    K.A = {n: sem(f"a_{n}") for n in
            ("q1", "q1f", "q1h", "q1l", "q", "qf", "qh", "ql", "v", "vev", "init",
             "ring", "taken", "mm", "sp", "ex", "mk", "pv", "oev", "vg", "ready", "nm", "rs", "vi", "og", "otr", "oh", "ol", "op", "bp", "xup")}
    K.q_st = [sem(f"q_st{c}") for c in range(NCH)]
    K.k_st = [sem(f"k_st{c}") for c in range(NCH)]
    K.ld_k = [sem(f"ld_k{u}") for u in range(3)]
    K.ld_r = [sem(f"ld_r{u}") for u in range(3)]


def bank(K, n):
    return K.psum[:, n, :]


def alone(K, e):
    e.sem_inc(K.passed, 1)


def norm_stats_dve(K, k, c):
    e, v = K.nc.vector, 0 if k == 1 else c % 2
    if k != 1 and c > 1:
        e.wait_ge(K.NS[k]["z"], c - 1)
    for t in range(TPC):
        e.bn_stats(K.stats[:, v, t, :], K.x[:, at(c * TPC + t, 1), :]).then_inc(K.NS[k]["bn"], 1)
    e.wait_ge(K.NS[k]["bn"], TPC * (c + 1))
    alone(K, e)
    for t in range(TPC):
        ins = e.bn_aggr(K.mv[:, v, t, :], K.stats[:, v, t, :])
    ins.then_inc(K.NS[k]["mv"], 1)


def norm_rstd_pool(K, k, c):
    e, v = K.nc.gpsimd, 0 if k == 1 else c % 2
    e.wait_ge(K.NS[k]["mv"], c + 1)
    alone(K, e)
    e.tensor_scalar(K.var_e[:, v, :], K.mv[:, v, :, 1], LN_EPS, None, ALU.add).then_inc(K.NS[k]["ve"], 1)
    e.wait_ge(K.NS[k]["ve"], c + 1)
    e.tensor_tensor(K.rstd[:, v, :], K.var_e[:, v, :], K.half_neg[:, :], ALU.pow).then_inc(K.NS[k]["rstd"], 1)


def norm_z_dve(K, k, c):
    e, v = K.nc.vector, 0 if k == 1 else c % 2
    e.wait_ge(K.NS[k]["rstd"], c + 1)
    e.wait_ge(K.NS[k]["mv"], c + 1)
    if k != 1 and c > 1:
        e.wait_ge(K.NS[k]["tr"], c - 1)
    for t in range(TPC):
        ins = e.tensor_scalar(K.z[v][:, t, :], K.x[:, at(c * TPC + t, 1), :], K.mv[:, v, t, 0:1],
                              K.rstd[:, v, t:t + 1], ALU.subtract, ALU.mult)
    ins.then_inc(K.NS[k]["z"], 1)


def norm_bank(k, c):
    return N_BANK if k == 1 else (N_BANK, Y_BANK)[c % 2]


def norm_tr_pe(K, k, c):
    e, v = K.nc.tensor, 0 if k == 1 else c % 2
    e.wait_ge(K.NS[k]["z"], c + 1)
    if k != 1 and c > 1:
        e.wait_ge(K.NS[k]["lo"], c - 1)
    for t in range(TPC):
        ins = e.transpose(bank(K, norm_bank(k, c))[:, t * P:(t + 1) * P], K.z[v][:, t, :], K.ident[:, :])
    ins.then_inc(K.NS[k]["tr"], 1)


def norm_hi_act(K, k, c):
    K.nc.scalar.wait_ge(K.NS[k]["tr"], c + 1)
    K.nc.scalar.copy(K.zt_h[:, at(c * CHUNK, CHUNK)], bank(K, norm_bank(k, c))).then_inc(K.NS[k]["hi"], 1)


def norm_lo_dve(K, k, c):
    K.nc.vector.wait_ge(K.NS[k]["hi"], c + 1)
    K.nc.vector.tensor_tensor(K.zt_l[:, at(c * CHUNK, CHUNK)], bank(K, norm_bank(k, c)),
                            K.zt_h[:, at(c * CHUNK, CHUNK)].bitcast(F32), ALU.subtract).then_inc(K.NS[k]["lo"], 1)


def logits_pe(K, f, k, c):
    e = K.nc.tensor
    if f == 0 and c == 0:
        e.wait_ge(K.sw_lo, 5)
    e.wait_ge(K.NS[k]["lo"], c + 1)
    for t in range(c * TPC, (c + 1) * TPC):
        dst = bank(K, R_BANK)[:, t * 2 * NGATE:(t + 1) * 2 * NGATE]
        zh, zl = K.zt_h[:, t * P:(t + 1) * P], K.zt_l[:, t * P:(t + 1) * P]
        e.matmul(dst, zh, K.rw[:, :], start=True, stop=True, skip_group_check=True)
        ins = e.matmul(dst[:, 0:NGATE], zl, K.rw[:, 0:NGATE], start=False, stop=True, skip_group_check=True)
    ins.then_inc(K.RS[f]["log"], 1)


def route_tr_pe(K, f):
    e = K.nc.tensor
    e.wait_ge(K.RS[f]["w"], 1)
    e.transpose(bank(K, R_BANK)[:, CHUNK - P:], K.r_w[:, :, :].rearrange("p t e -> p (t e)"),
                K.ident[:, :]).then_inc(K.RS[f]["tr"], 1)


def router_dve(K, f):
    e, s = K.nc.vector, K.RS[f]

    def wide_of(v):
        return v.unsqueeze(2).to_broadcast([P, TT, NGATE])

    e.wait_ge(K.ld["bias"], 16 * N_BIAS)
    e.wait_ge(s["log"], NCH)
    logits = bank(K, R_BANK)[:, 0:TT * 2 * NGATE].rearrange("p (t e) -> p t e", e=2 * NGATE)
    e.tensor_tensor(K.r_log[:, :, :], logits[:, :, 0:NGATE], K.rb_row[:, :].unsqueeze(1).to_broadcast([P, TT, NGATE]),
                    ALU.add).then_inc(s["sum"], 1)
    e.wait_ge(s["sum"], 1)
    e.tensor_tensor(K.r_log[:, :, :], K.r_log[:, :, :], logits[:, :, NGATE:], ALU.add).then_inc(s["step"], 1)
    e.wait_ge(s["step"], 1)
    e.tensor_reduce(K.r_m[:, :], K.r_log[:, :, :], AX.X, ALU.max).then_inc(s["step"], 1)
    e.wait_ge(s["step"], 2)
    e.tensor_tensor(K.r_c[:, :, :], K.r_log[:, :, :], wide_of(K.r_m[:, :]), ALU.subtract).then_inc(s["neg"], 1)
    rank = K.rank[:, :].unsqueeze(1).to_broadcast([P, TT, NGATE])
    e.wait_ge(s["neg"], 1)
    e.scalar_tensor_tensor(K.r_log[:, :, :], K.r_c[:, :, :], 0.0, rank, ALU.is_equal, ALU.mult).then_inc(s["step"], 1)
    e.wait_ge(s["step"], 3)
    e.tensor_reduce(K.r_m[:, :], K.r_log[:, :, :], AX.X, ALU.max).then_inc(s["step"], 1)
    e.wait_ge(s["step"], 4)
    e.tensor_tensor(K.r_s1[:, :, :], K.r_log[:, :, :], wide_of(K.r_m[:, :]), ALU.is_equal).then_inc(s["step"], 1)
    e.wait_ge(s["step"], 5)
    e.wait_ge(s["exp"], 1)
    e.scalar_tensor_tensor(K.r_w[:, :, :], K.r_s1[:, :, :], -2.0, K.r_exp[:, :, :], ALU.mult, ALU.add)\
     .then_inc(s["step"], 1)
    e.wait_ge(s["step"], 6)
    e.tensor_reduce(K.r_m[:, :], K.r_w[:, :, :], AX.X, ALU.max).then_inc(s["step"], 1)
    e.wait_ge(s["step"], 7)
    e.tensor_tensor(K.r_c[:, :, :], K.r_w[:, :, :], wide_of(K.r_m[:, :]), ALU.is_equal).then_inc(s["step"], 1)
    e.wait_ge(s["step"], 8)
    e.tensor_tensor(K.r_c[:, :, :], K.r_c[:, :, :], rank, ALU.mult).then_inc(s["step"], 1)
    e.wait_ge(s["step"], 9)
    e.tensor_reduce(K.r_m[:, :], K.r_c[:, :, :], AX.X, ALU.max).then_inc(s["step"], 1)
    e.wait_ge(s["step"], 10)
    e.tensor_tensor(K.r_s2[:, :, :], K.r_c[:, :, :], wide_of(K.r_m[:, :]), ALU.is_equal).then_inc(s["step"], 1)
    e.wait_ge(s["step"], 11)
    e.tensor_tensor(K.r_c[:, :, :], K.r_s1[:, :, :], K.r_s2[:, :, :], ALU.add).then_inc(s["step"], 1)
    e.wait_ge(s["step"], 12)
    e.tensor_tensor(K.r_c[:, :, :], K.r_c[:, :, :], K.r_exp[:, :, :], ALU.mult).then_inc(s["step"], 1)
    e.wait_ge(s["step"], 13)
    e.tensor_reduce(K.r_m[:, :], K.r_c[:, :, :], AX.X, ALU.add).then_inc(s["step"], 1)
    e.wait_ge(s["step"], 14)
    e.reciprocal(K.r_r[:, :], K.r_m[:, :]).then_inc(s["step"], 1)
    e.wait_ge(s["step"], 15)
    e.tensor_tensor(K.r_w[:, :, :], K.r_c[:, :, :], wide_of(K.r_r[:, :]), ALU.mult).then_inc(s["w"], 1)
    e.wait_ge(s["tr"], 1)
    e.tensor_copy(K.r_wt[:, :], bank(K, R_BANK)[:, CHUNK - P:]).then_inc(s["wt"], 1)


def router_act(K, f):
    K.nc.scalar.wait_ge(K.RS[f]["neg"], 1)
    K.nc.scalar.activation(K.r_exp[:, :, :], K.r_c[:, :, :], ACT.Exp).then_inc(K.RS[f]["exp"], 1)


def router_sp(K, f):
    K.nc.sync.wait_ge(K.RS[f]["wt"], 1)
    K.nc.sync.dma_start(K.wt_dram[f].rearrange("t e p -> (t e) p"), K.r_wt[:, :]).then_inc(K.RS[f]["st"], 16)
    K.nc.sync.wait_ge(K.RS[f]["st"], 16)


def slot_load(K, f, c, n):
    for a, b, e in SLOT_LOADS[n]:
        src = K.wt_dram[f][at(c * TPC, TPC), e - 1, :].partition_broadcast(b - a)
        K.nc.sync.dma_start(K.w_slots[a:b, n, :].rearrange("p (t q) -> p t q", q=P), src).then_inc(K.slot_sems[n], 16)


def slot_base(K, f, n):
    return 16 * len(SLOT_LOADS[n]) * NCH * f


def T(K, c, n):
    return c * NT + n


def up_pe(K, f, c, n, first=False):
    e, s = K.nc.tensor, K.FF[f]
    if n == 0:
        e.wait_ge(K.NS[2 * f]["lo"], c + 1)
    if not (first and n < 2):
        e.wait_ge(s["act"], T(K, c, n) - 1)
    w = slice(n * P, (n + 1) * P)
    zc = at(c * CHUNK, CHUNK)
    for which, b in (("g", G_BANK[n % 2]), ("u", U_BANK[n % 2])):
        e.matmul(bank(K, b), K.wide[which + "h"][:, w], K.zt_h[:, zc], start=True, stop=False)
        e.matmul(bank(K, b), K.wide[which + "h"][:, w], K.zt_l[:, zc], start=False, stop=False)
        ins = e.matmul(bank(K, b), K.wide[which + "l"][:, w], K.zt_h[:, zc], start=False, stop=True)
    ins.then_inc(s["up"], 1)


def down_pe(K, f, c, n, first=False):
    e, s = K.nc.tensor, K.FF[f]
    if n == 0 and not first:
        e.wait_ge(s["yev"], c)
    e.wait_ge(s["lo"], T(K, c, n) + 1)
    w = slice(n * P, (n + 1) * P)
    e.matmul(bank(K, Y_BANK), K.wide["dh"][:, w], K.act_h[:, PLACE[n], :], start=(n == 0), stop=False)
    e.matmul(bank(K, Y_BANK), K.wide["dl"][:, w], K.act_h[:, PLACE[n], :], start=False, stop=False)
    e.matmul(bank(K, Y_BANK), K.wide["dh"][:, w], K.act_l[:, PLACE[n], :], start=False,
             stop=(n == NT - 1)).then_inc(s["down"], 1)


def ytr_pe(K, f, c, first=False):
    e, s = K.nc.tensor, K.FF[f]
    e.wait_ge(s["yev"], c + 1)
    if not first:
        if f == 0:
            e.wait_ge(K.NS[1]["lo"], c)
        else:
            e.wait_ge(s["out"], c)
    for t in range(TPC):
        ins = e.transpose(bank(K, N_BANK)[:, t * P:(t + 1) * P], K.yt[:, t * P:(t + 1) * P], K.ident[:, :])
    ins.then_inc(s["ytr"], 1)


def ffn_pe(K, f):
    def body(c, before):
        for n in range(NT):
            up_pe(K, f, c, n, before is None)
            if n >= 3:
                down_pe(K, f, c, n - 3, before is None)
            elif before is not None:
                down_pe(K, f, before, n + NT - 3)
            if before is None and n == 1 and f == 1:
                route_tr_pe(K, 1)
            if before is not None and n == 4:
                ytr_pe(K, f, before)
            if before is not None and n == 10 and f == 0:
                norm_tr_pe(K, 1, before)
    body(0, None)
    with K.nc.tensor.Fori(1, NCH) as c:
        body(c, c - 1)
    for n in range(NT - 3, NT):
        down_pe(K, f, NCH - 1, n)
    if f == 1:
        ytr_pe(K, 1, NCH - 1)


def silu_act(K, f, c, n):
    e, s = K.nc.scalar, K.FF[f]
    e.wait_ge(s["up"], T(K, c, n) + 1)
    e.activation(K.silu[:, n % 2, :], bank(K, G_BANK[n % 2]), ACT.Silu).then_inc(s["silu"], 1)


def hi_act(K, f, c, n, first=False):
    e, s = K.nc.scalar, K.FF[f]
    if n >= FIRST_ROUTED:
        e.wait_ge(s["route"], c * NROUTED + (n - FIRST_ROUTED + 1))
    else:
        e.wait_ge(s["act"], T(K, c, n) + 1)
    if not (first and n < 4):
        e.wait_ge(s["down"], T(K, c, n - BACK[n]) + 1)
    e.copy(K.act_h[:, PLACE[n], :], K.act[:, PLACE[n], :]).then_inc(s["hi"], 1)


def ffn_act(K, f):
    def body(c, before):
        for n in range(NT):
            if n >= 2:
                hi_act(K, f, c, n - 2, before is None)
            elif before is not None:
                hi_act(K, f, before, n + NT - 2)
            silu_act(K, f, c, n)
            if before is not None and n == 11 and f == 0:
                norm_hi_act(K, 1, before)
    body(0, None)
    with K.nc.scalar.Fori(1, NCH) as c:
        body(c, c - 1)
    for n in range(NT - 2, NT):
        hi_act(K, f, NCH - 1, n)


def act_dve(K, f, c, n, first=False):
    e, s = K.nc.vector, K.FF[f]
    e.wait_ge(s["silu"], T(K, c, n) + 1)
    if not (first and n < 4):
        e.wait_ge(s["lo"], T(K, c, n - BACK[n]) + 1)
    e.tensor_tensor(K.act[:, PLACE[n], :], K.silu[:, n % 2, :], bank(K, U_BANK[n % 2]), ALU.mult).then_inc(s["act"], 1)


def lo_dve(K, f, c, n):
    e, s = K.nc.vector, K.FF[f]
    e.wait_ge(s["hi"], T(K, c, n) + 1)
    e.tensor_tensor(K.act_l[:, PLACE[n], :], K.act[:, PLACE[n], :], K.act_h[:, PLACE[n], :].bitcast(F32),
                    ALU.subtract).then_inc(s["lo"], 1)


def yev_dve(K, f, c, first=False):
    e, s = K.nc.vector, K.FF[f]
    e.wait_ge(s["down"], T(K, c, NT - 1) + 1)
    if not first:
        e.wait_ge(s["ytr"], c)
    e.tensor_scalar(K.yt[:, :], bank(K, Y_BANK), 0.5, None, ALU.mult).then_inc(s["yev"], 1)


def xup_dve(K, f, c):
    e, s = K.nc.vector, K.FF[f]
    e.wait_ge(s["ytr"], c + 1)
    xc = K.x[:, at(c * TPC, TPC), :]
    e.tensor_tensor(xc, xc, bank(K, N_BANK).rearrange("p (t e) -> p t e", e=EMB), ALU.add)\
     .then_inc(s["out"], 1)


def ffn_dve(K, f):
    def after(c, n):
        if n == 3:
            yev_dve(K, f, c)
        if n == 5:
            xup_dve(K, f, c)
        if f == 0:
            if n == 6:
                K.nc.vector.wait_ge(K.FF[0]["out"], c + 1)
                alone(K, K.nc.vector)
                norm_stats_dve(K, 1, c)
            if n == 9:
                norm_z_dve(K, 1, c)
            if n == 12:
                norm_lo_dve(K, 1, c)

    def body(c, before):
        for n in range(NT):
            if before is not None:
                after(before, n)
            if n >= 2:
                lo_dve(K, f, c, n - 2)
            elif before is not None:
                lo_dve(K, f, before, n + NT - 2)
            act_dve(K, f, c, n, before is None)
    body(0, None)
    with K.nc.vector.Fori(1, NCH) as c:
        body(c, c - 1)
    for n in range(NT - 2, NT):
        lo_dve(K, f, NCH - 1, n)
    if f == 1:
        yev_dve(K, 1, NCH - 1)
        xup_dve(K, 1, NCH - 1)


def ffn_pool(K, f):
    e, s = K.nc.gpsimd, K.FF[f]

    def body(c, before):
        for n in range(NT):
            if before is not None and n == 8 and f == 0:
                norm_rstd_pool(K, 1, before)
            if n < FIRST_ROUTED:
                continue
            slot = SLOT_OF[n]
            e.wait_ge(s["act"], T(K, c, n) + 1)
            if n == FIRST_ROUTED or SLOT_OF[n - 1] != slot:
                e.wait_ge(K.slot_sems[slot], slot_base(K, f, slot) + 16 * len(SLOT_LOADS[slot]) * (c + 1))
            e.tensor_tensor(K.act[:, PLACE[n], :], K.act[:, PLACE[n], :], K.w_slots[:, slot, :], ALU.mult)\
             .then_inc(s["route"], 1)
    body(0, None)
    with e.Fori(1, NCH) as c:
        body(c, c - 1)
    if f == 0:
        norm_rstd_pool(K, 1, NCH - 1)


def ffn_sp(K, f):
    e, s = K.nc.sync, K.FF[f]
    order = sorted(range(len(SLOT_LOADS)), key=lambda n: SLOT_END[n])
    for n in order:
        slot_load(K, f, 0, n)
    with e.Fori(1, NCH) as c:
        for n in order:
            e.wait_ge(s["route"], (c - 1) * NROUTED + (SLOT_END[n] - FIRST_ROUTED + 1))
            slot_load(K, f, c, n)
        if f == 1:
            store_out(K, c - 1)
    if f == 1:
        store_out(K, NCH - 1)
        e.wait_ge(K.ld["out"], 16 * NCH)


def store_out(K, c):
    K.nc.sync.wait_ge(K.FF[1]["out"], c + 1)
    K.nc.sync.dma_start(K.out_tiles[:, at(c * TPC, TPC), :], K.x[:, at(c * TPC, TPC), :])\
      .then_inc(K.ld["out"], 16)



def start_sp(K):
    e = K.nc.sync
    for b in range(BATCH):
        e.dma_start(K.x[:, b * KT:(b + 1) * KT, :], K.tokens[b].rearrange("(t p) e -> p t e", p=P)).then_inc(K.ld_x[b], 16)
    r0 = HID // P * P
    rg_rows, ru_rows = (w.rearrange("e i h -> (e i) h") for w in (K.gate_r, K.up_r))
    for w, shared, routed in (("g", K.gate_s, rg_rows), ("u", K.up_s, ru_rows)):
        dst = K.nat[w][:, :].rearrange("p (n h) -> p n h", h=EMB)
        head = (HID // P + 1) * P - HID
        e.dma_start(dst[:, 0:HID // P, :], shared[0:r0, :].rearrange("(n p) h -> p n h", p=P))\
         .then_inc(K.ld["nat"], 16)
        e.dma_start(dst[0:HID - r0, HID // P, :], shared[r0:HID, :]).then_inc(K.ld["nat"], 16)
        e.dma_start(dst[HID - r0:P, HID // P, :], routed[0:head, :]).then_inc(K.ld["nat"], 16)
        e.dma_start(dst[:, HID // P + 1:, :], routed[head:, :].rearrange("(n p) h -> p n h", p=P))\
         .then_inc(K.ld["nat"], 16)
    e.dma_start(K.nat["d"][:, 0:HID], K.down_s).then_inc(K.ld["nat"], 16)
    e.dma_start(K.nat["d"][:, HID:].rearrange("p (e i) -> p e i", i=HID), K.down_r.rearrange("e h i -> h e i"))\
     .then_inc(K.ld["nat"], 16)
    e.wait_ge(K.consts, N_CONST)
    def many(src, n):
        return src[:, :].unsqueeze(1).to_broadcast([32, n * SEQ // CHUNK, CHUNK])
    def rows(dram, a, b):
        return dram[:, a:b, :].rearrange("g r (s t) -> g (r s) t", t=CHUNK)
    e.dma_start(rows(K.q_dram, 0, 8), many(K.rows0, 8)).then_inc(K.ld["const"], 16)
    e.dma_start(rows(K.k_dram, 0, 2), many(K.rows1, 2)).then_inc(K.ld["const"], 16)
    e.dma_start(rows(K.k_dram, 2, 8), many(K.rows0, 6)).then_inc(K.ld["const"], 16)


def start_act(K):
    e = K.nc.scalar
    e.dma_start(K.nat_attn[:, :], K.attn_w).then_inc(K.ld["small"], 16)
    e.dma_start(K.nat_proj[:, :], K.proj_w).then_inc(K.ld["small"], 16)
    e.wait_ge(K.padded, 2)
    e.dma_start(K.nat_route[0:ROUTED, :], K.route_w).then_inc(K.ld["small"], 16)
    e.dma_start(K.rb_row[:, 0:ROUTED], K.route_b.partition_broadcast(P)).then_inc(K.ld["bias"], 16)
    e.dma_start(K.b_q[:, :], K.attn_b[0:EMB].rearrange("(p a) -> p a", a=1)).then_inc(K.ld["bias"], 16)
    e.dma_start(K.b_k[:, :], K.attn_b[EMB:2 * EMB].rearrange("(p a) -> p a", a=1)).then_inc(K.ld["bias"], 16)
    e.dma_start(K.b_v[:, :], K.attn_b[2 * EMB:3 * EMB].partition_broadcast(P)).then_inc(K.ld["bias"], 16)
    e.dma_start(K.b_p[:, :], K.proj_b.partition_broadcast(P)).then_inc(K.ld["bias"], 16)


def start_pool(K):
    e = K.nc.gpsimd
    e.memset(K.nat_route[:, :], 0.0).then_inc(K.padded, 1)
    e.memset(K.rb_row[:, :], MASKED).then_inc(K.padded, 1)
    e.memset(K.ident[:, :], 0.0).then_inc(K.blank, 1)
    e.memset(K.mask_b[:, :], 0.0).then_inc(K.blank, 1)
    e.iota(K.rank_i[:, :], pattern=[[-1, NGATE]], base=NGATE, channel_multiplier=0).then_inc(K.blank, 1)
    e.wait_ge(K.blank, 3)
    e.affine_select(out=K.ident[:, :], in_=K.ident[:, :], compare_op=ALU.not_equal, fill=1.0, base=0,
                    pattern=[[-1, P]], channel_multiplier=1).then_inc(K.blank, 1)
    e.wait_ge(K.blank, 4)
    e.tensor_copy(K.ident_b[:, :], K.ident[:, :]).then_inc(K.consts, 1)
    e.affine_select(out=K.mask_b[:, :], in_=K.mask_b[:, :], compare_op=ALU.is_ge, fill=MASKED, base=0,
                    pattern=[[1, P]], channel_multiplier=-1).then_inc(K.consts, 1)
    e.memset(K.rows0[:, :], 0.0).then_inc(K.consts, 1)
    e.memset(K.rows1[:, :], 1.0).then_inc(K.consts, 1)
    e.memset(K.half_neg[:, :], -0.5).then_inc(K.consts, 1)
    e.tensor_copy(K.rank[:, :], K.rank_i[:, :]).then_inc(K.consts, 1)
    e.memset(K.shared_rows, 1.0).then_inc(K.consts, 1)


def clear_pool(K):
    e = K.nc.gpsimd
    e.wait_ge(K.tp_pe, len(TP_GROUPS))
    e.wait_ge(K.sw_lo, 5)
    e.wait_ge(K.ld["const"], 16 * N_CONST_DMA)
    for u in range(3):
        e.memset(K.keys[u][:, :, :].bitcast(F32), 0.0).then_inc(K.cleared, 1)


def weights_small_pe(K):
    e = K.nc.tensor
    e.wait_ge(K.ld["small"], 16 * N_SMALL)
    e.wait_ge(K.consts, N_CONST)
    e.transpose(bank(K, 7)[:, 0:P], K.nat_attn[:, EMB:2 * EMB], K.ident[:, :])
    e.transpose(bank(K, 7)[:, P:2 * P], K.nat_route[:, :], K.ident[:, :]).then_inc(K.A["init"], 1)


def weights_pe(K, m):
    e, (w, n0, k) = K.nc.tensor, TP_GROUPS[m]
    if w == "g" and n0 == 0:
        e.wait_ge(K.ld["nat"], 16 * 10)
    if m >= len(TP_BANKS):
        e.wait_ge(K.tp_lo, m - len(TP_BANKS) + 1)
    for t in range(k):
        ins = e.transpose(bank(K, TP_BANKS[m % 4])[:, t * P:(t + 1) * P],
                          K.nat[w][:, (n0 + t) * P:(n0 + t + 1) * P], K.ident[:, :])
    ins.then_inc(K.tp_pe, 1)


def weights_act(K):
    e = K.nc.scalar
    e.wait_ge(K.ld["small"], 16 * N_SMALL)
    e.copy(K.small["qh"][:, :], K.nat_attn[:, 0:EMB]).then_inc(K.sw_hi, 1)
    e.copy(K.small["vh"][:, :], K.nat_attn[:, 2 * EMB:]).then_inc(K.sw_hi, 1)
    e.copy(K.small["ph"][:, :], K.nat_proj[:, :]).then_inc(K.sw_hi, 1)
    e.wait_ge(K.A["init"], 1)
    e.copy(K.small["kh"][:, :], bank(K, 7)[:, 0:P]).then_inc(K.sw_hi, 1)
    e.copy(K.rw[:, 0:NGATE], bank(K, 7)[:, P:P + NGATE]).then_inc(K.sw_hi, 1)


def weights_hi_act(K, m):
    w, n0, k = TP_GROUPS[m]
    K.nc.scalar.wait_ge(K.tp_pe, m + 1)
    K.nc.scalar.copy(K.wide[w + "h"][:, n0 * P:(n0 + k) * P], bank(K, TP_BANKS[m % 4])[:, 0:k * P]).then_inc(K.tp_hi, 1)


def weights_small_dve(K):
    e = K.nc.vector
    for n, (w, src) in enumerate((("q", K.nat_attn[:, 0:EMB]), ("v", K.nat_attn[:, 2 * EMB:]),
                                  ("p", K.nat_proj[:, :]), ("k", bank(K, 7)[:, 0:P]))):
        e.wait_ge(K.sw_hi, 5)
        e.tensor_tensor(K.small[w + "l"][:, :], src, K.small[w + "h"][:, :].bitcast(F32), ALU.subtract)\
         .then_inc(K.sw_lo, 1)
    e.tensor_tensor(K.rw[:, NGATE:], bank(K, 7)[:, P:P + NGATE], K.rw[:, 0:NGATE].bitcast(F32), ALU.subtract)\
     .then_inc(K.sw_lo, 1)


def weights_lo_dve(K, m):
    e, (w, n0, k) = K.nc.vector, TP_GROUPS[m]
    e.wait_ge(K.tp_hi, m + 1)
    cols = slice(n0 * P, (n0 + k) * P)
    e.tensor_tensor(K.wide[w + "l"][:, cols], bank(K, TP_BANKS[m % 4])[:, 0:k * P],
                    K.wide[w + "h"][:, cols].bitcast(F32), ALU.subtract).then_inc(K.tp_lo, 1)


def three(K, e, dst, left, right):
    e.matmul(dst, left[0], right[0], start=True, stop=False)
    e.matmul(dst, left[0], right[1], start=False, stop=False)
    return e.matmul(dst, left[1], right[0], start=False, stop=True)


def qv_pe(K, c):
    e, u, cols = K.nc.tensor, c % 2, slice(c * CHUNK, (c + 1) * CHUNK)
    e.wait_ge(K.NS[1]["lo"], c + 1)
    if c >= 2:
        e.wait_ge(K.A["q1f"], c - 1)
    three(K, e, bank(K, 0 + u), (K.small["qh"][:, :], K.small["ql"][:, :]), (K.zt_h[:, cols], K.zt_l[:, cols]))\
        .then_inc(K.A["q1"], 1)
    if c >= 2:
        e.wait_ge(K.A["vev"], c - 1)
    for t in range(TPC):
        tc = slice(c * CHUNK + t * P, c * CHUNK + (t + 1) * P)
        ins = three(K, e, bank(K, 6 + u)[:, t * P:(t + 1) * P], (K.zt_h[:, tc], K.zt_l[:, tc]),
                    (K.small["vh"][:, :], K.small["vl"][:, :]))
    ins.then_inc(K.A["v"], 1)


def q_pe(K, c):
    e, u = K.nc.tensor, c % 2
    e.wait_ge(K.A["q1l"], c + 1)
    if c >= 2:
        e.wait_ge(K.A["ql"], c - 1)
    three(K, e, bank(K, 2 + u), (K.small["kh"][:, :], K.small["kl"][:, :]), (K.q1_h[:, u, :], K.q1_l[:, u, :]))\
        .then_inc(K.A["q"], 1)


def qv_act(K, c):
    e, u = K.nc.scalar, c % 2
    e.wait_ge(K.A["q1"], c + 1)
    if c >= 2:
        e.wait_ge(K.A["q"], c - 1)
    e.activation(K.q1_f[:, u, :], bank(K, 0 + u), ACT.Identity, bias=K.b_q[:, 0:1]).then_inc(K.A["q1f"], 1)
    e.wait_ge(K.A["q1f"], c + 1)
    e.copy(K.q1_h[:, u, :], K.q1_f[:, u, :]).then_inc(K.A["q1h"], 1)


def q_act(K, c):
    e, u = K.nc.scalar, c % 2
    e.wait_ge(K.A["q"], c + 1)
    if c >= 2:
        e.wait_ge(K.A["ql"], c - 1)
        e.wait_ge(K.q_st[c - 2], 16 * 3)
    e.activation(K.q_f[:, u, :], bank(K, 2 + u), ACT.Identity, bias=K.b_k[:, 0:1]).then_inc(K.A["qf"], 1)
    e.wait_ge(K.A["qf"], c + 1)
    e.copy(K.q_h[:, u, :], K.q_f[:, u, :]).then_inc(K.A["qh"], 1)


def qv_dve(K, c):
    e, u, b, half = K.nc.vector, c % 2, c // 2, c % 2
    e.wait_ge(K.A["q1h"], c + 1)
    e.tensor_tensor(K.q1_l[:, u, :], K.q1_f[:, u, :], K.q1_h[:, u, :].bitcast(F32), ALU.subtract)\
     .then_inc(K.A["q1l"], 1)
    e.wait_ge(K.A["v"], c + 1)
    dst = K.v_all[:, b * GPB:(b + 1) * GPB, half * TPC:(half + 1) * TPC, :].rearrange("p g t m -> p t g m")
    src = bank(K, 6 + u).rearrange("p (t g m) -> p t g m", g=GPB, m=32)
    bias = K.b_v[:, :].rearrange("p (g m) -> p g m", m=32)
    for t in range(TPC):
        ins = e.tensor_tensor(dst[:, t], src[:, t], bias, ALU.add)
    ins.then_inc(K.A["vev"], 1)


def q_dve(K, c):
    e, u = K.nc.vector, c % 2
    e.wait_ge(K.A["qh"], c + 1)
    e.tensor_tensor(K.q_l[:, u, :], K.q_f[:, u, :], K.q_h[:, u, :].bitcast(F32), ALU.subtract)\
     .then_inc(K.A["ql"], 1)


def stack_store(K, dram, part, c, src, s):
    b, half = c // 2, c % 2
    dst = dram[b * HEADS:(b + 1) * HEADS, 8 + 8 * part:16 + 8 * part, half * CHUNK:(half + 1) * CHUNK]
    K.nc.sync.dma_start(dst, src.bitcast(F32)).then_inc(s, 16)


def keys_sp(K, c):
    e, cols = K.nc.sync, slice(c * CHUNK, (c + 1) * CHUNK)
    e.wait_ge(K.NS[1]["lo"], c + 1)
    stack_store(K, K.k_dram, 0, c, K.zt_h[:, cols], K.k_st[c])
    stack_store(K, K.k_dram, 1, c, K.zt_l[:, cols], K.k_st[c])
    stack_store(K, K.k_dram, 2, c, K.zt_h[:, cols], K.k_st[c])


def queries_sp(K, c):
    e, u = K.nc.sync, c % 2
    e.wait_ge(K.A["ql"], c + 1)
    stack_store(K, K.q_dram, 0, c, K.q_h[:, u, :], K.q_st[c])
    stack_store(K, K.q_dram, 1, c, K.q_h[:, u, :], K.q_st[c])
    stack_store(K, K.q_dram, 2, c, K.q_l[:, u, :], K.q_st[c])


def m_unit_pe(K, n, r_bank, u):
    e = K.nc.tensor
    pieces, j = MAX_BANKS[n // 4], n % 4
    dst = bank(K, r_bank)
    for m, (i, k0, nb, at0, diag) in enumerate(pieces):
        ins = e.matmul(dst[:, at0 * P:(at0 + nb) * P], K.queries[u][:, i * P:(i + 1) * P],
                       K.keys[u][:, j, k0 * P:(k0 + nb) * P], start=(m == 0), stop=True, skip_group_check=True)
    for i, k0, nb, at0, diag in pieces:
        if diag:
            last = (at0 + nb - 1) * P
            ins = e.matmul(dst[:, last:last + P], K.mask_b[:, :], K.ident_b[:, :], start=False, stop=True,
                           skip_group_check=True)
    return ins


def ring_pe(K, what, d, n, p, u, r, r_bank, start=False):
    e, v = K.nc.tensor, (u + d) % 3
    if not start:
        e.wait_ge(K.A["taken"], r - 2)
    if what == "max":
        if n == 0:
            e.wait_ge(K.ld_k[v], 80 * loads(p, u, d))
        ins = m_unit_pe(K, n, r_bank, v)
    elif what == "mrow":
        e.wait_ge(K.A["mm"], count(p, u, 1, d + 2))
        ins = e.transpose(bank(K, r_bank)[0:32, 0:P],
                          K.mm_hl[:, 2 * n:2 * n + 2, :, :].bitcast(F32).rearrange("p j a i -> p (j a i)"), K.ident[:, :])
    else:
        e.wait_ge(K.A["oev"], count(p, u, 2, 2 * d + n + 2))
        for t in range(4):
            ins = e.transpose(bank(K, r_bank)[:, t * P:(t + 1) * P], K.ot[:, n, t * P:(t + 1) * P], K.ident[:, :])
    ins.then_inc(K.A["ring"], 1)


def unit_pe(K, p, u, d, n, start=False):
    e = K.nc.tensor
    kt, half, heads = UNITS[n]
    v = (u + d) % 3
    if not start:
        e.wait_ge(K.A["ex"], count(p, u, NU, d * NU + n - 2))
    if n == 0:
        e.wait_ge(K.ld_r[v], 64 * loads(p, u, d))
    q0, q1 = max(kt * P, half * CHUNK), (half + 1) * CHUNK
    for m, j in enumerate(heads):
        ins = e.matmul(slot(K, u, d, n)[:, m * (q1 - q0):(m + 1) * (q1 - q0)],
                       K.keys[v][:, j, kt * P:(kt + 1) * P], K.queries[v][:, q0:q1], start=True, stop=True)
    ins.then_inc(K.A["sp"], 1)


def slot(K, u, d, n):
    return bank(K, SLOTS[((u + d) * NU + n) % 3])


def pv_pe(K, p, u, kt, half):
    e = K.nc.tensor
    if half == kt // 4:
        e.wait_ge(K.A["mk"], count(p, u, KT, kt + 1))
    else:
        e.wait_ge(K.A["ex"], count(p, u, NU, FIRST_UNIT[kt + 1]))
    if kt == 0:
        e.wait_ge(K.A["vg"], count(p, u, 1, 1))
        e.wait_ge(K.A["oev"], count(p, u, 2, 1))
    q0, q1 = max(kt * P, half * CHUNK), (half + 1) * CHUNK
    for j in range(4):
        ins = e.matmul(bank(K, O_BANK[half])[32 * j:32 * j + 32, q0 - half * CHUNK:CHUNK],
                       K.vg[:, kt, j, :], K.probs[:, kt % 2, j, q0:q1],
                       start=(kt == 0), stop=(kt == 4 * half + 3), skip_group_check=True)
    if half == 1:
        ins.then_inc(K.A["pv"], 1)


def pe_body(K, p, u, kind):
    ring, took = RINGS[kind], 0
    for step, order in enumerate(ORDERS[kind]):
        if kind == LAST and step == KT - 1:
            proj_tr_pe(K, 0)
        d, kt = (0, step + 1) if step + 1 < KT else (1, 0)
        units = list(range(FIRST_UNIT[kt], FIRST_UNIT[kt + 1])) if d == 0 or kind != LAST else []
        for what in order:
            if what == "U":
                unit_pe(K, p, u, d, units.pop(0))
            elif what == "R":
                kind_of, dd, n = ring[took]
                number = count(p, u, RINGN, RING0[kind] + took)
                ring_pe(K, kind_of, dd, n, p, u, number, RING[(u * RINGN + RING0[kind] + took) % 3])
                took += 1
            else:
                pv_pe(K, p, u, step, 1 if what == "a" else 0)
        assert not units
    assert took == len(ring)


def attn_pe(K):
    e = K.nc.tensor
    e.wait_ge(K.A["qf"], NCH)
    for r, (what, d, n) in enumerate(RING_PROLOGUE):
        ring_pe(K, what, d, n, 0, 0, r, RING[r % 3], start=r < 3)
    e.sem_inc(K.A["pv"], 1)
    for n in range(FIRST_UNIT[1]):
        unit_pe(K, 0, 0, 0, n, start=n < 3)
    with e.Fori(0, LOOP3) as p:
        for u in range(3):
            pe_body(K, p, u, LOOP)
    pe_body(K, LOOP3, 0, LAST_BUT_ONE)
    pe_body(K, LOOP3, 1, LAST)
    ring_pe(K, "out", -1, 1, GROUPS // 3, GROUPS % 3, RING_END, RING[RING_END % 3])


def ring_dve(K, what, d, n, p, u, r, r_bank, start=False):
    e = K.nc.vector
    e.wait_ge(K.A["ring"], r + 1)
    if what == "max":
        if n == 0:
            e.wait_ge(K.A["nm"], count(p, u, KT + 1, (KT + 1) * d))
        b, j = n // 4, n % 4
        e.tensor_reduce(K.mxp[:, j, 4 * b:4 * b + 4], bank(K, r_bank).rearrange("p (m k) -> p m k", k=P),
                        AX.X, ALU.max).then_inc(K.A["taken"], 1)
        if n == NMAX - 1:
            e.wait_ge(K.A["taken"], r + 1)
            e.wait_ge(K.A["mm"], count(p, u, 1, d + 1))
            for i, (lo, hi) in sorted(max_slots().items()):
                e.tensor_reduce(K.nmax[:, :, i:i + 1], K.mxp[:, :, lo:hi], AX.X, ALU.max, negate=True)\
                 .then_inc(K.A["nm"], 1)
            e.wait_ge(K.A["nm"], count(p, u, KT + 1, (KT + 1) * d + KT))
            e.tensor_copy(K.mm_hl[:, 0:4, 0, :], K.nmax[:, :, :]).then_inc(K.A["nm"], 1)
            e.wait_ge(K.A["nm"], count(p, u, KT + 1, (KT + 1) * (d + 1)))
            e.tensor_tensor(K.mm_hl[:, 0:4, 1, :], K.nmax[:, :, :], K.mm_hl[:, 0:4, 0, :].bitcast(F32),
                            ALU.subtract).then_inc(K.A["mm"], 1)
    elif what == "mrow":
        if not start:
            e.wait_ge(K.ld_r[(u + d - 1) % 3], 64 * loads(p, u, d - 1))
        e.tensor_copy(K.m_rows[32 * n:32 * n + 32, :], bank(K, r_bank)[0:32, 0:P]).then_inc(K.A["taken"], 1)
    else:
        b = bank(K, r_bank).rearrange("p (m c) -> p m c", c=32)
        e.wait_ge(K.A["taken"], r)
        e.reciprocal(K.rsum[:, :, :], b[:, :, HDIM:HDIM + 1]).then_inc(K.A["rs"], 1)
        e.wait_ge(K.A["rs"], count(p, u, 2, 2 * d + n + 2))
        dst = K.o_all[:, at(count(p, u, 1, d + 1), 1), 4 * n:4 * n + 4, :].rearrange("p g t (j c) -> p (g t j) c", c=HDIM)
        e.tensor_tensor(dst, b[:, :, 0:HDIM], K.rsum[:, :, :].to_broadcast([P, 16, HDIM]), ALU.mult)\
         .then_inc(K.A["taken"], 1)


def dve_body(K, p, u, kind):
    for k, (what, d, n) in enumerate(RINGS[kind]):
        number = count(p, u, RINGN, RING0[kind] + k)
        ring_dve(K, what, d, n, p, u, number, RING[(u * RINGN + RING0[kind] + k) % 3])


def attn_dve(K):
    e = K.nc.vector
    e.memset(K.mm_hl[:, :, :, :].bitcast(F32), 0.0).then_inc(K.A["mm"], 1)
    for r, (what, d, n) in enumerate(RING_PROLOGUE):
        ring_dve(K, what, d, n, 0, 0, r, RING[r % 3], start=True)
    with e.Fori(0, LOOP3) as p:
        for u in range(3):
            dve_body(K, p, u, LOOP)
    dve_body(K, LOOP3, 0, LAST_BUT_ONE)
    dve_body(K, LOOP3, 1, LAST)
    proj_lo_dve(K, 0)
    ring_dve(K, "out", -1, 1, GROUPS // 3, GROUPS % 3, RING_END, RING[RING_END % 3])


def unit_act(K, p, u, d, n, start=False):
    e = K.nc.scalar
    kt, half, heads = UNITS[n]
    e.wait_ge(K.A["sp"], count(p, u, NU, d * NU + n + 1))
    if n == FIRST_UNIT[kt] and not start:
        e.wait_ge(K.A["pv"], count(p, u, KT, d * KT + kt))
    q0, q1 = max(kt * P, half * CHUNK), (half + 1) * CHUNK
    src = slot(K, u, d, n)[:, 0:len(heads) * (q1 - q0)].rearrange("p (m q) -> p m q", q=q1 - q0)
    e.activation(K.probs[:, kt % 2, heads[0]:heads[-1] + 1, q0:q1], src, ACT.Exp, scale=SCALE).then_inc(K.A["ex"], 1)


def oev_act(K, p, u, kind, half):
    e = K.nc.scalar
    e.wait_ge(K.A["pv"], count(p, u, KT, 4 * half + 5))
    if half == 0:
        at0 = RINGS[LAST_BUT_ONE if kind == LAST else LOOP].index(("out", 0, 0)) + RING0[LOOP] - RINGN
    else:
        at0 = RINGS[kind].index(("out", -1, 1)) + RING0[kind]
    e.wait_ge(K.A["ring"], count(p, u, RINGN, at0 + 1))
    e.copy(K.ot[:, half, :], bank(K, O_BANK[half])).then_inc(K.A["oev"], 1)


def act_body(K, p, u, kind):
    for step in range(KT):
        d, kt = (0, step + 1) if step + 1 < KT else (1, 0)
        if d == 0 or kind != LAST:
            for n in range(FIRST_UNIT[kt], FIRST_UNIT[kt + 1]):
                unit_act(K, p, u, d, n)
        if step == 4:
            oev_act(K, p, u, kind, 0)
        if kind == LAST and step in (5, 6):
            gather_act(K, step - 5)
    if kind == LAST:
        proj_act(K, 0)
    oev_act(K, p, u, kind, 1)


def attn_act(K):
    e = K.nc.scalar
    e.wait_ge(K.A["ready"], 1)
    e.sem_inc(K.A["oev"], 1)
    for n in range(FIRST_UNIT[1]):
        unit_act(K, 0, 0, 0, n, start=True)
    with e.Fori(0, LOOP3) as p:
        for u in range(3):
            act_body(K, p, u, LOOP)
    act_body(K, LOOP3, 0, LAST_BUT_ONE)
    act_body(K, LOOP3, 1, LAST)


def mask_pool(K, p, u, kt):
    e = K.nc.gpsimd
    e.wait_ge(K.A["ex"], count(p, u, NU, FIRST_UNIT[kt] + DIAGONAL_UNITS[kt]))
    alone(K, e)
    blk = K.probs[:, kt % 2, :, kt * P:(kt + 1) * P]
    e.affine_select(out=blk, in_=blk, compare_op=ALU.is_ge, fill=0.0, base=0,
                    pattern=[[0, 4], [1, P]], channel_multiplier=-1).then_inc(K.A["mk"], 1)


def vg_pool(K, p, u, start=False):
    e = K.nc.gpsimd
    if not start:
        e.wait_ge(K.A["pv"], count(p, u, KT, 1))
    src = K.v_all[:, at(count(p, u, 1, 0), 1), :, :].rearrange("p g t (j c) -> p (g t j) c", c=HDIM)
    dst = K.vg[:, :, :, :].rearrange("p t j c -> p (t j) c")[:, :, 0:HDIM]
    e.tensor_copy(dst, src).then_inc(K.A["vg"], 1)


def pool_body(K, p, u):
    vg_pool(K, p, u)
    for kt in range(KT):
        mask_pool(K, p, u, kt)


def attn_pool(K):
    e = K.nc.gpsimd
    for c in range(NCH):
        e.wait_ge(K.q_st[c], 16 * 3)
    e.memset(K.vg[:, :, :, :], 0.0).then_inc(K.A["vi"], 1)
    e.memset(K.ot[:, :, :], 1.0).then_inc(K.A["ready"], 1)
    e.wait_ge(K.A["vi"], 1)
    e.memset(K.vg[:, :, :, HDIM:HDIM + 1], 1.0).then_inc(K.A["vi"], 1)
    e.wait_ge(K.A["vi"], 2)
    e.wait_ge(K.A["vev"], NCH)
    with e.Fori(0, LOOP3) as p:
        for u in range(3):
            pool_body(K, p, u)
    pool_body(K, LOOP3, 0)
    pool_body(K, LOOP3, 1)


def stack_load(K, p, u, d):
    queries_load(K, p, u, d)
    keys_load(K, p, u, d)


def queries_load(K, p, u, d):
    v, row = (u + d) % 3, count(p, u, 4, 4 * d)
    K.nc.sync.dma_start(K.queries[v][:, :].bitcast(F32), K.q_dram[at(row, 4)].rearrange("g r t -> (g r) t"))\
     .then_inc(K.ld_k[v], 16)


def keys_load(K, p, u, d):
    v, row = (u + d) % 3, count(p, u, 4, 4 * d)
    for j in range(4):
        K.nc.sync.dma_start(K.keys[v][32 * j:32 * j + 32, j, :].bitcast(F32),
                            K.k_dram[at(row + j, 1)].rearrange("g r t -> (g r) t")).then_inc(K.ld_k[v], 16)


def rows_load(K, p, u, d, r):
    e, v = K.nc.sync, (u + d) % 3
    e.wait_ge(K.ld_k[v], 80 * loads(p, u, d))
    alone(K, e)
    for j in range(4):
        if j % 2 == 0:
            e.wait_ge(K.A["taken"], r + (j // 2 + 1))
        dst = K.queries[v][32 * j:32 * j + 2, :].bitcast(F32).rearrange("p (i q) -> p i q", q=P)
        e.dma_start(dst, K.m_rows[2 * KT * j:2 * KT * (j + 1), :].bitcast(F32)).then_inc(K.ld_r[v], 16)


def sp_body(K, p, u, kind):
    if kind == LOOP:
        K.nc.sync.wait_ge(K.A["sp"], count(p, u, NU, 1))
        stack_load(K, p, u, 2)
    rows_load(K, p, u, 1, count(p, u, RINGN, RING0[kind] + RINGS[kind].index(("mrow", 1, 0))))


def attn_sp(K):
    e = K.nc.sync
    for c in range(NCH - 1):
        keys_sp(K, c)
    queries_sp(K, 0)
    for c in range(NCH // 2):
        e.wait_ge(K.k_st[c], 16 * 3)
    e.wait_ge(K.ld["const"], 16 * N_CONST_DMA)
    e.wait_ge(K.cleared, 3)
    keys_load(K, 0, 0, 0)
    queries_sp(K, 1)
    keys_load(K, 0, 0, 1)
    for c in range(NCH // 2):
        e.wait_ge(K.q_st[c], 16 * 3)
    queries_load(K, 0, 0, 0)
    queries_load(K, 0, 0, 1)
    keys_sp(K, NCH - 1)
    for c in range(NCH // 2, NCH):
        queries_sp(K, c)
    for c in range(NCH // 2, NCH):
        e.wait_ge(K.k_st[c], 16 * 3)
        e.wait_ge(K.q_st[c], 16 * 3)
    rows_load(K, 0, 0, 0, RING_PROLOGUE.index(("mrow", 0, 0)))
    with e.Fori(0, LOOP3) as p:
        for u in range(3):
            sp_body(K, p, u, LOOP)
    sp_body(K, LOOP3, 0, LAST_BUT_ONE)


def proj_tr_pe(K, c):
    e, u = K.nc.tensor, c % 2
    if c >= 2:
        e.wait_ge(K.A["ol"], c - 1)
    e.wait_ge(K.A["og"], c + 1)
    for t in range(TPC):
        ins = e.transpose(bank(K, O_BANK[u])[:, t * P:(t + 1) * P], K.ao_f[:, u, t * P:(t + 1) * P], K.ident[:, :])
    ins.then_inc(K.A["otr"], 1)


def proj_mm(K, c):
    e, u = K.nc.tensor, c % 2
    e.wait_ge(K.A["ol"], c + 1)
    if c >= 2:
        e.wait_ge(K.A["xup"], c - 1)
    for t in range(TPC):
        tc = slice(t * P, (t + 1) * P)
        ins = three(K, e, bank(K, 3 - u)[:, tc], (K.ao_h[:, u, tc], K.ao_l[:, u, tc]), (K.small["ph"][:, :], K.small["pl"][:, :]))
    ins.then_inc(K.A["op"], 1)


def gather_act(K, c):
    e, b, u = K.nc.scalar, c // 2, c % 2
    if c == 0:
        e.wait_ge(K.A["taken"], RING0[LAST] + RINGN * (GROUPS - 1))
    if c == 2:
        e.wait_ge(K.A["taken"], RING_END + 1)
    if c >= 2:
        e.wait_ge(K.A["otr"], c - 1)
    src = K.o_all[:, 1 + b * GPB:1 + (b + 1) * GPB, TPC * (c % 2):TPC * (c % 2) + TPC, :]
    e.copy(K.ao_f[:, u, :].rearrange("p (t g m) -> p g t m", g=GPB, m=32), src).then_inc(K.A["og"], 1)


def proj_act(K, c):
    e, u = K.nc.scalar, c % 2
    e.wait_ge(K.A["otr"], c + 1)
    if c >= 2:
        e.wait_ge(K.A["op"], c - 1)
    e.copy(K.ao_h[:, u, :], bank(K, O_BANK[u])).then_inc(K.A["oh"], 1)


def proj_lo_dve(K, c):
    e, u = K.nc.vector, c % 2
    e.wait_ge(K.A["oh"], c + 1)
    e.tensor_tensor(K.ao_l[:, u, :], bank(K, O_BANK[u]), K.ao_h[:, u, :].bitcast(F32), ALU.subtract).then_inc(K.A["ol"], 1)


def proj_x_dve(K, c):
    e, u = K.nc.vector, c % 2
    e.wait_ge(K.A["op"], c + 1)
    xc = K.x[:, c * TPC:(c + 1) * TPC, :]
    e.tensor_tensor(xc, xc, bank(K, 3 - u).rearrange("p (t e) -> p t e", e=EMB), ALU.add).then_inc(K.A["xup"], 1)


def proj_bias_pool(K):
    e = K.nc.gpsimd
    e.wait_ge(K.NS[1]["z"], NCH)
    for c in range(NCH):
        xc = K.x[:, c * TPC:(c + 1) * TPC, :]
        e.tensor_tensor(xc, xc, K.b_p[:, :].unsqueeze(1).to_broadcast([P, TPC, EMB]), ALU.add).then_inc(K.A["bp"], 1)


TAIL_PE = (("proj", 0), ("proj_tr", 1), ("proj_tr", 2), ("proj", 1), ("proj_tr", 3), ("proj", 2),
           ("norm_tr", 0), ("proj", 3), ("norm_tr", 1), ("logits", 0), ("norm_tr", 2), ("logits", 1),
           ("norm_tr", 3), ("logits", 2), ("logits", 3))
TAIL_DVE = (("proj_lo", 1), ("x", 0), ("stats", 0), ("proj_lo", 2), ("x", 1), ("z", 0), ("stats", 1),
            ("proj_lo", 3), ("x", 2), ("stats", 2), ("z", 1), ("norm_lo", 0), ("x", 3), ("stats", 3), ("z", 2),
            ("norm_lo", 1), ("z", 3), ("norm_lo", 2), ("norm_lo", 3))


def build(nc, tokens, attn_w, attn_b, proj_w, proj_b, gate_s, up_s, down_s, gate_r, up_r, down_r,
          route_w, route_b, result):
    K = Chip()
    K.nc, K.tokens, K.result = nc, tokens, result
    K.attn_w, K.attn_b, K.proj_w, K.proj_b = attn_w, attn_b, proj_w, proj_b
    K.gate_s, K.up_s, K.down_s = gate_s, up_s, down_s
    K.gate_r, K.up_r, K.down_r = gate_r, up_r, down_r
    K.route_w, K.route_b = route_w, route_b
    with ExitStack() as ctx:
        place_memory(K, ctx)

        block = ctx.enter_context(K.nc.Block())

        @block.sync
        def _(e):
            start_sp(K)
            router_sp(K, 0)
            ffn_sp(K, 0)
            attn_sp(K)
            router_sp(K, 1)
            ffn_sp(K, 1)

        @block.tensor
        def _(e):
            weights_small_pe(K)
            for c in range(NCH + 1):
                if c < NCH:
                    norm_tr_pe(K, 0, c)
                if c == NCH:
                    for m in range(len(TP_BANKS)):
                        weights_pe(K, m)
                if c:
                    logits_pe(K, 0, 0, c - 1)
            for m in range(len(TP_BANKS), 2 * len(TP_BANKS)):
                weights_pe(K, m)
            route_tr_pe(K, 0)
            for m in range(2 * len(TP_BANKS), len(TP_GROUPS)):
                weights_pe(K, m)
            e.wait_ge(K.tp_lo, len(TP_GROUPS))
            ffn_pe(K, 0)
            ytr_pe(K, 0, NCH - 1)
            qv_pe(K, 0)
            q_pe(K, 0)
            qv_pe(K, 1)
            q_pe(K, 1)
            norm_tr_pe(K, 1, NCH - 1)
            qv_pe(K, 2)
            qv_pe(K, 3)
            q_pe(K, 2)
            q_pe(K, 3)
            attn_pe(K)
            for step, c in TAIL_PE:
                if step == "proj_tr":
                    proj_tr_pe(K, c)
                elif step == "proj":
                    proj_mm(K, c)
                elif step == "norm_tr":
                    norm_tr_pe(K, 2, c)
                else:
                    logits_pe(K, 1, 2, c)
            ffn_pe(K, 1)

        @block.scalar
        def _(e):
            start_act(K)
            weights_act(K)
            for c in range(NCH):
                norm_hi_act(K, 0, c)
            for m in range(len(TP_BANKS)):
                weights_hi_act(K, m)
            router_act(K, 0)
            for m in range(len(TP_BANKS), len(TP_GROUPS)):
                weights_hi_act(K, m)
            ffn_act(K, 0)
            qv_act(K, 0)
            q_act(K, 0)
            qv_act(K, 1)
            q_act(K, 1)
            norm_hi_act(K, 1, NCH - 1)
            qv_act(K, 2)
            qv_act(K, 3)
            q_act(K, 2)
            q_act(K, 3)
            attn_act(K)
            for c in range(NCH + 3):
                if c < 2:
                    gather_act(K, c + 2)
                if 0 < c < NCH:
                    proj_act(K, c)
                if c >= 3:
                    norm_hi_act(K, 2, c - 3)
            router_act(K, 1)
            ffn_act(K, 1)

        @block.gpsimd
        def _(e):
            start_pool(K)
            for c in range(NCH):
                norm_rstd_pool(K, 0, c)
            clear_pool(K)
            ffn_pool(K, 0)
            proj_bias_pool(K)
            attn_pool(K)
            for c in range(NCH):
                norm_rstd_pool(K, 2, c)
            e.wait_ge(K.NS[2]["lo"], 1)
            e.memset(K.shared_rows, 1.0).then_inc(K.ones, 1)
            e.wait_ge(K.ones, 1)
            ffn_pool(K, 1)

        @block.vector
        def _(e):
            for c in range(NCH + 2):
                if c == 2:
                    weights_small_dve(K)
                if c < NCH:
                    e.wait_ge(K.ld_x[c // 2], 16)
                    norm_stats_dve(K, 0, c)
                if 0 <= c - 1 < NCH:
                    norm_z_dve(K, 0, c - 1)
                if c >= 2:
                    norm_lo_dve(K, 0, c - 2)
            for m in range(len(TP_BANKS)):
                weights_lo_dve(K, m)
            router_dve(K, 0)
            for m in range(len(TP_BANKS), len(TP_GROUPS)):
                weights_lo_dve(K, m)
            ffn_dve(K, 0)
            yev_dve(K, 0, NCH - 1)
            qv_dve(K, 0)
            xup_dve(K, 0, NCH - 1)
            e.wait_ge(K.FF[0]["out"], NCH)
            norm_stats_dve(K, 1, NCH - 1)
            q_dve(K, 0)
            qv_dve(K, 1)
            norm_z_dve(K, 1, NCH - 1)
            q_dve(K, 1)
            norm_lo_dve(K, 1, NCH - 1)
            qv_dve(K, 2)
            qv_dve(K, 3)
            q_dve(K, 2)
            q_dve(K, 3)
            attn_dve(K)
            e.wait_ge(K.A["bp"], NCH)
            for step, c in TAIL_DVE:
                if step == "proj_lo":
                    proj_lo_dve(K, c)
                elif step == "x":
                    proj_x_dve(K, c)
                elif step == "stats":
                    e.wait_ge(K.A["xup"], c + 1)
                    norm_stats_dve(K, 2, c)
                elif step == "z":
                    norm_z_dve(K, 2, c)
                else:
                    norm_lo_dve(K, 2, c)
            router_dve(K, 1)
            ffn_dve(K, 1)


_INS = ["attn_hidden_states", "attn_c_attn_w", "attn_c_attn_b", "attn_c_proj_w", "attn_c_proj_b",
        "ffn_sg", "ffn_su", "ffn_sd", "ffn_rg", "ffn_ru", "ffn_rd", "ffn_wr", "ffn_rb"]


def kernel(**inputs):
    import concourse.bacc as bacc
    from concourse.bass_utils import run_bass_kernel_spmd

    nc = bacc.Bacc("TRN2", target_bir_lowering=False, num_devices=1)
    arrays, args = {}, []
    for name in _INS:
        a = np.ascontiguousarray(inputs["L0_" + name])
        arrays["in_" + name] = a
        args.append(nc.dram_tensor("in_" + name, a.shape, mybir.dt.from_np(a.dtype), kind="ExternalInput").ap())
    out = nc.dram_tensor("out", (BATCH, SEQ, EMB), F32, kind="ExternalOutput").ap()
    build(nc, *args, out)
    r = run_bass_kernel_spmd(nc, [arrays], core_ids=[0])
    return r.results[0]["out"]
```
